# Optimizing a Trainium2 kernel written in Bass

```python
import numpy as np
import jax
import jax.numpy as jnp

def _softmax(x, axis=-1):
    return jax.nn.softmax(x, axis=axis)

def _gelu(x):
    return jax.nn.gelu(x, approximate=True)

def _silu(x):
    return jax.nn.silu(x)

def _sigmoid(x):
    return jax.nn.sigmoid(x)

def _layernorm(x, axis=-1, eps=1e-05):
    m = jnp.mean(x, axis=axis, keepdims=True)
    v = jnp.var(x, axis=axis, keepdims=True)
    return (x - m) / jnp.sqrt(v + eps)

def _scatter_add(tgt, idx, src, axis=0):
    return tgt.at[idx].add(src)

def _segment_sum(src, seg, n):
    return jax.ops.segment_sum(src, seg, n)
kernel_name = 'mk_metaformer_d2_conv_nchw128_r2_895375'

def setup_inputs(seed: int=0):
    np.random.seed(seed)
    _w = jnp.asarray

    def _rec_inputs():
        import jax
        import jax.numpy as jnp
        _gk = jax.random.key(seed)
        x = -8.268e-05 + 0.9999 * jax.random.normal(jax.random.fold_in(_gk, 1), (8, 64, 112, 112), jnp.float32)
        return x
    x = _rec_inputs()

    def _L0_conv_setup():
        import jax, jax.numpy as jnp
        import numpy as np
        WIN = 7
        BN_EPS = 1e-05

        def _conv1x1(t, w):
            return jnp.einsum('bchw,oc->bohw', t, w)
        key = jax.random.key(seed)
        ks = jax.random.split(key, 9)
        B, C, H, W = (8, 64, 112, 112)
        mid = C // 2
        x = jax.random.normal(ks[0], (B, C, H, W), jnp.float32)
        s = 1.0 / np.sqrt(C)
        wq = jax.random.normal(ks[1], (mid, C), jnp.float32) * s
        wk = jax.random.normal(ks[2], (mid, C), jnp.float32) * s
        wv = jax.random.normal(ks[3], (mid, C), jnp.float32) * s
        wo = jax.random.normal(ks[4], (C, mid), jnp.float32) * (1.0 / np.sqrt(mid))
        bn_gamma = jax.random.uniform(ks[5], (C,), jnp.float32, 0.5, 1.5)
        bn_beta = jax.random.normal(ks[6], (C,), jnp.float32) * 0.1
        bn_mean = jax.random.normal(ks[7], (C,), jnp.float32) * 0.1
        bn_var = jax.random.uniform(ks[8], (C,), jnp.float32, 0.5, 1.5)
        return dict(x=x, wq=wq, wk=wk, wv=wv, wo=wo, bn_gamma=bn_gamma, bn_beta=bn_beta, bn_mean=bn_mean, bn_var=bn_var)
    _L0_conv_all = _L0_conv_setup()
    _L0_conv_in = {k: v for k, v in _L0_conv_all.items() if k in ('wq', 'wk', 'wv', 'wo', 'bn_gamma', 'bn_beta', 'bn_mean', 'bn_var')}
    del _L0_conv_all

    def _L0_ffn_setup():
        import jax, jax.numpy as jnp
        import numpy as np
        B, N, D, C, E, K = (8, 4096, 64, 64, 8, 2)
        key = jax.random.key(seed)
        k0, k1, k2 = jax.random.split(key, 3)
        x = jax.random.normal(k0, (B, N, D), dtype=jnp.float32)
        router_w = jax.random.normal(k1, (D, E), dtype=jnp.float32) * 0.05
        router_b = jnp.zeros((E,), dtype=jnp.float32)
        expert_w = jax.random.normal(k2, (E, D, C), dtype=jnp.float32) * (1.0 / np.sqrt(D))
        expert_b = jnp.zeros((E, C), dtype=jnp.float32)
        return {'x': x, 'router_w': router_w, 'router_b': router_b, 'expert_w': expert_w, 'expert_b': expert_b}
    _L0_ffn_all = _L0_ffn_setup()
    _L0_ffn_in = {k: v for k, v in _L0_ffn_all.items() if k in ('router_w', 'router_b', 'expert_w', 'expert_b')}
    del _L0_ffn_all

    def _L1_conv_setup():
        import jax, jax.numpy as jnp
        import numpy as np
        WS = 8
        D_MODEL = 64
        EXPAND = 2
        D_INNER = EXPAND * D_MODEL
        D_STATE = 16
        D_CONV = 4
        DT_RANK = (D_MODEL + 15) // 16
        B, H, W = (2, 128, 128)

        def _silu(x):
            return x * jax.nn.sigmoid(x)

        def _selective_scan(u, dt, A, Bm, Cm, Dp):

            def step(h, inp):
                dt_t, B_t, C_t, u_t = inp
                dA = jnp.exp(dt_t[:, :, None] * A)
                dBu = (dt_t * u_t)[:, :, None] * B_t[:, None, :]
                h = dA * h + dBu
                y = jnp.einsum('bdn,bn->bd', h, C_t)
                return (h, y)
            h0 = jnp.zeros((u.shape[0], A.shape[0], A.shape[1]), u.dtype)
            xs = (dt.transpose(1, 0, 2), Bm.transpose(1, 0, 2), Cm.transpose(1, 0, 2), u.transpose(1, 0, 2))
            _, ys = jax.lax.scan(step, h0, xs)
            return ys.transpose(1, 0, 2) + u * Dp

        def _mamba(xw, W_in, conv_w, conv_b, W_xproj, W_dt, b_dt, A_log, Dp, W_out):
            b = xw.shape[0]
            seq = xw.reshape(b, D_MODEL, WS * WS).transpose(0, 2, 1)
            xz = seq @ W_in
            x, z = jnp.split(xz, 2, axis=-1)
            xc = x.transpose(0, 2, 1)
            xc = jax.lax.conv_general_dilated(xc, conv_w[:, None, :], window_strides=(1,), padding=[(D_CONV - 1, 0)], feature_group_count=D_INNER, dimension_numbers=('NCH', 'OIH', 'NCH'))
            x = _silu((xc + conv_b[:, None]).transpose(0, 2, 1))
            xp = x @ W_xproj
            dt, Bm, Cm = jnp.split(xp, [DT_RANK, DT_RANK + D_STATE], axis=-1)
            dt = jax.nn.softplus(dt @ W_dt + b_dt)
            A = -jnp.exp(A_log)
            y = _selective_scan(x, dt, A, Bm, Cm, Dp)
            y = y * _silu(z)
            out = y @ W_out
            return out.transpose(0, 2, 1).reshape(b, D_MODEL, WS, WS)
        key = jax.random.key(seed)
        ks = jax.random.split(key, 12)
        s = 0.02
        inp = {'x': jax.random.normal(ks[0], (B, D_MODEL, H, W), jnp.float32), 'pos': jnp.zeros((1, D_MODEL, WS, WS), jnp.float32), 'W_in': s * jax.random.normal(ks[1], (D_MODEL, 2 * D_INNER), jnp.float32), 'conv_w': s * jax.random.normal(ks[2], (D_INNER, D_CONV), jnp.float32), 'conv_b': jnp.zeros((D_INNER,), jnp.float32), 'W_xproj': s * jax.random.normal(ks[3], (D_INNER, DT_RANK + 2 * D_STATE), jnp.float32), 'W_dt': s * jax.random.normal(ks[4], (DT_RANK, D_INNER), jnp.float32), 'b_dt': jnp.full((D_INNER,), -4.6, jnp.float32), 'A_log': jnp.log(jnp.broadcast_to(jnp.arange(1, D_STATE + 1, dtype=jnp.float32), (D_INNER, D_STATE))), 'Dp': jnp.ones((D_INNER,), jnp.float32), 'W_out': s * jax.random.normal(ks[5], (D_INNER, D_MODEL), jnp.float32)}
        return inp
    _L1_conv_all = _L1_conv_setup()
    _L1_conv_in = {k: v for k, v in _L1_conv_all.items() if k in ('pos', 'W_in', 'conv_w', 'conv_b', 'W_xproj', 'W_dt', 'b_dt', 'A_log', 'Dp', 'W_out')}
    del _L1_conv_all

    def _L1_ffn_setup():
        import jax, jax.numpy as jnp
        import numpy as np
        B, S, D, E, H, O, K = (256, 1024, 64, 32, 256, 64, 8)
        key = jax.random.key(seed)
        k0, k1, k2, k3 = jax.random.split(key, 4)
        x = jax.random.normal(k0, (B, S, D), dtype=jnp.float32)
        gate_w = jax.random.normal(k1, (E, D), dtype=jnp.float32) * (1.0 / np.sqrt(D))
        gate_b = jnp.zeros((E,), dtype=jnp.float32)
        weight1 = jax.random.uniform(k2, (E, D + 1, H), dtype=jnp.float32, minval=-1.0, maxval=1.0) * (1.0 / np.sqrt(D + 1))
        weight2 = jax.random.uniform(k3, (E, H + 1, O), dtype=jnp.float32, minval=-1.0, maxval=1.0) * (1.0 / np.sqrt(H + 1))
        return {'x': x, 'gate_w': gate_w, 'gate_b': gate_b, 'weight1': weight1, 'weight2': weight2}
    _L1_ffn_all = _L1_ffn_setup()
    _L1_ffn_in = {k: v for k, v in _L1_ffn_all.items() if k in ('gate_w', 'gate_b', 'weight1', 'weight2')}
    del _L1_ffn_all
    return {'x': x, 'L0_conv_wq': _L0_conv_in['wq'], 'L0_conv_wk': _L0_conv_in['wk'], 'L0_conv_wv': _L0_conv_in['wv'], 'L0_conv_wo': _L0_conv_in['wo'], 'L0_conv_bn_gamma': _L0_conv_in['bn_gamma'], 'L0_conv_bn_beta': _L0_conv_in['bn_beta'], 'L0_conv_bn_mean': _L0_conv_in['bn_mean'], 'L0_conv_bn_var': _L0_conv_in['bn_var'], 'L0_ffn_router_w': _L0_ffn_in['router_w'], 'L0_ffn_router_b': _L0_ffn_in['router_b'], 'L0_ffn_expert_w': _L0_ffn_in['expert_w'], 'L0_ffn_expert_b': _L0_ffn_in['expert_b'], 'L1_conv_pos': _L1_conv_in['pos'], 'L1_conv_W_in': _L1_conv_in['W_in'], 'L1_conv_conv_w': _L1_conv_in['conv_w'], 'L1_conv_conv_b': _L1_conv_in['conv_b'], 'L1_conv_W_xproj': _L1_conv_in['W_xproj'], 'L1_conv_W_dt': _L1_conv_in['W_dt'], 'L1_conv_b_dt': _L1_conv_in['b_dt'], 'L1_conv_A_log': _L1_conv_in['A_log'], 'L1_conv_Dp': _L1_conv_in['Dp'], 'L1_conv_W_out': _L1_conv_in['W_out'], 'L1_ffn_gate_w': _L1_ffn_in['gate_w'], 'L1_ffn_gate_b': _L1_ffn_in['gate_b'], 'L1_ffn_weight1': _L1_ffn_in['weight1'], 'L1_ffn_weight2': _L1_ffn_in['weight2']}

def reference(x, L0_conv_wq, L0_conv_wk, L0_conv_wv, L0_conv_wo, L0_conv_bn_gamma, L0_conv_bn_beta, L0_conv_bn_mean, L0_conv_bn_var, L0_ffn_router_w, L0_ffn_router_b, L0_ffn_expert_w, L0_ffn_expert_b, L1_conv_pos, L1_conv_W_in, L1_conv_conv_w, L1_conv_conv_b, L1_conv_W_xproj, L1_conv_W_dt, L1_conv_b_dt, L1_conv_A_log, L1_conv_Dp, L1_conv_W_out, L1_ffn_gate_w, L1_ffn_gate_b, L1_ffn_weight1, L1_ffn_weight2):
    import jax
    import jax.numpy as jnp

    def _L0_conv_ref(x, wq, wk, wv, wo, bn_gamma, bn_beta, bn_mean, bn_var):
        import jax, jax.numpy as jnp
        import numpy as np
        WIN = 7
        BN_EPS = 1e-05

        def _conv1x1(t, w):
            return jnp.einsum('bchw,oc->bohw', t, w)
        B, C, H, W = x.shape
        win = WIN
        ph = (win - H % win) % win
        pw = (win - W % win) % win
        xp = jnp.pad(x, ((0, 0), (0, 0), (0, ph), (0, pw))) if ph or pw else x
        Hp, Wp = (H + ph, W + pw)
        nH, nW = (Hp // win, Wp // win)
        Q = _conv1x1(xp, wq)
        K = _conv1x1(xp, wk)
        V = _conv1x1(xp, wv)
        mid = Q.shape[1]
        scale = mid ** (-0.5)

        def to_win(t):
            t = t.reshape(B, mid, nH, win, nW, win)
            return t.transpose(0, 2, 4, 3, 5, 1).reshape(B * nH * nW, win * win, mid)
        Qw, Kw, Vw = (to_win(Q), to_win(K), to_win(V))
        attn = jax.nn.softmax(jnp.einsum('nqc,nkc->nqk', Qw, Kw) * scale, axis=-1)
        ow = jnp.einsum('nqk,nkc->nqc', attn, Vw)
        ow = ow.reshape(B, nH, nW, win, win, mid).transpose(0, 5, 1, 3, 2, 4)
        ow = ow.reshape(B, mid, Hp, Wp)[:, :, :H, :W]
        y = _conv1x1(ow, wo)
        inv = bn_gamma / jnp.sqrt(bn_var + BN_EPS)
        return y * inv[None, :, None, None] + (bn_beta - bn_mean * inv)[None, :, None, None]

    def _L0_ffn_ref(x, router_w, router_b, expert_w, expert_b):
        import jax, jax.numpy as jnp
        import numpy as np
        B, N, D, C, E, K = (8, 4096, 64, 64, 8, 2)
        router_probs = jax.nn.softmax(x @ router_w + router_b, axis=-1)
        top_p, top_i = jax.lax.top_k(router_probs, K)
        top_p = top_p / jnp.sum(top_p, axis=-1, keepdims=True)
        expert_out = jnp.einsum('bnd,edc->bnec', x, expert_w) + expert_b
        gathered = jnp.take_along_axis(expert_out, top_i[..., None], axis=2)
        return jnp.einsum('bnk,bnkc->bnc', top_p, gathered)

    def _L1_conv_ref(x, pos, W_in, conv_w, conv_b, W_xproj, W_dt, b_dt, A_log, Dp, W_out):
        import jax, jax.numpy as jnp
        import numpy as np
        WS = 8
        D_MODEL = 64
        EXPAND = 2
        D_INNER = EXPAND * D_MODEL
        D_STATE = 16
        D_CONV = 4
        DT_RANK = (D_MODEL + 15) // 16
        B, H, W = (2, 128, 128)

        def _silu(x):
            return x * jax.nn.sigmoid(x)

        def _selective_scan(u, dt, A, Bm, Cm, Dp):

            def step(h, inp):
                dt_t, B_t, C_t, u_t = inp
                dA = jnp.exp(dt_t[:, :, None] * A)
                dBu = (dt_t * u_t)[:, :, None] * B_t[:, None, :]
                h = dA * h + dBu
                y = jnp.einsum('bdn,bn->bd', h, C_t)
                return (h, y)
            h0 = jnp.zeros((u.shape[0], A.shape[0], A.shape[1]), u.dtype)
            xs = (dt.transpose(1, 0, 2), Bm.transpose(1, 0, 2), Cm.transpose(1, 0, 2), u.transpose(1, 0, 2))
            _, ys = jax.lax.scan(step, h0, xs)
            return ys.transpose(1, 0, 2) + u * Dp

        def _mamba(xw, W_in, conv_w, conv_b, W_xproj, W_dt, b_dt, A_log, Dp, W_out):
            b = xw.shape[0]
            seq = xw.reshape(b, D_MODEL, WS * WS).transpose(0, 2, 1)
            xz = seq @ W_in
            x, z = jnp.split(xz, 2, axis=-1)
            xc = x.transpose(0, 2, 1)
            xc = jax.lax.conv_general_dilated(xc, conv_w[:, None, :], window_strides=(1,), padding=[(D_CONV - 1, 0)], feature_group_count=D_INNER, dimension_numbers=('NCH', 'OIH', 'NCH'))
            x = _silu((xc + conv_b[:, None]).transpose(0, 2, 1))
            xp = x @ W_xproj
            dt, Bm, Cm = jnp.split(xp, [DT_RANK, DT_RANK + D_STATE], axis=-1)
            dt = jax.nn.softplus(dt @ W_dt + b_dt)
            A = -jnp.exp(A_log)
            y = _selective_scan(x, dt, A, Bm, Cm, Dp)
            y = y * _silu(z)
            out = y @ W_out
            return out.transpose(0, 2, 1).reshape(b, D_MODEL, WS, WS)
        b, d, Hh, Ww = x.shape
        nh, nw = (Hh // WS, Ww // WS)
        xw = x.reshape(b, d, nh, WS, nw, WS).transpose(0, 2, 4, 1, 3, 5).reshape(b * nh * nw, d, WS, WS)
        xw = xw + pos
        yw = _mamba(xw, W_in, conv_w, conv_b, W_xproj, W_dt, b_dt, A_log, Dp, W_out)
        y = yw.reshape(b, nh, nw, d, WS, WS).transpose(0, 3, 1, 4, 2, 5).reshape(b, d, Hh, Ww)
        return y

    def _L1_ffn_ref(x, gate_w, gate_b, weight1, weight2):
        import jax, jax.numpy as jnp
        import numpy as np
        B, S, D, E, H, O, K = (256, 1024, 64, 32, 256, 64, 8)
        Bn, Sn, Dn = x.shape
        logits = jnp.einsum('bsd,ed->bse', x, gate_w) + gate_b
        probs = jax.nn.softmax(logits, axis=1)
        vals, idx = jax.lax.top_k(probs.transpose(0, 2, 1), K)
        topv = vals.transpose(0, 2, 1)
        topi = idx.transpose(0, 2, 1)
        flat_idx = topi.reshape(Bn, K * E)
        gathered = jnp.take_along_axis(x, flat_idx[:, :, None], axis=1)
        gathered = gathered.reshape(Bn, K, E, Dn)
        pooled = jnp.einsum('bked,bke->bed', gathered, topv)
        ones = jnp.ones((E, Bn, 1), dtype=x.dtype)
        h = jnp.concatenate([pooled.transpose(1, 0, 2), ones], axis=-1)
        h = jax.nn.gelu(jnp.einsum('ebd,edh->ebh', h, weight1), approximate=False)
        h = jnp.concatenate([h, ones], axis=-1)
        out = jnp.einsum('ebh,eho->ebo', h, weight2)
        out = out.transpose(1, 0, 2)
        weighted = jnp.einsum('beo,bke->bkeo', out, topv).reshape(Bn, K * E, O)
        outputs = jnp.zeros((Bn, Sn, O), dtype=x.dtype)
        outputs = outputs.at[jnp.arange(Bn)[:, None], flat_idx].add(weighted)
        return outputs

    def _gn(v, G=32, eps=1e-05):
        B_, C_, H_, W_ = v.shape
        g = v.reshape(B_, G, C_ // G, H_, W_)
        m = jnp.mean(g, axis=(2, 3, 4), keepdims=True)
        s = jnp.var(g, axis=(2, 3, 4), keepdims=True)
        return ((g - m) / jnp.sqrt(s + eps)).reshape(v.shape)

    def _ln_c(v, eps=1e-06):
        m = jnp.mean(v, axis=1, keepdims=True)
        s = jnp.var(v, axis=1, keepdims=True)
        return (v - m) / jnp.sqrt(s + eps)

    def _ln_t(v, eps=1e-05):
        m = jnp.mean(v, axis=-1, keepdims=True)
        s = jnp.var(v, axis=-1, keepdims=True)
        return (v - m) / jnp.sqrt(s + eps)

    def _to_tokens(v):
        B_, C_, H_, W_ = v.shape
        return v.reshape(B_, C_, H_ * W_).transpose(0, 2, 1)

    def _from_tokens(t, like):
        B_, C_, H_, W_ = like.shape
        return t.transpose(0, 2, 1).reshape(B_, C_, H_, W_)
    x = x + _L0_conv_ref(_ln_c(x), L0_conv_wq, L0_conv_wk, L0_conv_wv, L0_conv_wo, L0_conv_bn_gamma, L0_conv_bn_beta, L0_conv_bn_mean, L0_conv_bn_var)
    t = _to_tokens(x)
    t = t + _L0_ffn_ref(_ln_t(t), L0_ffn_router_w, L0_ffn_router_b, L0_ffn_expert_w, L0_ffn_expert_b)
    x = _from_tokens(t, x)
    x = x + _L1_conv_ref(_ln_c(x), L1_conv_pos, L1_conv_W_in, L1_conv_conv_w, L1_conv_conv_b, L1_conv_W_xproj, L1_conv_W_dt, L1_conv_b_dt, L1_conv_A_log, L1_conv_Dp, L1_conv_W_out)
    t = _to_tokens(x)
    t = t + _L1_ffn_ref(_ln_t(t), L1_ffn_gate_w, L1_ffn_gate_b, L1_ffn_weight1, L1_ffn_weight2)
    x = _from_tokens(t, x)
    return x

_drawn_inputs = setup_inputs


def setup_inputs(seed=0):
    import zlib

    import numpy as np

    out = dict(_drawn_inputs(seed))
    spreads = {'L0_ffn_router_b': (0.0, 0.1),
     'L0_ffn_expert_b': (0.0, 0.1),
     'L1_conv_pos': (0.0, 0.8),
     'L1_conv_conv_b': (0.0, 0.8),
     'L1_conv_b_dt': (-4.599999904632568, 0.6),
     'L1_conv_Dp': (1.0, 0.6),
     'L1_ffn_gate_b': (0.0, 0.8)}
    factors = {'L1_conv_W_in': 8.0,
     'L1_conv_conv_w': 8.0,
     'L1_conv_W_xproj': 8.0,
     'L1_conv_A_log': 8.0,
     'L1_conv_W_out': 8.0,
     'L1_ffn_gate_w': 8.0,
     'L1_ffn_weight1': 8.0,
     'L1_ffn_weight2': 8.0,
     'L1_conv_W_dt': 8.0}
    for name, (base, spread) in spreads.items():
        noise = np.random.default_rng([zlib.crc32(name.encode()), seed]).standard_normal(out[name].shape)
        drawn = base * np.exp(spread * noise) if base else spread * noise
        out[name] = jnp.asarray(drawn.astype(out[name].dtype))
    for name, factor in factors.items():
        out[name] = (out[name] * factor).astype(out[name].dtype)
    return out
```

```python
from contextlib import ExitStack

import concourse.bass as bass
from concourse import mybir

F32 = mybir.dt.float32
BF16 = mybir.dt.bfloat16
U32 = mybir.dt.uint32
ALU = mybir.AluOpType
ACT = mybir.ActivationFunctionType
AX = mybir.AxisListType

P = 128
C = 64
WIN = 7
WT = WIN * WIN
WP = 64
NE = 8
WS = 8
ST = WS * WS
CONV = 4
NS = 16
RK = 4
DI = 128
EC = 32
HID = 256
TOPK = 8
BANK = 512
SLOTS = 2
RESET = 1.0e15
BIG = 1.0e30
UNIT = 16
TILES = 2 * UNIT
RA = 4
RB = 2
RC = 8
SMALL = 21
TAKEN = -3.0e38


def banks(n):
    return [(a, min(a + BANK, n)) for a in range(0, n, BANK)]


def program(nc, x, wq, wk, wv, wo, gamma, beta, mean, var, router_w, router_b, expert_w, expert_b,
            pos, w_in, conv_w, conv_b, w_xproj, w_dt, b_dt, a_log, d_skip, w_out,
            gate_w, gate_b, weight1, weight2, out, x2, x3, logits, tokens):
    B, _, H, W = x.shape
    HW = H * W
    NP = B // 2
    TA = WIN * W
    NWA = W // WIN
    SA = H // WIN
    TB = WS * W
    NWB = W // WS
    SB = H // WS
    NCH = TB // P
    ROWS = WIN
    GB = NE * ROWS * 2

    def pairs(t):
        return t.rearrange("(k i) c h w -> k (i c) (h w)", i=2)

    x_v, out_v = pairs(x), pairs(out)

    with ExitStack() as top:
        def sbuf(name, shape, dt=F32, on=top):
            return on.enter_context(nc.sbuf_tensor(name, shape, dt))

        def psum(name, shape, dt=F32, on=top):
            return on.enter_context(nc.psum_tensor(name, shape, dt))

        phase_sems = []

        def new_sem(name, turn=0):
            handle = nc.alloc_semaphore(name=name)
            phase_sems.append(handle)
            if turn:
                nc.sync.sem_inc(handle, turn)
            return handle

        def end_phase():
            nc.clear_and_free_semaphores(phase_sems)
            phase_sems.clear()
            nc.all_engine_barrier()

        def new_sems(name, n=SLOTS, turn=0):
            return [new_sem(f"{name}{i}", turn) for i in range(n)]

        ident = sbuf("ident", [P, P])
        ident_bf = sbuf("ident_bf", [P, P], BF16)
        center = sbuf("center", [P, P])
        average = sbuf("average", [P, P])
        w_qk = sbuf("w_qk", [P, P])
        w_vo = sbuf("w_vo", [P, P])
        shift = sbuf("shift", [P, P])
        w_router = sbuf("w_router", [P, 2 * NE])
        b_router = sbuf("b_router", [P, NE])
        rank8 = sbuf("rank8", [P, NE])
        w_exp = sbuf("w_exp", [P, NE, P])
        b_exp = sbuf("b_exp", [48, P])
        b_exp3 = sbuf("b_exp3", [48, 3, P], BF16)
        pick = sbuf("pick", [48, NE, P], BF16)
        pos_t = sbuf("pos_t", [P, ST])
        w_z = sbuf("w_z", [P, 2, DI])
        w_conv = sbuf("w_conv", [P, 2, CONV, DI])
        conv_bias = sbuf("conv_bias", [P, 1])
        wx = sbuf("wx", [P, RK + 2 * NS])
        wx4 = sbuf("wx4", [RK, P])
        wdt = sbuf("wdt", [RK, DI])
        w_dt_full = sbuf("w_dt_full", [P, DI])
        dt_bias = sbuf("dt_bias", [P, 1])
        decay = sbuf("decay", [P, 4, 4])
        spread = sbuf("spread", [P, 4, P])
        w_bc = sbuf("w_bc", [P, 4, 2 * NS])
        rows_bc = sbuf("rows_bc", [P, 8, P], BF16)
        fold = sbuf("fold", [P, 32])
        skip = sbuf("skip", [P, P])
        skip_col = sbuf("skip_col", [P, 1])
        w_out_t = sbuf("w_out_t", [P, C])
        w_gate = sbuf("w_gate", [P, 2 * EC])
        b_gate = sbuf("b_gate", [2 * EC, 1])
        eps_bn = sbuf("eps_bn", [P, 1])
        eps_6 = sbuf("eps_6", [P, 1])
        one_col = sbuf("one_col", [P, 1])

        with ExitStack() as st:
            wq2 = sbuf("wq2", [C // 2, 2, C], on=st)
            wv2 = sbuf("wv2", [C // 2, 2, C], on=st)
            wk_t = sbuf("wk_t", [C // 2, C], on=st)
            wo_t = sbuf("wo_t", [C // 2, C], on=st)
            bn_row = sbuf("bn_row", [P, 4, C], on=st)
            inv_row = sbuf("inv_row", [P, C], on=st)
            tmp_row = sbuf("tmp_row", [P, C], on=st)
            rest = sbuf("rest", [48, P], on=st)
            rest2 = sbuf("rest2", [48, P], on=st)
            fold4 = sbuf("fold4", [P, 4, 32], on=st)
            w_in_t = sbuf("w_in_t", [P, 2 * DI], on=st)
            taps = sbuf("taps", [P, DI, CONV], on=st)
            pq = psum("pq", [P, BANK], on=st)
            pv = psum("pv", [P, BANK], on=st)
            pd = psum("pd", [P, BANK], on=st)
            zeroed = new_sem("setup_zeroed")
            loaded = new_sem("setup_loaded")
            masks = new_sem("setup_masks")
            acts = new_sem("setup_acts")
            prods = new_sem("setup_prods")
            dves = new_sem("setup_dves")

            loads = []
            for i in range(2):
                c0 = C * i
                loads += [
                    (wq2[:, i, :], wq), (wv2[:, i, :], wv),
                    (w_router[c0:c0 + C, NE * i:NE * i + NE], router_w),
                    (w_exp[c0:c0 + C, :, c0:c0 + C], expert_w.rearrange("e d c -> d e c")),
                    (pos_t[c0:c0 + C, :], pos.rearrange("a c h w -> (a c) (h w)")),
                    (w_in_t[c0:c0 + C, :], w_in),
                    (w_gate[c0:c0 + C, EC * i:EC * i + EC], gate_w.rearrange("e c -> c e")),
                    (b_gate[EC * i:EC * i + EC, :], gate_b.rearrange("(e a) -> e a", a=1)),
                ]
                for part in range(3):
                    r0 = 16 * part + NE * i
                    loads.append((b_exp[r0:r0 + NE, c0:c0 + C], expert_b))
            for n, v in enumerate((gamma, beta, mean, var)):
                loads.append((bn_row[:, n, :], v.partition_broadcast(P)))
            for n in range(4):
                for b in range(4):
                    loads.append((decay[32 * n:32 * n + 32, b, :],
                                  a_log.rearrange("(b j) (m n) -> b n j m", j=32, n=4)[b, n]))
            loads += [
                (wk_t[:, :], wk), (wo_t[:, :], wo.rearrange("o m -> m o")),
                (b_router[:, :], router_b.partition_broadcast(P)),
                (taps[:, :, :].rearrange("p d k -> p (d k)"), conv_w.rearrange("d k -> (d k)").partition_broadcast(P)),
                (conv_bias[:, :], conv_b.rearrange("(c a) -> c a", a=1)),
                (wx[:, :], w_xproj), (wx4[:, :], w_xproj[:, 0:RK].rearrange("d r -> r d")),
                (wdt[:, :], w_dt), (dt_bias[:, :], b_dt.rearrange("(c a) -> c a", a=1)),
                (skip_col[:, :], d_skip.rearrange("(c a) -> c a", a=1)),
                (w_out_t[:, :], w_out),
            ]

            with nc.Block() as block:
                @block.sync
                def _(sp):
                    sp.wait_ge(zeroed, 8)
                    for dst, src in loads:
                        with nc.allow_non_contiguous_dma(reason="small weights, once"):
                            sp.dma_start(dst, src).then_inc(loaded, 16)
                    sp.wait_ge(loaded, 16 * len(loads))

                @block.gpsimd
                def _(pool):
                    g = nc.gpsimd
                    n = [0]

                    def link(ins):
                        n[0] += 1
                        ins.then_inc(masks, 1)
                        pool.wait_ge(masks, n[0])

                    def mark(t, pattern, base=0):
                        link(g.affine_select(out=t, in_=t, compare_op=ALU.not_equal, fill=1.0, base=base,
                                             pattern=pattern, channel_multiplier=1))

                    for t in (ident, ident_bf, pick, spread, fold4, average, rows_bc):
                        link(g.memset(t[:], 0.0))
                    link(g.memset(average[0:C, 0:C], 1.0 / C))
                    link(g.memset(average[C:P, C:P], 1.0 / C))
                    mark(ident[:], [[-1, P]])
                    mark(ident_bf[:], [[-1, P]])
                    mark(spread[:].rearrange("p b (n j) -> p b n j", j=32), [[-32, 4], [0, 4], [-1, 32]])
                    mark(fold4[:], [[-32, 4], [-1, 32]])
                    for part in range(3):
                        mark(pick[:].rearrange("r e (i c) -> r e i c", i=2), [[-1, NE], [-NE, 2], [0, C]], -16 * part)
                    for part in (0, 2, 3):
                        mark(rows_bc[:].rearrange("r m (n j) -> r m n j", j=32), [[-4, 8], [-1, 4], [0, 32]], -32 * part)
                    link(g.iota(rank8[:], pattern=[[-1, NE]], base=NE, channel_multiplier=0,
                                allow_small_or_imprecise_dtypes=True))

                @block.scalar
                def _(act):
                    act.wait_ge(zeroed, 11)
                    act.wait_ge(loaded, 16 * len(loads))
                    nc.scalar.activation(inv_row[:], bn_row[:, 3, :], ACT.Ln, bias=eps_bn[:]).then_inc(acts, 1)
                    act.wait_ge(acts, 1)
                    nc.scalar.activation(inv_row[:], inv_row[:], ACT.Exp, scale=-0.5).then_inc(acts, 1)
                    nc.scalar.activation(decay[:], decay[:], ACT.Exp).then_inc(acts, 1)

                @block.tensor
                def _(pe):
                    pe.wait_ge(loaded, 16 * len(loads))
                    nc.tensor.matmul(pq[:, 0:C], wq2[:].rearrange("m i c -> m (i c)"), wk_t[:],
                                     start=True, stop=True).then_inc(prods, 1)
                    nc.tensor.matmul(pv[:, 0:C], wv2[:].rearrange("m i c -> m (i c)"), wo_t[:],
                                     start=True, stop=True).then_inc(prods, 1)
                    nc.tensor.matmul(pd[:, 0:DI], wx4[:], wdt[:], start=True, stop=True).then_inc(prods, 1)

                @block.vector
                def _(dve):
                    v = nc.vector
                    for t in (w_router, w_exp, b_exp, w_gate, w_qk, w_vo, w_z, w_conv):
                        v.memset(t[:], 0.0).then_inc(zeroed, 1)
                    v.memset(eps_bn[:], 1e-5).then_inc(zeroed, 1)
                    v.memset(eps_6[:], 1e-6).then_inc(zeroed, 1)
                    v.memset(one_col[:], 1.0).then_inc(zeroed, 1)
                    dve.wait_ge(zeroed, 11)
                    dve.wait_ge(masks, 20)
                    dve.wait_ge(acts, 3)
                    dve.wait_ge(prods, 3)
                    n = [0]

                    def link(ins):
                        n[0] += 1
                        ins.then_inc(dves, 1)
                        dve.wait_ge(dves, n[0])

                    link(v.tensor_tensor(center[:], ident[:], average[:], ALU.subtract))
                    link(v.tensor_tensor(inv_row[:], inv_row[:], bn_row[:, 0, :], ALU.mult))
                    link(v.tensor_tensor(tmp_row[:], inv_row[:], bn_row[:, 2, :], ALU.mult))
                    for c0 in (0, C):
                        link(v.tensor_tensor(shift[:, c0:c0 + C], bn_row[:, 1, :], tmp_row[:], ALU.subtract))
                    for c0 in (0, C):
                        s = slice(c0, c0 + C)
                        link(v.tensor_scalar(w_qk[s, s], pq[s, 0:C], float(C // 2) ** -0.5, None, ALU.mult))
                        link(v.tensor_tensor(w_vo[s, s], pv[s, 0:C], inv_row[s, :], ALU.mult))
                    link(v.tensor_copy(b_exp3[:, 0, :], b_exp[:]))
                    link(v.tensor_tensor(rest[:], b_exp[:], b_exp3[:, 0, :], ALU.subtract))
                    link(v.tensor_copy(b_exp3[:, 1, :], rest[:]))
                    link(v.tensor_tensor(rest2[:], rest[:], b_exp3[:, 1, :], ALU.subtract))
                    link(v.tensor_copy(b_exp3[:, 2, :], rest2[:]))
                    for i in range(2):
                        q = slice(C * i, C * i + C)
                        link(v.tensor_copy(w_z[q, i, :], w_in_t[q, DI:2 * DI]))
                        for k in range(CONV):
                            link(v.tensor_tensor(w_conv[q, i, k, :], w_in_t[q, 0:DI], taps[q, :, k], ALU.mult))
                    link(v.tensor_copy(w_dt_full[:], pd[:, 0:DI]))
                    link(v.tensor_scalar(decay[:], decay[:], -1.0, -1e-12, ALU.mult, ALU.min))
                    for part in range(4):
                        link(v.tensor_copy(w_bc[:, part, :], wx[:, RK:RK + 2 * NS]))
                    link(v.tensor_reduce(fold[:], fold4[:].rearrange("p n j -> p j n"), AX.X, ALU.add))
                    link(v.tensor_scalar(skip[:], ident[:], skip_col[:, 0:1], None, ALU.mult))


        def phase_a():
            HALF = SA // SLOTS
            with ExitStack() as st:
                def sb(name, shape, dt=F32):
                    return [sbuf(f"{name}{i}", shape, dt, st) for i in range(SLOTS)]

                xt = sb("a_x", [P, TA])
                sq = sb("a_sq", [P, TA])
                xw = sb("a_xw", [P, NWA, WP])
                ts = sb("a_t", [P, NWA, WP])
                pr = sb("a_p", [P, NWA, WP])
                pt = sb("a_pt", [P, NWA // 2, P])
                vw = sb("a_vw", [P, NWA // 2, P])
                mx = sb("a_mx", [P, NWA])
                sm = sb("a_sm", [P, NWA])
                x1 = sb("a_x1", [P, TA])
                xn = sb("a_xn", [P, TA])
                xg = [sbuf(f"a_xg{i}", [P, TA], F32, st) for i in range(2 * SLOTS)]
                res = sb("a_res", [P, TA])
                lg = sb("a_lg", [W, 2 * WIN, NE])
                ex = sb("a_ex", [W, 2 * WIN, NE])
                cd = sb("a_cd", [W, 2 * WIN, NE])
                o1 = sb("a_o1", [W, 2 * WIN, NE])
                o2 = sb("a_o2", [W, 2 * WIN, NE])
                g1 = sb("a_g1", [W, 2 * WIN])
                g3 = sb("a_g3", [W, WIN, 48], BF16)
                gt = sb("a_gt", [48, TA], BF16)
                pa = [psum(f"a_pa{i}", [P, 2 * BANK], F32, st) for i in range(SLOTS)]
                pb = [psum(f"a_pb{i}", [P, 2 * BANK], F32, st) for i in range(SLOTS)]

                def sems(name, turn=1):
                    return new_sems("a_" + name, SLOTS, turn)

                pads_zero = new_sem("a_pads")
                x_loaded, stored = sems("loaded", 16), sems("stored", 16)
                xc_ready, sq_ready, var_ready, ln_ready, rstd_ready = (sems(n) for n in ("xc", "sq", "var", "ln", "rstd"))
                xw_ready = sems("xw", 2)
                t_ready, ts_ready, score_ready, max_ready, sub_ready, exp_ready, sum_ready, rec_ready, prob_ready = (
                    sems(n) for n in ("t", "ts", "score", "max", "sub", "exp", "sum", "rec", "prob"))
                tr_ready, pt_ready, v_ready, vw_ready, o_ready, x1_ready = (
                    sems(n) for n in ("tr", "pt", "v", "vw", "o", "x1"))
                xc2_ready, sq2_ready, var2_ready, ln2_ready, rstd2_ready, xn_ready = (
                    sems(n) for n in ("xc2_", "sq2_", "var2_", "ln2_", "rstd2_", "xn"))
                rout_ready, expl_ready, gtr_ready, gt_ready = (sems(n) for n in ("rout", "expl", "gtr", "gt"))
                small = sems("small", SMALL)
                gate_ready, xg_ready, moe_ready = (sems(n, NE) for n in ("gate", "xg", "moe"))
                acc_ready, res_ready = sems("acc"), sems("res")
                nc.all_engine_barrier()

                def win(t):
                    return t[:].rearrange("p (r w c) -> p r w c", r=WIN, c=WIN)

                def by_win(t):
                    return t[:, :, 0:WT].rearrange("p w (r c) -> p r w c", r=WIN)

                with nc.Block() as block:
                    @block.sync
                    def _(sp):
                        for k in range(NP):
                            with sp.Fori(0, HALF) as j:
                                it = j + (k * HALF + 1)
                                for s in range(SLOTS):
                                    at = (j * SLOTS + s) * TA
                                    sp.wait_ge(x1_ready[s], it)
                                    sp.dma_start(xt[s][:], x_v[k, :, bass.ds(at, TA)]).then_inc(x_loaded[s], 16)
                                for s in range(SLOTS):
                                    at = (j * SLOTS + s) * TA
                                    sp.wait_ge(res_ready[s], it + 1)
                                    sp.dma_start(x2[:, bass.ds(at + k * HW, TA)], res[s][:]).then_inc(stored[s], 16)
                        for s in range(SLOTS):
                            sp.wait_ge(stored[s], 16 * (NP * HALF + 1))

                    @block.gpsimd
                    def _(pool):
                        for s in range(SLOTS):
                            nc.gpsimd.memset(xw[s][:], 0.0).then_inc(pads_zero, 1)
                            nc.gpsimd.memset(pr[s][:], 0.0).then_inc(pads_zero, 1)

                    @block.scalar
                    def _(act):
                        a = nc.scalar.activation
                        nc.scalar.preload_act_table_set("natural_log_exp_and_others")
                        act.wait_ge(pads_zero, 2 * SLOTS)
                        with act.Fori(1, NP * HALF + 1) as it:
                            for s in range(SLOTS):
                                act.wait_ge(xc_ready[s], it + 1)
                                a(sq[s][:], pa[s][:, 0:TA], ACT.Square).then_inc(sq_ready[s], 1)
                            for s in range(SLOTS):
                                act.wait_ge(var_ready[s], it + 1)
                                a(sq[s][:], pb[s][:, 0:TA], ACT.Ln, bias=eps_6[:]).then_inc(ln_ready[s], 1)
                            for s in range(SLOTS):
                                act.wait_ge(ln_ready[s], it + 1)
                                a(sq[s][:], sq[s][:], ACT.Exp, scale=-0.5).then_inc(rstd_ready[s], 1)
                            for s in range(SLOTS):
                                act.wait_ge(t_ready[s], it + 1)
                                a(ts[s][:].rearrange("p w t -> p (w t)"), pb[s][:, 0:NWA * WP], ACT.Copy).then_inc(ts_ready[s], 1)
                            for s in range(SLOTS):
                                act.wait_ge(sub_ready[s], it + 1)
                                a(pr[s][:, :, 0:WT], pr[s][:, :, 0:WT], ACT.Exp).then_inc(exp_ready[s], 1)
                            for s in range(SLOTS):
                                act.wait_ge(tr_ready[s], it + 1)
                                a(pt[s][:].rearrange("p w t -> p (w t)"), pb[s][:, 0:NWA * WP], ACT.Copy).then_inc(pt_ready[s], 1)
                            for s in range(SLOTS):
                                act.wait_ge(xc2_ready[s], it + 1)
                                a(sq[s][:], pa[s][:, 0:TA], ACT.Square).then_inc(sq2_ready[s], 1)
                            for s in range(SLOTS):
                                act.wait_ge(var2_ready[s], it + 1)
                                a(sq[s][:], pb[s][:, 0:TA], ACT.Ln, bias=eps_bn[:]).then_inc(ln2_ready[s], 1)
                            for s in range(SLOTS):
                                act.wait_ge(ln2_ready[s], it + 1)
                                a(sq[s][:], sq[s][:], ACT.Exp, scale=-0.5).then_inc(rstd2_ready[s], 1)
                            for s in range(SLOTS):
                                act.wait_ge(small[s], SMALL * it + 3)
                                a(ex[s][:], lg[s][:], ACT.Exp).then_inc(expl_ready[s], 1)
                            for s in range(SLOTS):
                                act.wait_ge(gtr_ready[s], it + 1)
                                a(gt[s][:].rearrange("g (r w) -> g r w", r=WIN),
                                  pb[s][0:48, 0:WIN * P].rearrange("g (r w) -> g r w", r=WIN)[:, :, 0:W], ACT.Copy).then_inc(gt_ready[s], 1)

                    @block.vector
                    def _(dve):
                        v = nc.vector
                        dve.wait_ge(pads_zero, 2 * SLOTS)
                        with dve.Fori(1, NP * HALF + 1) as it:
                            for s in range(SLOTS):
                                dve.wait_ge(rstd_ready[s], it + 1)
                                for side in range(2):
                                    ws = slice(side * (NWA // 2), (side + 1) * (NWA // 2))
                                    v.tensor_tensor(by_win(xw[s][:, side::2, :]), win(pa[s][:, 0:TA])[:, :, ws], win(sq[s])[:, :, ws],
                                                    ALU.mult).then_inc(xw_ready[s], 1)
                            for s in range(SLOTS):
                                score = pa[s][:].rearrange("p (w t) -> p w t", t=WP)[:, :, 0:WT]
                                dve.wait_ge(score_ready[s], it + 1)
                                v.tensor_reduce(mx[s][:], score, AX.X, ALU.max).then_inc(max_ready[s], 1)
                            for s in range(SLOTS):
                                score = pa[s][:].rearrange("p (w t) -> p w t", t=WP)[:, :, 0:WT]
                                dve.wait_ge(max_ready[s], it + 1)
                                v.tensor_tensor(pr[s][:, :, 0:WT], score, mx[s][:].unsqueeze(2).broadcast_to([P, NWA, WT]),
                                                ALU.subtract).then_inc(sub_ready[s], 1)
                            for s in range(SLOTS):
                                dve.wait_ge(v_ready[s], it + 1)
                                v.tensor_tensor(vw[s][:], pa[s][:, 0:NWA * WP].rearrange("p (w t) -> p w t", t=P),
                                                shift[:].unsqueeze(1).broadcast_to([P, NWA // 2, P]), ALU.add).then_inc(vw_ready[s], 1)
                            for s in range(SLOTS):
                                dve.wait_ge(exp_ready[s], it + 1)
                                v.tensor_reduce(sm[s][:], pr[s][:, :, 0:WT], AX.X, ALU.add).then_inc(sum_ready[s], 1)
                            for s in range(SLOTS):
                                dve.wait_ge(sum_ready[s], it + 1)
                                v.reciprocal(mx[s][:], sm[s][:]).then_inc(rec_ready[s], 1)
                            for s in range(SLOTS):
                                dve.wait_ge(rec_ready[s], it + 1)
                                v.tensor_tensor(pr[s][:, :, 0:WT], pr[s][:, :, 0:WT],
                                                mx[s][:].unsqueeze(2).broadcast_to([P, NWA, WT]), ALU.mult).then_inc(prob_ready[s], 1)
                            for s in range(SLOTS):
                                o = pb[s][:].rearrange("p (w t) -> p w t", t=WP)
                                dve.wait_ge(o_ready[s], it + 1)
                                v.tensor_tensor(win(x1[s]), by_win(o), win(xt[s]), ALU.add).then_inc(x1_ready[s], 1)
                            for s in range(SLOTS):
                                dve.wait_ge(rstd2_ready[s], it + 1)
                                v.tensor_tensor(xn[s][:], pa[s][:, 0:TA], sq[s][:], ALU.mult).then_inc(xn_ready[s], 1)

                            shape = [W, 2 * WIN, NE]
                            rank = rank8[0:W, :].unsqueeze(1).broadcast_to(shape)
                            bias = b_router[0:W, :].unsqueeze(1).broadcast_to(shape)

                            def wide(s):
                                return g1[s][:].unsqueeze(2).broadcast_to(shape)

                            def part(s, n):
                                return g3[s][:, :, 16 * n:16 * n + 16]

                            def rows(t):
                                return t[:].rearrange("p (r i) e -> p r (i e)", i=2)

                            def chain(s, n):
                                dve.wait_ge(small[s], SMALL * it + n)

                            for s in range(SLOTS):
                                dve.wait_ge(rout_ready[s], it + 1)
                                v.tensor_tensor(lg[s][:], pa[s][0:W, 0:2 * WIN * NE].rearrange("p (r e) -> p r e", e=NE), bias,
                                                ALU.add).then_inc(small[s], 1)
                            for s in range(SLOTS):
                                chain(s, 1)
                                v.tensor_reduce(g1[s][:], lg[s][:], AX.X, ALU.max).then_inc(small[s], 1)
                            for s in range(SLOTS):
                                chain(s, 2)
                                v.tensor_tensor(lg[s][:], lg[s][:], wide(s), ALU.subtract).then_inc(small[s], 1)
                            for s in range(SLOTS):
                                chain(s, 3)
                                v.scalar_tensor_tensor(cd[s][:], lg[s][:], 0.0, rank, ALU.is_ge, ALU.mult).then_inc(small[s], 1)
                            for s in range(SLOTS):
                                chain(s, 4)
                                v.tensor_reduce(g1[s][:], cd[s][:], AX.X, ALU.max).then_inc(small[s], 1)
                            for s in range(SLOTS):
                                chain(s, 5)
                                v.tensor_tensor(o1[s][:], cd[s][:], wide(s), ALU.is_equal).then_inc(small[s], 1)
                            for s in range(SLOTS):
                                dve.wait_ge(expl_ready[s], it + 1)
                                chain(s, 6)
                                v.scalar_tensor_tensor(lg[s][:], o1[s][:], -BIG, lg[s][:], ALU.mult, ALU.add).then_inc(small[s], 1)
                            for s in range(SLOTS):
                                chain(s, 7)
                                v.tensor_reduce(g1[s][:], lg[s][:], AX.X, ALU.max).then_inc(small[s], 1)
                            for s in range(SLOTS):
                                chain(s, 8)
                                v.tensor_tensor(cd[s][:], lg[s][:], wide(s), ALU.is_ge).then_inc(small[s], 1)
                            for s in range(SLOTS):
                                chain(s, 9)
                                v.tensor_tensor(cd[s][:], cd[s][:], rank, ALU.mult).then_inc(small[s], 1)
                            for s in range(SLOTS):
                                chain(s, 10)
                                v.tensor_reduce(g1[s][:], cd[s][:], AX.X, ALU.max).then_inc(small[s], 1)
                            for s in range(SLOTS):
                                chain(s, 11)
                                v.tensor_tensor(o2[s][:], cd[s][:], wide(s), ALU.is_equal).then_inc(small[s], 1)
                            for s in range(SLOTS):
                                chain(s, 12)
                                v.tensor_tensor(o1[s][:], o1[s][:], o2[s][:], ALU.add).then_inc(small[s], 1)
                            for s in range(SLOTS):
                                chain(s, 13)
                                v.tensor_tensor(o1[s][:], o1[s][:], ex[s][:], ALU.mult).then_inc(small[s], 1)
                            for s in range(SLOTS):
                                chain(s, 14)
                                v.tensor_reduce(g1[s][:], o1[s][:], AX.X, ALU.add).then_inc(small[s], 1)
                            for s in range(SLOTS):
                                chain(s, 15)
                                v.reciprocal(g1[s][:], g1[s][:]).then_inc(small[s], 1)
                            for s in range(SLOTS):
                                chain(s, 16)
                                v.tensor_tensor(o1[s][:], o1[s][:], wide(s), ALU.mult).then_inc(small[s], 1)
                            for s in range(SLOTS):
                                chain(s, 17)
                                v.tensor_copy(part(s, 0), rows(o1[s])).then_inc(small[s], 1)
                            for s in range(SLOTS):
                                chain(s, 18)
                                v.tensor_tensor(rows(cd[s]), rows(o1[s]), part(s, 0), ALU.subtract).then_inc(small[s], 1)
                            for s in range(SLOTS):
                                chain(s, 19)
                                v.tensor_copy(part(s, 1), rows(cd[s])).then_inc(small[s], 1)
                            for s in range(SLOTS):
                                chain(s, 20)
                                v.tensor_tensor(part(s, 2), rows(cd[s]), part(s, 1), ALU.subtract).then_inc(small[s], 1)
                            for x in range(NE):
                                for s in range(SLOTS):
                                    dve.wait_ge(gate_ready[s], NE * it + x + 1)
                                    if x >= 2:
                                        dve.wait_ge(moe_ready[s], NE * it + x - 1)
                                    v.tensor_tensor(xg[2 * s + x % 2][:], xn[s][:], pb[s][:, 0:TA], ALU.mult).then_inc(xg_ready[s], 1)
                            for s in range(SLOTS):
                                dve.wait_ge(acc_ready[s], it + 1)
                                dve.wait_ge(stored[s], 16 * it)
                                v.tensor_tensor(res[s][:], pa[s][:, 0:TA], x1[s][:], ALU.add).then_inc(res_ready[s], 1)

                    @block.tensor
                    def _(pe):
                        mm = nc.tensor.matmul
                        pe.wait_ge(pads_zero, 2 * SLOTS)

                        def strip(dst, weight, src):
                            for a, b in banks(TA):
                                last = mm(dst[:, a:b], weight, src[:, a:b], start=True, stop=True)
                            return last

                        with pe.Fori(1, NP * HALF + 1) as it:
                            for s in range(SLOTS):
                                pe.wait_ge(x_loaded[s], 16 * it + 16)
                                pe.wait_ge(res_ready[s], it)
                                strip(pa[s], center[:], xt[s]).then_inc(xc_ready[s], 1)
                            for s in range(SLOTS):
                                pe.wait_ge(sq_ready[s], it + 1)
                                strip(pb[s], average[:], sq[s]).then_inc(var_ready[s], 1)
                            for s in range(SLOTS):
                                pe.wait_ge(xw_ready[s], 2 * it + 2)
                                for a, b in banks(NWA * WP):
                                    last = mm(pb[s][:, a:b], w_qk[:], xw[s][:].rearrange("p w t -> p (w t)")[:, a:b],
                                              start=True, stop=True)
                                last.then_inc(t_ready[s], 1)
                            for s in range(SLOTS):
                                pe.wait_ge(pads_zero, 2 * SLOTS)
                                pe.wait_ge(ts_ready[s], it + 1)
                                for w in range(NWA):
                                    for i in range(2):
                                        r = slice(C * i, C * i + C)
                                        last = mm(pa[s][r, w * WP:w * WP + WT], ts[s][r, w, :], xw[s][r, w, 0:WT],
                                                  start=True, stop=True)
                                last.then_inc(score_ready[s], 1)
                            for s in range(SLOTS):
                                pe.wait_ge(sub_ready[s], it + 1)
                                for w in range(NWA // 2):
                                    last = mm(pa[s][:, w * P:(w + 1) * P], xw[s][:, 2 * w:2 * w + 2, :].rearrange("p w t -> p (w t)"),
                                              w_vo[:], start=True, stop=True)
                                last.then_inc(v_ready[s], 1)
                            for s in range(SLOTS):
                                pe.wait_ge(prob_ready[s], it + 1)
                                for w in range(NWA // 2):
                                    last = nc.tensor.transpose(pb[s][:, w * P:(w + 1) * P],
                                                               pr[s][:, 2 * w:2 * w + 2, :].rearrange("p w t -> p (w t)"), ident[:])
                                last.then_inc(tr_ready[s], 1)
                            for s in range(SLOTS):
                                pe.wait_ge(pads_zero, 2 * SLOTS)
                                pe.wait_ge(pt_ready[s], it + 1)
                                pe.wait_ge(vw_ready[s], it + 1)
                                for w in range(NWA):
                                    side, q = w // (NWA // 2), w % (NWA // 2)
                                    h = slice(WP * side, WP * side + WP)
                                    for i in range(2):
                                        last = mm(pb[s][C * i:C * i + C, w * WP:w * WP + WT], vw[s][h, q, C * i:C * i + C],
                                                  pt[s][h, q, WP * i:WP * i + WT], start=True, stop=True)
                                last.then_inc(o_ready[s], 1)
                            for s in range(SLOTS):
                                pe.wait_ge(x1_ready[s], it + 1)
                                strip(pa[s], center[:], x1[s]).then_inc(xc2_ready[s], 1)
                            for s in range(SLOTS):
                                pe.wait_ge(sq2_ready[s], it + 1)
                                strip(pb[s], average[:], sq[s]).then_inc(var2_ready[s], 1)
                            for s in range(SLOTS):
                                pe.wait_ge(xn_ready[s], it + 1)
                                for r in range(WIN):
                                    last = mm(pa[s][0:W, r * 2 * NE:(r + 1) * 2 * NE], xn[s][:, r * W:(r + 1) * W], w_router[:],
                                              start=True, stop=True)
                                last.then_inc(rout_ready[s], 1)
                            for s in range(SLOTS):
                                pe.wait_ge(small[s], SMALL * it + SMALL)
                                for r in range(WIN):
                                    last = mm(pb[s][0:48, r * P:r * P + W], g3[s][:, r, :], ident_bf[0:W, 0:W],
                                              start=True, stop=True)
                                last.then_inc(gtr_ready[s], 1)

                            def spread_gate(s, x):
                                for a, b in banks(TA):
                                    last = mm(pb[s][:, a:b], pick[:, x, :], gt[s][:, a:b], start=True, stop=True)
                                last.then_inc(gate_ready[s], 1)

                            for s in range(SLOTS):
                                pe.wait_ge(gt_ready[s], it + 1)
                                spread_gate(s, 0)
                            for x in range(NE):
                                for s in range(SLOTS):
                                    pe.wait_ge(xg_ready[s], NE * it + x + 1)
                                    if x < NE - 1:
                                        spread_gate(s, x + 1)
                                    for a, b in banks(TA):
                                        last = mm(pa[s][:, a:b], w_exp[:, x, :], xg[2 * s + x % 2][:, a:b],
                                                  start=(x == 0), stop=False)
                                    last.then_inc(moe_ready[s], 1)
                            for s in range(SLOTS):
                                for n in range(3):
                                    for a, b in banks(TA):
                                        last = mm(pa[s][:, a:b], b_exp3[:, n, :], gt[s][:, a:b], start=False, stop=(n == 2))
                                last.then_inc(acc_ready[s], 1)

        def phase_b():
            N = NP * SB

            final = ("out", "xc2", "var2", "lgp", "tok0", "tok1")
            ahead = ("xc", "var", "z", "conv", "pre", "xp", "ndt0", "ndu0", "ndt1", "ndu1", "nB", "ndt2", "ndu2", "nC")
            core0 = ("dt3", "du3", "B1", "C1", "z", "conv", "B2", "C2", "out", "pre", "xc2", "var2", "xp", "B3", "C3",
                     "lgp", "tok0", "tok1", "ndt0", "ndu0", "ndt1", "ndu1", "nB", "ndt2", "ndu2", "nC")
            core1 = ("dt3", "du3", "xc", "B1", "C1", "var", "z", "conv", "B2", "C2", "pre", "xp", "B3", "C3",
                     "ndt0", "ndu0", "ndt1", "ndu1", "nB", "ndt2", "ndu2", "nC")
            whole = [(0, n) for n in core0] + [(1, n) for n in core1]
            first_turn = [(0, n) for n in core0 if n not in final]
            last_turn = [(0, n) for n in core0] + [(1, n) for n in core1 if n not in ahead] + [(2, n) for n in final]
            TURN = len(whole)
            assert TURN % 2 == 0 and N >= 3
            MIDDLE, FIRST, LAST = "middle", "first", "last"

            def place(core, name, it, kind):
                if core == -1:
                    c = ahead.index(name)
                elif core == 0 and kind == FIRST:
                    c = len(ahead) + first_turn.index((0, name))
                elif core >= 1 and kind == LAST:
                    c = len(ahead) - len(final) + TURN * (N - 1) + last_turn.index((core, name))
                else:
                    c = len(ahead) - len(final) - TURN + whole.index((core, name))
                    return c % 2, it * (TURN // 2) + c // 2
                return c % 2, c // 2

            with ExitStack() as st:
                def sb(name, shape, dt=F32):
                    return sbuf("b_" + name, shape, dt, st)

                def ring(name, n):
                    return [sb(f"{name}{i}", [P, TB]) for i in range(n)]

                def sem(name, turn=1):
                    return new_sem("b_" + name, turn)

                def sems(name, n=2, turn=1):
                    return [sem(f"{name}{i}", turn) for i in range(n)]

                xt = sb("x", [P, TB])
                xr = sb("xr", [P, TB])
                sq = sb("sq", [P, TB])
                xc = sb("xc", [P, TB])
                seq = sb("seq", [P, NWB, CONV - 1 + ST])
                resets = sb("resets", [P, NWB])
                x3s = sb("x3s", [P, TB])
                sq2 = sb("sq2", [P, TB])
                xl = sb("xl", [P, TB])
                lg = sb("lg", [2 * EC, TB])
                tok = sb("tok", [P, TB])
                gate = ring("gate", 2)
                yz = ring("yz", 2)
                u, dt, dtu, t1, t2, rest = (sb(n, [P, TB]) for n in ("u", "dt", "dtu", "t1", "t2", "rest"))
                parts = [sb(f"parts{i}", [P, TB], BF16) for i in range(2)]
                dts = ring("dts", 4)
                dus = ring("dus", 4)
                bt = ring("bt", 2)
                ct = ring("ct", 2)
                aa = ring("a", RA)
                bb = ring("b", RB)
                hh = ring("h", RA)
                hc = ring("hc", RC)
                ww = [psum(f"b_w{i}", [P, 2 * BANK], F32, st) for i in range(2)]
                yy = [psum(f"b_y{i}", [P, 2 * BANK], F32, st) for i in range(2)]

                pads_zero = sem("pads", 0)
                x_loaded, xr_loaded, x3_stored, lg_stored = (sem(n, 16) for n in ("loaded", "xrl", "x3st", "lgst"))
                tok_stored = sem("tokst", 32)
                made = sems("made")
                moved = sems("moved")
                sq_ready, rstd_ready, xn_ready, seq_ready = (sem(n) for n in ("sq", "rstd", "xn", "seq"))
                abs_ready, e_ready, l_ready, dt_ready, dtu_ready, reset_ready = (
                    sems(n) for n in ("abs", "e", "l", "dt", "dtu", "reset"))
                high_ready, mid_ready, parts_ready, skip_ready, yz_ready = (
                    sems(n) for n in ("high", "mid", "parts", "skip", "yz"))
                a_ready, h_ready = (sems(n, RA, TILES // RA) for n in ("a", "h"))
                b_ready = sems("b", RB, TILES // RB)
                hc_ready = sems("hc", RC, TILES // RC)
                folded = sem("fold", 8)
                sq2_ready, rstd2_ready, xl_ready = (sem(n) for n in ("sq2", "rstd2", "xl"))
                nc.all_engine_barrier()

                def win(t):
                    return t[:, 0:TB].rearrange("p (r w c) -> p r w c", r=WS, c=WS)

                def seqs(t):
                    return t[:, 0:TB].rearrange("p (w r c) -> p r w c", r=WS, c=WS)

                tokens_v = tokens.rearrange("(i r p) c -> i p r c", i=2, p=P)

                def used(it, s, n):
                    return it * (TILES // n) + s // n

                def wait_made(eng, core, name, it, kind):
                    w, c = place(core, name, it, kind)
                    eng.wait_ge(made[w], c + 2)
                    return ww[w]

                def wait_moved(eng, core, name, it, kind):
                    w, c = place(core, name, it, kind)
                    eng.wait_ge(moved[w], c + 2)

                def read(core, name, it, kind):
                    return moved[place(core, name, it, kind)[0]]

                def before(i, it, kind):
                    if i:
                        return 0, it, kind
                    return (-1, it, kind) if kind == FIRST else (1, it - 1, MIDDLE)

                def wait_spread(eng, name, t, i, it, kind):
                    if t < 3:
                        wait_moved(eng, before(i, it, kind)[0], f"n{name}{t}", *before(i, it, kind)[1:])
                    elif t == 3:
                        wait_moved(eng, i, f"{name}3", it, kind)

                def wait_block(eng, name, t, i, it, kind):
                    if t == 0:
                        wait_moved(eng, before(i, it, kind)[0], f"n{name}", *before(i, it, kind)[1:])
                    elif t % 4 == 0:
                        wait_moved(eng, i, f"{name}{t // 4}", it, kind)

                with nc.Block() as block:
                    @block.sync
                    def _(sp):
                        def turn(it, kind):
                            p = it - 1
                            if kind != LAST:
                                sp.wait_ge(sq_ready, it + 1)
                                sp.dma_start(xt[:], x2[:, bass.ds((p + 1) * TB, TB)]).then_inc(x_loaded, 16)
                            if kind != FIRST:
                                store(0, it, kind)
                            sp.dma_start(xr[:], x2[:, bass.ds(p * TB, TB)]).then_inc(xr_loaded, 16)

                        def store(core, it, kind):
                            p = it - 2
                            wait_moved(sp, core, "out", it - (core == 2), kind)
                            sp.dma_start(x3[:, bass.ds(p * TB, TB)], x3s[:]).then_inc(x3_stored, 16)
                            wait_moved(sp, core, "lgp", it - (core == 2), kind)
                            sp.dma_start(logits[:, bass.ds(p * TB, TB)], lg[:]).then_inc(lg_stored, 16)
                            wait_moved(sp, core, "tok0", it - (core == 2), kind)
                            wait_moved(sp, core, "tok1", it - (core == 2), kind)
                            for i in range(2):
                                sp.dma_start(tokens_v[i, :, bass.ds(p * NCH, NCH), :],
                                             tok[:].rearrange("p (n i c) -> p n i c", i=2, c=C)[:, :, i, :]).then_inc(tok_stored, 16)

                        sp.dma_start(xt[:], x2[:, 0:TB]).then_inc(x_loaded, 16)
                        turn(1, FIRST)
                        with sp.Fori(2, N) as it:
                            turn(it, MIDDLE)
                        turn(N, LAST)
                        store(2, N + 1, LAST)
                        sp.wait_ge(x3_stored, 16 * (N + 1))
                        sp.wait_ge(lg_stored, 16 * (N + 1))
                        sp.wait_ge(tok_stored, 32 * (N + 1))

                    @block.gpsimd
                    def _(pool):
                        def tile(t, i, it, kind):
                            s = UNIT * i + t
                            wait_block(pool, "C", t, i, it, kind)
                            pool.wait_ge(h_ready[s % RA], used(it, s, RA) + 1)
                            if t % 4 == 0:
                                pool.wait_ge(folded, 8 * it + s // 4 - RC // 4 + 1)
                            nc.gpsimd.tensor_tensor(hc[s % RC][:], hh[s % RA][:], ct[t // 4 % 2][:], ALU.mult).then_inc(hc_ready[s % RC], 1)

                        def products(i, o, cur):
                            if cur is not None:
                                wait_moved(pool, cur[0], "du3", *cur[1:])
                            pool.wait_ge(dt_ready[i], o + 1)
                            nc.gpsimd.tensor_tensor(dtu[:], dt[:], u[:], ALU.mult).then_inc(dtu_ready[i], 1)
                            pool.wait_ge(dtu_ready[i], o + 1)
                            first = dt[:].rearrange("p (w t) -> p w t", t=ST)[:, :, 0]
                            nc.gpsimd.tensor_tensor(first, first, resets[:], ALU.add).then_inc(reset_ready[i], 1)

                        def turn(it, kind):
                            for i in range(2):
                                for t in range(UNIT):
                                    tile(t, i, it, kind)
                                    if t == 9 and not (i and kind == LAST):
                                        products(1 - i, it + i, (i, it, kind))

                        nc.gpsimd.memset(seq[:], 0.0).then_inc(pads_zero, 1)
                        nc.gpsimd.memset(resets[:], RESET).then_inc(pads_zero, 1)
                        pool.wait_ge(pads_zero, 2)
                        products(0, 1, None)
                        turn(1, FIRST)
                        with pool.Fori(2, N) as it:
                            turn(it, MIDDLE)
                        turn(N, LAST)

                    @block.scalar
                    def _(act):
                        a = nc.scalar.activation

                        def move(core, name, it, kind, dst, func=ACT.Copy, rows=P, cols=slice(0, TB), **more):
                            w = wait_made(act, core, name, it, kind)
                            a(dst, w[0:rows, cols], func, **more).then_inc(read(core, name, it, kind), 1)

                        def move_spread(core, b, name, it, kind, i, cur):
                            if cur is not None:
                                s = UNIT * i + 12 + b
                                act.wait_ge(a_ready[s % RA], used(cur, s, RA) + 1)
                            move(core, f"{name}dt{b}", it, kind, dts[b][:])
                            if cur is not None:
                                act.wait_ge(b_ready[s % RB], used(cur, s, RB) + 1)
                            move(core, f"{name}du{b}", it, kind, dus[b][:])

                        def move_block(core, name, m, it, kind, i, cur):
                            if cur is not None:
                                s = UNIT * i + 4 * (m - 2) + 3
                                if name[-2:] in ("nB", "B1", "B2", "B3"):
                                    act.wait_ge(b_ready[s % RB], used(cur, s, RB) + 1)
                                else:
                                    act.wait_ge(hc_ready[s % RC], used(cur, s, RC) + 1)
                            move(core, name, it, kind, (bt if "B" in name else ct)[m % 2][:])

                        def norm_start(core, it, kind, o):
                            act.wait_ge(seq_ready, o)
                            w = wait_made(act, core, "xc", it, kind)
                            a(sq[:], w[:, 0:TB], ACT.Square).then_inc(sq_ready, 1)
                            a(xc[:], w[:, 0:TB], ACT.Copy).then_inc(read(core, "xc", it, kind), 1)

                        def norm_end(core, it, kind):
                            move(core, "var", it, kind, sq[:], ACT.Ln, bias=eps_6[:])
                            wait_moved(act, core, "var", it, kind)
                            a(sq[:], sq[:], ACT.Exp, scale=-0.5).then_inc(rstd_ready, 1)

                        def silus(core, it, kind, i, o):
                            act.wait_ge(yz_ready[i], o)
                            move(core, "z", it, kind, gate[i][:], ACT.Silu)
                            act.wait_ge(skip_ready[1 - i], o + i)
                            act.wait_ge(dtu_ready[1 - i], o + i)
                            move(core, "conv", it, kind, u[:], ACT.Silu, bias=conv_bias[:])

                        def softplus_start(core, it, kind, i, o):
                            act.wait_ge(dt_ready[1 - i], o + i)
                            w = wait_made(act, core, "pre", it, kind)
                            a(t1[:], w[:, 0:TB], ACT.Abs, bias=dt_bias[:]).then_inc(abs_ready[i], 1)
                            a(t2[:], w[:, 0:TB], ACT.Relu, bias=dt_bias[:]).then_inc(read(core, "pre", it, kind), 1)

                        def softplus_exp(i, o):
                            act.wait_ge(abs_ready[i], o + 1)
                            a(t1[:], t1[:], ACT.Exp, scale=-1.0).then_inc(e_ready[i], 1)

                        def softplus_ln(i, o):
                            act.wait_ge(e_ready[i], o + 1)
                            a(t1[:], t1[:], ACT.Ln, bias=one_col[:]).then_inc(l_ready[i], 1)

                        def high_part(core, it, kind, i):
                            w = wait_made(act, core, "xp", it, kind)
                            a(parts[i][:], w[:, 0:TB], ACT.Copy).then_inc(high_ready[i], 1)

                        def final_norm_start(core, it, kind):
                            w = wait_made(act, core, "xc2", it, kind)
                            a(sq2[:], w[:, 0:TB], ACT.Square).then_inc(sq2_ready, 1)
                            a(xl[:], w[:, 0:TB], ACT.Copy).then_inc(read(core, "xc2", it, kind), 1)

                        def final_norm_end(core, it, kind):
                            move(core, "var2", it, kind, sq2[:], ACT.Ln, bias=eps_bn[:])
                            wait_moved(act, core, "var2", it, kind)
                            a(sq2[:], sq2[:], ACT.Exp, scale=-0.5).then_inc(rstd2_ready, 1)

                        def final_moves(core, it, kind, o):
                            act.wait_ge(lg_stored, 16 * o)
                            move(core, "lgp", it, kind, lg[:], ACT.Identity, rows=2 * EC, bias=b_gate[:])
                            act.wait_ge(tok_stored, 32 * o)
                            move(core, "tok0", it, kind, tok[:, 0:BANK], cols=slice(0, BANK))
                            move(core, "tok1", it, kind, tok[:, BANK:TB], cols=slice(0, TB - BANK))

                        def core(i, it, kind):
                            ends = kind == LAST and i == 1
                            finals = kind != FIRST and i == 0
                            n, o = 1 - i, it + i
                            here = (i, it, kind)
                            for t in range(UNIT):
                                s = UNIT * i + t
                                wait_spread(act, "dt", t, *here)
                                act.wait_ge(h_ready[s % RA], used(it, s, RA))
                                a(aa[s % RA][:], dts[t % 4][:], ACT.Exp,
                                  scale=decay[:, t % 4, t // 4:t // 4 + 1]).then_inc(a_ready[s % RA], 1)
                                if t == 0:
                                    move_spread(i, 3, "", it, kind, i - 1, it)
                                    if i and not ends:
                                        norm_start(i, it, kind, o)
                                if t == 1:
                                    move_block(i, "B1", 1, it, kind, i, it)
                                if t == 2:
                                    move_block(i, "C1", 1, it, kind, i, it)
                                    if i and not ends:
                                        norm_end(i, it, kind)
                                if t == 5 and not ends:
                                    silus(i, it, kind, n, o)
                                if t == 6:
                                    move_block(i, "B2", 2, it, kind, i, it)
                                    move_block(i, "C2", 2, it, kind, i, it)
                                if t == 8:
                                    if not ends:
                                        softplus_start(i, it, kind, n, o)
                                    if finals:
                                        final_norm_start(i, it, kind)
                                    if not ends:
                                        softplus_exp(n, o)
                                if t == 9:
                                    if finals:
                                        final_norm_end(i, it, kind)
                                    if not ends:
                                        softplus_ln(n, o)
                                        high_part(i, it, kind, n)
                                    move_block(i, "B3", 3, it, kind, i, it)
                                if t == 10:
                                    move_block(i, "C3", 3, it, kind, i, it)
                                if t == 12 and finals:
                                    final_moves(i, it, kind, it - 1)
                                if t == 13 and not ends:
                                    move_spread(i, 0, "n", it, kind, i, it)
                                if t == 14 and not ends:
                                    move_spread(i, 1, "n", it, kind, i, it)
                                    move_block(i, "nB", 4, it, kind, i, it)
                                if t == 15 and not ends:
                                    move_spread(i, 2, "n", it, kind, i, it)
                                    move_block(i, "nC", 4, it, kind, i, it)

                        here = (-1, 0, FIRST)
                        norm_start(*here, 1)
                        norm_end(*here)
                        silus(*here, 0, 1)
                        softplus_start(*here, 0, 1)
                        softplus_exp(0, 1)
                        softplus_ln(0, 1)
                        high_part(*here, 0)
                        move_spread(-1, 0, "n", 0, FIRST, 0, None)
                        move_spread(-1, 1, "n", 0, FIRST, 0, None)
                        move_block(-1, "nB", 0, 0, FIRST, 0, None)
                        move_spread(-1, 2, "n", 0, FIRST, 0, None)
                        move_block(-1, "nC", 0, 0, FIRST, 0, None)
                        for i in range(2):
                            core(i, 1, FIRST)
                        with act.Fori(2, N) as it:
                            for i in range(2):
                                core(i, it, MIDDLE)
                        for i in range(2):
                            core(i, N, LAST)
                        final_norm_start(2, N, LAST)
                        final_norm_end(2, N, LAST)
                        final_moves(2, N, LAST, N)

                    @block.vector
                    def _(dve):
                        v = nc.vector

                        def inputs(t, i, it, kind):
                            s = UNIT * i + t
                            wait_spread(dve, "du", t, i, it, kind)
                            wait_block(dve, "B", t, i, it, kind)
                            dve.wait_ge(h_ready[(s - RB) % RA], used(it, s - RB, RA) + 1)
                            v.tensor_tensor(bb[s % RB][:], dus[t % 4][:], bt[t // 4 % 2][:], ALU.mult).then_inc(b_ready[s % RB], 1)

                        def scan(s, it):
                            dve.wait_ge(a_ready[s % RA], used(it, s, RA) + 1)
                            dve.wait_ge(b_ready[s % RB], used(it, s, RB) + 1)
                            dve.wait_ge(hc_ready[(s - RA) % RC], used(it, s - RA, RC) + 1)
                            v.tensor_tensor_scan(hh[s % RA][:], aa[s % RA][:], bb[s % RB][:], 0.0,
                                                 ALU.mult, ALU.add).then_inc(h_ready[s % RA], 1)

                        def norm(core, it, kind, o, seq_free):
                            dve.wait_ge(rstd_ready, o + 1)
                            wait_moved(dve, core, "xc", it, kind)
                            v.tensor_tensor(xc[:], xc[:], sq[:], ALU.mult).then_inc(xn_ready, 1)
                            dve.wait_ge(xn_ready, o + 1)
                            if seq_free:
                                wait_moved(dve, 0, "conv", it, kind)
                            v.tensor_tensor(seq[:, :, CONV - 1:].rearrange("p w (r c) -> p r w c", c=WS), win(xc),
                                            pos_t[:].rearrange("p (r c) -> p r c", c=WS).unsqueeze(2).broadcast_to([P, WS, NWB, WS]),
                                            ALU.add).then_inc(seq_ready, 1)

                        def steps(i, o, cur):
                            dve.wait_ge(l_ready[i], o + 1)
                            wait_moved(dve, *cur[0:1], "pre", *cur[1:])
                            if cur[0] >= 0:
                                wait_moved(dve, cur[0], "dt3", *cur[1:])
                                dve.wait_ge(dtu_ready[1 - i], o + i)
                            v.tensor_tensor(dt[:], t1[:], t2[:], ALU.add).then_inc(dt_ready[i], 1)

                        def low_parts(i, o, cur):
                            h = slice(C, P)
                            w = wait_made(dve, cur[0], "xp", *cur[1:])
                            dve.wait_ge(high_ready[i], o + 1)
                            dve.wait_ge(parts_ready[1 - i], o + i)
                            v.tensor_tensor(rest[h, :], w[h, 0:TB], parts[i][h, :], ALU.subtract).then_inc(read(cur[0], "xp", *cur[1:]), 1)
                            wait_moved(dve, cur[0], "xp", *cur[1:])
                            v.tensor_copy(parts[i][h, :], rest[h, :]).then_inc(mid_ready[i], 1)
                            dve.wait_ge(mid_ready[i], o + 1)
                            q = slice(96, P)
                            v.tensor_tensor(parts[i][q, :], rest[q, :], parts[i][q, :], ALU.subtract).then_inc(parts_ready[i], 1)

                        def gated(i, it, rows):
                            dve.wait_ge(folded, rows)
                            v.tensor_tensor(yz[i][:], yy[i][:, 0:TB], gate[i][:], ALU.mult).then_inc(yz_ready[i], 1)

                        def residual(core, it, kind, o):
                            w = wait_made(dve, core, "out", it, kind)
                            dve.wait_ge(x3_stored, 16 * o)
                            dve.wait_ge(xr_loaded, 16 * o + 16)
                            v.tensor_tensor(win(x3s), seqs(w), win(xr), ALU.add).then_inc(read(core, "out", it, kind), 1)

                        def final_norm(core, it, kind, o):
                            dve.wait_ge(rstd2_ready, o + 1)
                            wait_moved(dve, core, "xc2", it, kind)
                            v.tensor_tensor(xl[:], xl[:], sq2[:], ALU.mult).then_inc(xl_ready, 1)

                        def core(i, it, kind):
                            ends = kind == LAST and i == 1
                            finals = kind != FIRST and i == 0
                            n, o, here = 1 - i, it + i, (i, it, kind)
                            for t in range(UNIT):
                                s = UNIT * i + t
                                inputs(t, *here)
                                if not (kind == FIRST and s == 0):
                                    scan(s - 1, it)
                                if t == 4 and i and not ends:
                                    norm(*here, o, True)
                                if t == 5 and not (kind == FIRST and i == 0):
                                    gated(1 - i, it, 8 * it + 4 * i + 8 - 8)
                                if t == 7 and finals:
                                    residual(*here, it - 1)
                                if t == 10 and not ends:
                                    low_parts(n, o, here)
                                    steps(n, o, here)
                                if t == 11 and finals:
                                    final_norm(*here, it - 1)

                        dve.wait_ge(pads_zero, 2)
                        norm(-1, 0, FIRST, 1, False)
                        low_parts(0, 1, (-1, 0, FIRST))
                        steps(0, 1, (-1, 0, FIRST))
                        for i in range(2):
                            core(i, 1, FIRST)
                        with dve.Fori(2, N) as it:
                            for i in range(2):
                                core(i, it, MIDDLE)
                        for i in range(2):
                            core(i, N, LAST)
                        scan(TILES - 1, N)
                        gated(1, N, 8 * N + 8)
                        residual(2, N, LAST, N)
                        final_norm(2, N, LAST, N)

                    @block.tensor
                    def _(pe):
                        mm = nc.tensor.matmul

                        def product(core, name, it, kind):
                            w, c = place(core, name, it, kind)
                            pe.wait_ge(moved[w], c + 1)
                            return ww[w]

                        def strip(core, name, it, kind, weight, src, rows=slice(0, P)):
                            w = product(core, name, it, kind)
                            for lo, hi in banks(TB):
                                last = mm(w[rows, lo:hi], weight, src[:, lo:hi], start=True, stop=True)
                            last.then_inc(made[place(core, name, it, kind)[0]], 1)

                        def windows(core, name, it, kind, weights, shifts):
                            w = product(core, name, it, kind)
                            for lo, hi in banks(TB):
                                for n, (weight, shift) in enumerate(zip(weights, shifts)):
                                    last = mm(w[:, lo:hi], weight, seq[:, lo // ST:hi // ST, shift:shift + ST],
                                              start=(n == 0), stop=(n == len(weights) - 1))
                            last.then_inc(made[place(core, name, it, kind)[0]], 1)

                        def norm_start(core, it, kind, o):
                            pe.wait_ge(x_loaded, 16 * o + 16)
                            strip(core, "xc", it, kind, center[:], xt)

                        def norm_end(core, it, kind, o):
                            pe.wait_ge(sq_ready, o + 1)
                            strip(core, "var", it, kind, average[:], sq)

                        def project(core, it, kind, i, o):
                            pe.wait_ge(seq_ready, o + 1)
                            windows(core, "z", it, kind, [w_z[:, i, :]], [CONV - 1])
                            windows(core, "conv", it, kind, [w_conv[:, i, k, :] for k in range(CONV)], range(CONV))

                        def pre(core, it, kind):
                            wait_moved(pe, core, "conv", it, kind)
                            strip(core, "pre", it, kind, w_dt_full[:], u)

                        def xp(core, it, kind):
                            strip(core, "xp", it, kind, w_bc[:].rearrange("p a n -> p (a n)"), u)

                        def spread_block(core, b, name, it, kind, i, o):
                            if o is not None:
                                pe.wait_ge(reset_ready[i], o + 1)
                            strip(core, f"{name}dt{b}", it, kind, spread[:, b, :], dt)
                            strip(core, f"{name}du{b}", it, kind, spread[:, b, :], dtu)

                        def state_block(core, name, m, it, kind, i, o=None):
                            if o is not None:
                                pe.wait_ge(parts_ready[i], o + 1)
                            strip(core, name, it, kind, rows_bc[:, m, :], parts[i])

                        def skip_start(i, it):
                            pe.wait_ge(yz_ready[i], it)
                            for lo, hi in banks(TB):
                                last = mm(yy[i][:, lo:hi], skip[:], u[:, lo:hi], start=True, stop=False)
                            last.then_inc(skip_ready[i], 1)

                        def fold_row(i, it, row):
                            for b in range(4):
                                s = UNIT * i + 4 * row + b
                                pe.wait_ge(hc_ready[s % RC], used(it, s, RC) + 1)
                            for lo, hi in banks(TB):
                                for b in range(4):
                                    s = UNIT * i + 4 * row + b
                                    last = mm(yy[i][32 * b:32 * b + 32, lo:hi], fold[:], hc[s % RC][:, lo:hi],
                                              start=False, stop=(row == 3))
                            last.then_inc(folded, 1)

                        def out(core, it, kind, o):
                            for i in range(2):
                                pe.wait_ge(yz_ready[i], o + 1)
                            w = product(core, "out", it, kind)
                            for lo, hi in banks(TB):
                                for i in range(2):
                                    last = mm(w[C * i:C * i + C, lo:hi], w_out_t[:], yz[i][:, lo:hi], start=True, stop=True)
                            last.then_inc(made[place(core, "out", it, kind)[0]], 1)

                        def final_norm_start(core, it, kind, o):
                            wait_moved(pe, core, "out", it, kind)
                            strip(core, "xc2", it, kind, center[:], x3s)

                        def final_norm_end(core, it, kind, o):
                            pe.wait_ge(sq2_ready, o + 1)
                            strip(core, "var2", it, kind, average[:], sq2)

                        def final_products(core, it, kind, o):
                            pe.wait_ge(xl_ready, o + 1)
                            strip(core, "lgp", it, kind, w_gate[:], xl, rows=slice(0, 2 * EC))
                            for name, n0, n1 in (("tok0", 0, 4), ("tok1", 4, NCH)):
                                w = product(core, name, it, kind)
                                for n in range(n0, n1):
                                    last = nc.tensor.transpose(w[:, (n - n0) * P:(n - n0 + 1) * P], xl[:, n * P:(n + 1) * P], ident[:])
                                last.then_inc(made[place(core, name, it, kind)[0]], 1)

                        def core(i, it, kind):
                            ends = kind == LAST and i == 1
                            finals = kind != FIRST and i == 0
                            n, o, here = 1 - i, it + i, (i, it, kind)
                            for t in range(UNIT):
                                if t == 0:
                                    skip_start(i, it)
                                    spread_block(i, 3, "", it, kind, i, None)
                                    if i and not ends:
                                        norm_start(*here, o)
                                if t == 1:
                                    state_block(i, "B1", 1, it, kind, i)
                                if t == 2:
                                    state_block(i, "C1", 5, it, kind, i)
                                    if i and not ends:
                                        norm_end(*here, o)
                                if t == 3 and not (kind == FIRST and i == 0):
                                    fold_row(1 - i, it - (1 - i), 3)
                                if t == 5 and not ends:
                                    project(*here, n, o)
                                if t == 6:
                                    state_block(i, "B2", 2, it, kind, i)
                                    state_block(i, "C2", 6, it, kind, i)
                                if t == 6 and finals:
                                    out(*here, it - 1)
                                if t == 7:
                                    fold_row(i, it, 0)
                                if t == 8:
                                    if not ends:
                                        pre(*here)
                                    if finals:
                                        final_norm_start(*here, it - 1)
                                if t == 9:
                                    if finals:
                                        final_norm_end(*here, it - 1)
                                    if not ends:
                                        xp(*here)
                                    state_block(i, "B3", 3, it, kind, i)
                                if t == 10:
                                    state_block(i, "C3", 7, it, kind, i)
                                if t == 11:
                                    fold_row(i, it, 1)
                                if t == 12 and finals:
                                    final_products(*here, it - 1)
                                if t == 13 and not ends:
                                    spread_block(i, 0, "n", it, kind, n, o)
                                if t == 14 and not ends:
                                    spread_block(i, 1, "n", it, kind, n, None)
                                    state_block(i, "nB", 0, it, kind, n, o)
                                if t == 15 and not ends:
                                    spread_block(i, 2, "n", it, kind, n, None)
                                    state_block(i, "nC", 4, it, kind, n)
                                if t == 15:
                                    fold_row(i, it, 2)

                        here = (-1, 0, FIRST)
                        norm_start(*here, 1)
                        norm_end(*here, 1)
                        project(*here, 0, 1)
                        pre(*here)
                        xp(*here)
                        spread_block(-1, 0, "n", 0, FIRST, 0, 1)
                        spread_block(-1, 1, "n", 0, FIRST, 0, None)
                        state_block(-1, "nB", 0, 0, FIRST, 0, 1)
                        spread_block(-1, 2, "n", 0, FIRST, 0, None)
                        state_block(-1, "nC", 4, 0, FIRST, 0)
                        for i in range(2):
                            core(i, 1, FIRST)
                        with pe.Fori(2, N) as it:
                            for i in range(2):
                                core(i, it, MIDDLE)
                        for i in range(2):
                            core(i, N, LAST)
                        fold_row(1, N, 3)
                        out(2, N, LAST, N)
                        final_norm_start(2, N, LAST, N)
                        final_norm_end(2, N, LAST, N)
                        final_products(2, N, LAST, N)

        def phase_c():
            IMG = min(4, B)
            R = IMG * EC
            CK = TB if HW // TB % 2 == 0 else TB // 2
            NK = HW // CK
            with ExitStack() as st:
                def sb(name, shape, dt=F32):
                    return sbuf("c_" + name, shape, dt, st)

                def sem(name, turn=0):
                    return new_sem("c_" + name, turn)

                lt = sb("l", [R, HW])
                gt = sb("g", [R, HW])
                w1 = sb("w1", [C + 1, EC, HID])
                w2 = sb("w2", [P, EC, 2, C])
                w2b = sb("w2b", [1, EC, C])
                ones = sb("ones", [1, IMG])
                top = sb("top", [R, TOPK])
                idx = sb("idx", [R, TOPK], U32)
                idf = sb("idf", [R, TOPK])
                base = sb("base", [R, 1])
                neg = sb("neg", [R, 1])
                tot = sb("tot", [R, 1])
                rec = sb("rec", [R, 1])
                p8 = sb("p8", [R, TOPK])
                rows = sb("rows", [R, TOPK, C])
                pool_t = sb("pooled", [R, C])
                pool_x = sb("pooled_t", [C + 1, R])
                hid = sb("hid", [P, 2 * EC, IMG])
                ot = sb("ot", [C, IMG, EC])
                mix = sb("mix", [R, IMG // 2, P])
                xs = [sb(f"x{i}", [P, CK]) for i in range(2)]
                ys = [sb(f"y{i}", [P, CK]) for i in range(2)]
                pt = psum("c_pt", [P, BANK], F32, st)
                ph = psum("c_ph", [P, BANK], F32, st)
                po = psum("c_po", [P, BANK], F32, st)
                pr = psum("c_pr", [P, BANK], F32, st)
                py = [psum(f"c_py{i}", [P, 2 * BANK], F32, st) for i in range(2)]

                w_loaded, l_loaded, zeroed, top_ready, neg_ready, exp_ready, e8_ready, taken = (
                    sem(n) for n in ("wl", "ll", "zero", "top", "neg", "exp", "e8", "taken"))
                chain, idx_ready, gathered, pooled, tr_ready, px_ready, h_ready, gelu_ready = (
                    sem(n) for n in ("chain", "idx", "gath", "pooled", "tr", "px", "h", "gelu"))
                o_ready, ot_ready, or_ready, mix_ready, g_ready = (sem(n) for n in ("o", "ot", "or", "mix", "gr"))
                x_loaded, stored = ([sem(f"{n}{i}", 16) for i in range(2)] for n in ("xl", "st"))
                y_prod, y_ready = ([sem(f"{n}{i}", 1) for i in range(2)] for n in ("yp", "yr"))
                nc.all_engine_barrier()
                DV = 6 + TOPK

                for tile in range(B // IMG):
                    b0 = tile * IMG
                    half = NK // 2
                    turns = []
                    for kk in range(IMG // 2):
                        turns.append((kk, half))
                    per = (IMG // 2) * half

                    with nc.Block() as block:
                        @block.sync
                        def _(sp):
                            for kk in range(IMG // 2):
                                at = (b0 // 2 + kk) * HW
                                sp.dma_start(lt[2 * EC * kk:2 * EC * (kk + 1), :], logits[:, at:at + HW]).then_inc(l_loaded, 16)
                            if tile == 0:
                                sp.dma_start(w1[:], weight1.rearrange("e d h -> d e h")).then_inc(w_loaded, 16)
                                for n in range(4):
                                    h, q = n // 2, C * (n % 2)
                                    sp.dma_start(w2[q:q + C, :, h, :],
                                                 weight2[:, h * P + q:h * P + q + C, :].rearrange("e h o -> h e o")).then_inc(w_loaded, 16)
                                sp.dma_start(w2b[:], weight2[:, HID:HID + 1, :].rearrange("e a o -> a e o")).then_inc(w_loaded, 16)
                            for kk, n in turns:
                                k = b0 // 2 + kk
                                with sp.Fori(0, n) as j:
                                    for s in range(2):
                                        at = (j * 2 + s) * CK
                                        done = j + (tile * per + kk * half + 1)
                                        sp.wait_ge(y_ready[s], done)
                                        sp.dma_start(xs[s][:], x3[:, bass.ds(at + k * HW, CK)]).then_inc(x_loaded[s], 16)
                                    for s in range(2):
                                        at = (j * 2 + s) * CK
                                        done = j + (tile * per + kk * half + 1)
                                        sp.wait_ge(y_ready[s], done + 1)
                                        sp.dma_start(out_v[k, :, bass.ds(at, CK)], ys[s][:]).then_inc(stored[s], 16)
                            for s in range(2):
                                sp.wait_ge(stored[s], 16 * (per * (tile + 1) + 1))

                        @block.gpsimd
                        def _(pool):
                            pool.wait_ge(idx_ready, tile + 1)
                            for n in range(TOPK):
                                nc.gpsimd.indirect_dma_start(out=rows[:, n, :], out_offset=None, in_=tokens,
                                                             in_offset=bass.IndirectOffsetOnAxis(ap=idx[:, n:n + 1], axis=0)).then_inc(gathered, 16)

                        @block.scalar
                        def _(act):
                            a = nc.scalar.activation
                            act.wait_ge(neg_ready, tile + 1)
                            a(gt[:], lt[:], ACT.Exp, bias=neg[:], accum_out=tot[:]).then_inc(exp_ready, 1)
                            a(p8[:], top[:], ACT.Exp, bias=neg[:]).then_inc(e8_ready, 1)
                            act.wait_ge(h_ready, tile + 1)
                            a(hid[:].rearrange("p e b -> p (e b)"), ph[:, 0:2 * EC * IMG], ACT.Gelu).then_inc(gelu_ready, 1)

                        @block.vector
                        def _(dve):
                            v = nc.vector
                            if tile == 0:
                                for n in range(IMG):
                                    v.memset(base[EC * n:EC * n + EC, :], float((n % 2 * NP + n // 2) * HW)).then_inc(zeroed, 1)
                                v.memset(pool_x[C:C + 1, :], 1.0).then_inc(zeroed, 1)
                                v.memset(ones[:], 1.0).then_inc(zeroed, 1)
                                v.memset(mix[:], 0.0).then_inc(zeroed, 1)
                                dve.wait_ge(zeroed, IMG + 3)
                            dve.wait_ge(l_loaded, 16 * (IMG // 2) * (tile + 1))
                            v.max(top[:], lt[:]).then_inc(top_ready, 1)
                            dve.wait_ge(top_ready, tile + 1)
                            v.tensor_scalar(neg[:], top[:, 0:1], -1.0, None, ALU.mult).then_inc(neg_ready, 1)
                            n = [tile * DV]

                            def link(ins):
                                n[0] += 1
                                ins.then_inc(chain, 1)
                                dve.wait_ge(chain, n[0])

                            link(v.max_index(idx[:], top[:], lt[:]))
                            link(v.tensor_copy(idf[:], idx[:]))
                            link(v.tensor_scalar(idf[:], idf[:], base[:, 0:1], float(b0 // 2 * HW), ALU.add, ALU.add))
                            v.tensor_copy(idx[:], idf[:]).then_inc(idx_ready, 1)
                            dve.wait_ge(exp_ready, tile + 1)
                            link(v.match_replace(lt[:], top[:], lt[:], TAKEN))
                            v.scalar_tensor_tensor(gt[:], lt[:], 0.99 * TAKEN, gt[:], ALU.is_le, ALU.mult).then_inc(g_ready, 1)
                            link(v.reciprocal(rec[:], tot[:]))
                            dve.wait_ge(e8_ready, tile + 1)
                            link(v.tensor_scalar(p8[:], p8[:], rec[:, 0:1], None, ALU.mult))
                            dve.wait_ge(gathered, 16 * TOPK * (tile + 1))
                            link(v.tensor_scalar(pool_t[:], rows[:, 0, :], p8[:, 0:1], None, ALU.mult))
                            for m in range(1, TOPK):
                                link(v.scalar_tensor_tensor(pool_t[:], rows[:, m, :], p8[:, m:m + 1], pool_t[:], ALU.mult, ALU.add))
                            dve.wait_ge(tr_ready, tile + 1)
                            v.tensor_copy(pool_x[0:C, :], pt[0:C, 0:R]).then_inc(px_ready, 1)
                            dve.wait_ge(o_ready, tile + 1)
                            v.tensor_copy(ot[:], po[0:C, 0:R].rearrange("o (e b) -> o b e", b=IMG)).then_inc(ot_ready, 1)
                            dve.wait_ge(or_ready, tile + 1)
                            for b in range(IMG):
                                q = slice(EC * b, EC * b + EC)
                                v.tensor_scalar(mix[q, b // 2, C * (b % 2):C * (b % 2) + C], pr[q, 0:C], rec[q, 0:1], None,
                                                ALU.mult).then_inc(mix_ready, 1)
                            for kk, turn in turns:
                                with dve.Fori(0, turn) as j:
                                    done = j + (tile * per + kk * half + 1)
                                    for s in range(2):
                                        dve.wait_ge(y_prod[s], done + 1)
                                        dve.wait_ge(x_loaded[s], 16 * done + 16)
                                        dve.wait_ge(stored[s], 16 * done)
                                        v.tensor_tensor(ys[s][:], py[s][:, 0:CK], xs[s][:], ALU.add).then_inc(y_ready[s], 1)

                        @block.tensor
                        def _(pe):
                            mm = nc.tensor.matmul
                            pe.wait_ge(chain, DV * (tile + 1))
                            nc.tensor.transpose(pt[0:C, 0:R], pool_t[:], ident[0:R, 0:R]).then_inc(tr_ready, 1)
                            pe.wait_ge(px_ready, tile + 1)
                            pe.wait_ge(w_loaded, 96)
                            by_expert = pool_x[:].rearrange("d (b e) -> d e b", e=EC)
                            for x in range(EC):
                                for h in range(2):
                                    at = (2 * x + h) * IMG
                                    last = mm(ph[:, at:at + IMG], w1[:, x, h * P:(h + 1) * P], by_expert[:, x, :], start=True, stop=True)
                            last.then_inc(h_ready, 1)
                            pe.wait_ge(gelu_ready, tile + 1)
                            for x in range(EC):
                                dst = po[0:C, x * IMG:(x + 1) * IMG]
                                for h in range(2):
                                    mm(dst, w2[:, x, h, :], hid[:, 2 * x + h, :], start=(h == 0), stop=False)
                                last = mm(dst, w2b[:, x, :], ones[:], start=False, stop=True)
                            last.then_inc(o_ready, 1)
                            pe.wait_ge(ot_ready, tile + 1)
                            nc.tensor.transpose(pr[0:R, 0:C], ot[:].rearrange("o b e -> o (b e)"), ident[0:C, 0:C]).then_inc(or_ready, 1)
                            pe.wait_ge(mix_ready, IMG * (tile + 1))
                            pe.wait_ge(g_ready, tile + 1)
                            for kk, turn in turns:
                                with pe.Fori(0, turn) as j:
                                    done = j + (tile * per + kk * half + 1)
                                    for s in range(2):
                                        pe.wait_ge(y_ready[s], done)
                                        for a, b in banks(CK):
                                            last = mm(py[s][:, a:b], mix[:, kk, :], gt[:, bass.ds((j * 2 + s) * CK + a, b - a)],
                                                      start=True, stop=True)
                                        last.then_inc(y_prod[s], 1)

        end_phase()
        phase_a()
        end_phase()
        phase_b()
        end_phase()
        phase_c()


_INS = ['x', 'L0_conv_wq', 'L0_conv_wk', 'L0_conv_wv', 'L0_conv_wo', 'L0_conv_bn_gamma', 'L0_conv_bn_beta',
        'L0_conv_bn_mean', 'L0_conv_bn_var', 'L0_ffn_router_w', 'L0_ffn_router_b', 'L0_ffn_expert_w',
        'L0_ffn_expert_b', 'L1_conv_pos', 'L1_conv_W_in', 'L1_conv_conv_w', 'L1_conv_conv_b', 'L1_conv_W_xproj',
        'L1_conv_W_dt', 'L1_conv_b_dt', 'L1_conv_A_log', 'L1_conv_Dp', 'L1_conv_W_out', 'L1_ffn_gate_w',
        'L1_ffn_gate_b', 'L1_ffn_weight1', 'L1_ffn_weight2']


def kernel(**inputs):
    import numpy as _np
    import concourse.bacc as _bacc
    from concourse.bass_utils import run_bass_kernel_spmd as _run

    arrays = {f"in_{name}": _np.ascontiguousarray(inputs[name]) for name in _INS}
    nc = _bacc.Bacc("TRN2", target_bir_lowering=False, num_devices=1)
    args = [nc.dram_tensor(f"in_{name}", arrays[f"in_{name}"].shape, F32, kind="ExternalInput").ap() for name in _INS]
    b, c, h, w = arrays["in_x"].shape
    out = nc.dram_tensor("out", [b, c, h, w], F32, kind="ExternalOutput").ap()
    x2 = nc.dram_tensor("x2", [2 * c, b // 2 * h * w], F32, kind="Internal").ap()
    x3 = nc.dram_tensor("x3", [2 * c, b // 2 * h * w], F32, kind="Internal").ap()
    logits = nc.dram_tensor("logits", [2 * EC, b // 2 * h * w], F32, kind="Internal").ap()
    tokens = nc.dram_tensor("tokens", [b * h * w, C], F32, kind="Internal").ap()
    program(nc, *args, out, x2, x3, logits, tokens)
    r = _run(nc, [arrays], core_ids=[0])
    return r.results[0]["out"]
```

```python
from contextlib import ExitStack

import concourse.bass as bass
from concourse import mybir

F32 = mybir.dt.float32
BF16 = mybir.dt.bfloat16
U32 = mybir.dt.uint32
ALU = mybir.AluOpType
ACT = mybir.ActivationFunctionType
AX = mybir.AxisListType

P = 128
C = 64
WIN = 7
WT = WIN * WIN
WP = 64
NE = 8
WS = 8
ST = WS * WS
CONV = 4
NS = 16
RK = 4
DI = 128
EC = 32
HID = 256
TOPK = 8
BANK = 512
SLOTS = 2
RESET = 1.0e15
BIG = 1.0e30
UNIT = 16
TILES = 2 * UNIT
RA = 4
RB = 2
RC = 8
SMALL = 21
TAKEN = -3.0e38


def banks(n):
    return [(a, min(a + BANK, n)) for a in range(0, n, BANK)]


def program(nc, x, wq, wk, wv, wo, gamma, beta, mean, var, router_w, router_b, expert_w, expert_b,
            pos, w_in, conv_w, conv_b, w_xproj, w_dt, b_dt, a_log, d_skip, w_out,
            gate_w, gate_b, weight1, weight2, out, x2, x3, logits, tokens):
    B, _, H, W = x.shape
    HW = H * W
    NP = B // 2
    TA = WIN * W
    NWA = W // WIN
    SA = H // WIN
    TB = WS * W
    NWB = W // WS
    SB = H // WS
    NCH = TB // P
    ROWS = WIN
    GB = NE * ROWS * 2

    def pairs(t):
        return t.rearrange("(k i) c h w -> k (i c) (h w)", i=2)

    x_v, out_v = pairs(x), pairs(out)

    with ExitStack() as top:
        def sbuf(name, shape, dt=F32, on=top):
            return on.enter_context(nc.sbuf_tensor(name, shape, dt))

        def psum(name, shape, dt=F32, on=top):
            return on.enter_context(nc.psum_tensor(name, shape, dt))

        phase_sems = []

        def new_sem(name, turn=0):
            handle = nc.alloc_semaphore(name=name)
            phase_sems.append(handle)
            if turn:
                nc.sync.sem_inc(handle, turn)
            return handle

        def end_phase():
            nc.clear_and_free_semaphores(phase_sems)
            phase_sems.clear()
            nc.all_engine_barrier()

        def new_sems(name, n=SLOTS, turn=0):
            return [new_sem(f"{name}{i}", turn) for i in range(n)]

        ident = sbuf("ident", [P, P])
        ident_bf = sbuf("ident_bf", [P, P], BF16)
        center = sbuf("center", [P, P])
        average = sbuf("average", [P, P])
        w_qk = sbuf("w_qk", [P, P])
        w_vo = sbuf("w_vo", [P, P])
        shift = sbuf("shift", [P, P])
        w_router = sbuf("w_router", [P, 2 * NE])
        b_router = sbuf("b_router", [P, NE])
        rank8 = sbuf("rank8", [P, NE])
        w_exp = sbuf("w_exp", [P, NE, P])
        b_exp = sbuf("b_exp", [48, P])
        b_exp3 = sbuf("b_exp3", [48, 3, P], BF16)
        pick = sbuf("pick", [48, NE, P], BF16)
        pos_t = sbuf("pos_t", [P, ST])
        w_z = sbuf("w_z", [P, 2, DI])
        w_conv = sbuf("w_conv", [P, 2, CONV // 2, DI])
        conv_bias = sbuf("conv_bias", [P, 1])
        wx = sbuf("wx", [P, RK + 2 * NS])
        wx4 = sbuf("wx4", [RK, P])
        wdt = sbuf("wdt", [RK, DI])
        w_dt_full = sbuf("w_dt_full", [P, DI])
        dt_bias = sbuf("dt_bias", [P, 1])
        decay = sbuf("decay", [P, 4, 4])
        spread = sbuf("spread", [P, 4, P])
        w_bc = sbuf("w_bc", [P, 4, 2 * NS])
        rows_bc = sbuf("rows_bc", [P, 8, P], BF16)
        fold = sbuf("fold", [P, 32])
        skip = sbuf("skip", [P, P])
        skip_col = sbuf("skip_col", [P, 1])
        w_out_t = sbuf("w_out_t", [P, C])
        w_gate = sbuf("w_gate", [P, 2 * EC])
        b_gate = sbuf("b_gate", [2 * EC, 1])
        eps_bn = sbuf("eps_bn", [P, 1])
        eps_6 = sbuf("eps_6", [P, 1])
        one_col = sbuf("one_col", [P, 1])

        with ExitStack() as st:
            wq2 = sbuf("wq2", [C // 2, 2, C], on=st)
            wv2 = sbuf("wv2", [C // 2, 2, C], on=st)
            wk_t = sbuf("wk_t", [C // 2, C], on=st)
            wo_t = sbuf("wo_t", [C // 2, C], on=st)
            bn_row = sbuf("bn_row", [P, 4, C], on=st)
            inv_row = sbuf("inv_row", [P, C], on=st)
            tmp_row = sbuf("tmp_row", [P, C], on=st)
            rest = sbuf("rest", [48, P], on=st)
            rest2 = sbuf("rest2", [48, P], on=st)
            fold4 = sbuf("fold4", [P, 4, 32], on=st)
            w_in_t = sbuf("w_in_t", [P, 2 * DI], on=st)
            taps = sbuf("taps", [P, DI, CONV], on=st)
            pq = psum("pq", [P, BANK], on=st)
            pv = psum("pv", [P, BANK], on=st)
            pd = psum("pd", [P, BANK], on=st)
            zeroed = new_sem("setup_zeroed")
            loaded = new_sem("setup_loaded")
            masks = new_sem("setup_masks")
            acts = new_sem("setup_acts")
            prods = new_sem("setup_prods")
            dves = new_sem("setup_dves")

            loads = []
            for i in range(2):
                c0 = C * i
                loads += [
                    (wq2[:, i, :], wq), (wv2[:, i, :], wv),
                    (w_router[c0:c0 + C, NE * i:NE * i + NE], router_w),
                    (w_exp[c0:c0 + C, :, c0:c0 + C], expert_w.rearrange("e d c -> d e c")),
                    (pos_t[c0:c0 + C, :], pos.rearrange("a c h w -> (a c) (h w)")),
                    (w_in_t[c0:c0 + C, :], w_in),
                    (w_gate[c0:c0 + C, EC * i:EC * i + EC], gate_w.rearrange("e c -> c e")),
                    (b_gate[EC * i:EC * i + EC, :], gate_b.rearrange("(e a) -> e a", a=1)),
                ]
                for part in range(3):
                    r0 = 16 * part + NE * i
                    loads.append((b_exp[r0:r0 + NE, c0:c0 + C], expert_b))
            for n, v in enumerate((gamma, beta, mean, var)):
                loads.append((bn_row[:, n, :], v.partition_broadcast(P)))
            for n in range(4):
                for b in range(4):
                    loads.append((decay[32 * n:32 * n + 32, b, :],
                                  a_log.rearrange("(b j) (m n) -> b n j m", j=32, n=4)[b, n]))
            loads += [
                (wk_t[:, :], wk), (wo_t[:, :], wo.rearrange("o m -> m o")),
                (b_router[:, :], router_b.partition_broadcast(P)),
                (taps[:, :, :].rearrange("p d k -> p (d k)"), conv_w.rearrange("d k -> (d k)").partition_broadcast(P)),
                (conv_bias[:, :], conv_b.rearrange("(c a) -> c a", a=1)),
                (wx[:, :], w_xproj), (wx4[:, :], w_xproj[:, 0:RK].rearrange("d r -> r d")),
                (wdt[:, :], w_dt), (dt_bias[:, :], b_dt.rearrange("(c a) -> c a", a=1)),
                (skip_col[:, :], d_skip.rearrange("(c a) -> c a", a=1)),
                (w_out_t[:, :], w_out),
            ]

            with nc.Block() as block:
                @block.sync
                def _(sp):
                    sp.wait_ge(zeroed, 8)
                    for dst, src in loads:
                        with nc.allow_non_contiguous_dma(reason="small weights, once"):
                            sp.dma_start(dst, src).then_inc(loaded, 16)
                    sp.wait_ge(loaded, 16 * len(loads))

                @block.gpsimd
                def _(pool):
                    g = nc.gpsimd
                    n = [0]

                    def link(ins):
                        n[0] += 1
                        ins.then_inc(masks, 1)
                        pool.wait_ge(masks, n[0])

                    def mark(t, pattern, base=0):
                        link(g.affine_select(out=t, in_=t, compare_op=ALU.not_equal, fill=1.0, base=base,
                                             pattern=pattern, channel_multiplier=1))

                    for t in (ident, ident_bf, pick, spread, fold4, average, rows_bc):
                        link(g.memset(t[:], 0.0))
                    link(g.memset(average[0:C, 0:C], 1.0 / C))
                    link(g.memset(average[C:P, C:P], 1.0 / C))
                    mark(ident[:], [[-1, P]])
                    mark(ident_bf[:], [[-1, P]])
                    mark(spread[:].rearrange("p b (n j) -> p b n j", j=32), [[-32, 4], [0, 4], [-1, 32]])
                    mark(fold4[:], [[-32, 4], [-1, 32]])
                    for part in range(3):
                        mark(pick[:].rearrange("r e (i c) -> r e i c", i=2), [[-1, NE], [-NE, 2], [0, C]], -16 * part)
                    for part in (0, 2, 3):
                        mark(rows_bc[:].rearrange("r m (n j) -> r m n j", j=32), [[-4, 8], [-1, 4], [0, 32]], -32 * part)
                    link(g.iota(rank8[:], pattern=[[-1, NE]], base=NE, channel_multiplier=0,
                                allow_small_or_imprecise_dtypes=True))

                @block.scalar
                def _(act):
                    act.wait_ge(zeroed, 11)
                    act.wait_ge(loaded, 16 * len(loads))
                    nc.scalar.activation(inv_row[:], bn_row[:, 3, :], ACT.Ln, bias=eps_bn[:]).then_inc(acts, 1)
                    act.wait_ge(acts, 1)
                    nc.scalar.activation(inv_row[:], inv_row[:], ACT.Exp, scale=-0.5).then_inc(acts, 1)
                    nc.scalar.activation(decay[:], decay[:], ACT.Exp).then_inc(acts, 1)

                @block.tensor
                def _(pe):
                    pe.wait_ge(loaded, 16 * len(loads))
                    nc.tensor.matmul(pq[:, 0:C], wq2[:].rearrange("m i c -> m (i c)"), wk_t[:],
                                     start=True, stop=True).then_inc(prods, 1)
                    nc.tensor.matmul(pv[:, 0:C], wv2[:].rearrange("m i c -> m (i c)"), wo_t[:],
                                     start=True, stop=True).then_inc(prods, 1)
                    nc.tensor.matmul(pd[:, 0:DI], wx4[:], wdt[:], start=True, stop=True).then_inc(prods, 1)

                @block.vector
                def _(dve):
                    v = nc.vector
                    for t in (w_router, w_exp, b_exp, w_gate, w_qk, w_vo, w_z, w_conv):
                        v.memset(t[:], 0.0).then_inc(zeroed, 1)
                    v.memset(eps_bn[:], 1e-5).then_inc(zeroed, 1)
                    v.memset(eps_6[:], 1e-6).then_inc(zeroed, 1)
                    v.memset(one_col[:], 1.0).then_inc(zeroed, 1)
                    dve.wait_ge(zeroed, 11)
                    dve.wait_ge(masks, 20)
                    dve.wait_ge(acts, 3)
                    dve.wait_ge(prods, 3)
                    n = [0]

                    def link(ins):
                        n[0] += 1
                        ins.then_inc(dves, 1)
                        dve.wait_ge(dves, n[0])

                    link(v.tensor_tensor(center[:], ident[:], average[:], ALU.subtract))
                    link(v.tensor_tensor(inv_row[:], inv_row[:], bn_row[:, 0, :], ALU.mult))
                    link(v.tensor_tensor(tmp_row[:], inv_row[:], bn_row[:, 2, :], ALU.mult))
                    for c0 in (0, C):
                        link(v.tensor_tensor(shift[:, c0:c0 + C], bn_row[:, 1, :], tmp_row[:], ALU.subtract))
                    for c0 in (0, C):
                        s = slice(c0, c0 + C)
                        link(v.tensor_scalar(w_qk[s, s], pq[s, 0:C], float(C // 2) ** -0.5, None, ALU.mult))
                        link(v.tensor_tensor(w_vo[s, s], pv[s, 0:C], inv_row[s, :], ALU.mult))
                    link(v.tensor_copy(b_exp3[:, 0, :], b_exp[:]))
                    link(v.tensor_tensor(rest[:], b_exp[:], b_exp3[:, 0, :], ALU.subtract))
                    link(v.tensor_copy(b_exp3[:, 1, :], rest[:]))
                    link(v.tensor_tensor(rest2[:], rest[:], b_exp3[:, 1, :], ALU.subtract))
                    link(v.tensor_copy(b_exp3[:, 2, :], rest2[:]))
                    for i in range(2):
                        q = slice(C * i, C * i + C)
                        link(v.tensor_copy(w_z[q, i, :], w_in_t[q, DI:2 * DI]))
                        for k in range(CONV):
                            q = slice(C * ((i + k // 2) % 2), C * ((i + k // 2) % 2) + C)
                            link(v.tensor_tensor(w_conv[q, i, k % 2, :], w_in_t[q, 0:DI], taps[q, :, k], ALU.mult))
                    link(v.tensor_copy(w_dt_full[:], pd[:, 0:DI]))
                    link(v.tensor_scalar(decay[:], decay[:], -1.0, -1e-12, ALU.mult, ALU.min))
                    for part in range(4):
                        link(v.tensor_copy(w_bc[:, part, :], wx[:, RK:RK + 2 * NS]))
                    link(v.tensor_reduce(fold[:], fold4[:].rearrange("p n j -> p j n"), AX.X, ALU.add))
                    link(v.tensor_scalar(skip[:], ident[:], skip_col[:, 0:1], None, ALU.mult))


        def phase_a():
            HALF = SA // SLOTS
            with ExitStack() as st:
                def sb(name, shape, dt=F32):
                    return [sbuf(f"{name}{i}", shape, dt, st) for i in range(SLOTS)]

                xt = sb("a_x", [P, TA])
                sq = sb("a_sq", [P, TA])
                xw = sb("a_xw", [P, NWA, WP])
                ts = sb("a_t", [P, NWA, WP])
                pr = sb("a_p", [P, NWA, WP])
                pt = sb("a_pt", [P, NWA // 2, P])
                vw = sb("a_vw", [P, NWA // 2, P])
                mx = sb("a_mx", [P, NWA])
                sm = sb("a_sm", [P, NWA])
                x1 = sb("a_x1", [P, TA])
                xn = sb("a_xn", [P, TA])
                xg = [sbuf(f"a_xg{i}", [P, TA], F32, st) for i in range(2 * SLOTS)]
                res = sb("a_res", [P, TA])
                lg = sb("a_lg", [W, 2 * WIN, NE])
                ex = sb("a_ex", [W, 2 * WIN, NE])
                cd = sb("a_cd", [W, 2 * WIN, NE])
                o1 = sb("a_o1", [W, 2 * WIN, NE])
                o2 = sb("a_o2", [W, 2 * WIN, NE])
                g1 = sb("a_g1", [W, 2 * WIN])
                g3 = sb("a_g3", [W, WIN, 48], BF16)
                gt = sb("a_gt", [48, TA], BF16)
                pa = [psum(f"a_pa{i}", [P, 2 * BANK], F32, st) for i in range(SLOTS)]
                pb = [psum(f"a_pb{i}", [P, 2 * BANK], F32, st) for i in range(SLOTS)]

                def sems(name, turn=1):
                    return new_sems("a_" + name, SLOTS, turn)

                pads_zero = new_sem("a_pads")
                x_loaded, stored = sems("loaded", 16), sems("stored", 16)
                xc_ready, sq_ready, var_ready, ln_ready, rstd_ready = (sems(n) for n in ("xc", "sq", "var", "ln", "rstd"))
                xw_ready = sems("xw", 2)
                t_ready, ts_ready, score_ready, max_ready, sub_ready, exp_ready, sum_ready, rec_ready, prob_ready = (
                    sems(n) for n in ("t", "ts", "score", "max", "sub", "exp", "sum", "rec", "prob"))
                tr_ready, pt_ready, v_ready, vw_ready, o_ready, x1_ready = (
                    sems(n) for n in ("tr", "pt", "v", "vw", "o", "x1"))
                xc2_ready, sq2_ready, var2_ready, ln2_ready, rstd2_ready, xn_ready = (
                    sems(n) for n in ("xc2_", "sq2_", "var2_", "ln2_", "rstd2_", "xn"))
                rout_ready, expl_ready, gtr_ready, gt_ready = (sems(n) for n in ("rout", "expl", "gtr", "gt"))
                small = sems("small", SMALL)
                gate_ready, xg_ready, moe_ready = (sems(n, NE) for n in ("gate", "xg", "moe"))
                acc_ready, res_ready = sems("acc"), sems("res")
                nc.all_engine_barrier()

                def win(t):
                    return t[:].rearrange("p (r w c) -> p r w c", r=WIN, c=WIN)

                def by_win(t):
                    return t[:, :, 0:WT].rearrange("p w (r c) -> p r w c", r=WIN)

                with nc.Block() as block:
                    @block.sync
                    def _(sp):
                        for k in range(NP):
                            with sp.Fori(0, HALF) as j:
                                it = j + (k * HALF + 1)
                                for s in range(SLOTS):
                                    at = (j * SLOTS + s) * TA
                                    sp.wait_ge(x1_ready[s], it)
                                    sp.dma_start(xt[s][:], x_v[k, :, bass.ds(at, TA)]).then_inc(x_loaded[s], 16)
                                for s in range(SLOTS):
                                    at = (j * SLOTS + s) * TA
                                    sp.wait_ge(res_ready[s], it + 1)
                                    sp.dma_start(x2[:, bass.ds(at + k * HW, TA)], res[s][:]).then_inc(stored[s], 16)
                        for s in range(SLOTS):
                            sp.wait_ge(stored[s], 16 * (NP * HALF + 1))

                    @block.gpsimd
                    def _(pool):
                        for s in range(SLOTS):
                            nc.gpsimd.memset(xw[s][:], 0.0).then_inc(pads_zero, 1)
                            nc.gpsimd.memset(pr[s][:], 0.0).then_inc(pads_zero, 1)

                    @block.scalar
                    def _(act):
                        a = nc.scalar.activation
                        nc.scalar.preload_act_table_set("natural_log_exp_and_others")
                        act.wait_ge(pads_zero, 2 * SLOTS)
                        with act.Fori(1, NP * HALF + 1) as it:
                            for s in range(SLOTS):
                                act.wait_ge(xc_ready[s], it + 1)
                                a(sq[s][:], pa[s][:, 0:TA], ACT.Square).then_inc(sq_ready[s], 1)
                            for s in range(SLOTS):
                                act.wait_ge(var_ready[s], it + 1)
                                a(sq[s][:], pb[s][:, 0:TA], ACT.Ln, bias=eps_6[:]).then_inc(ln_ready[s], 1)
                            for s in range(SLOTS):
                                act.wait_ge(ln_ready[s], it + 1)
                                a(sq[s][:], sq[s][:], ACT.Exp, scale=-0.5).then_inc(rstd_ready[s], 1)
                            for s in range(SLOTS):
                                act.wait_ge(t_ready[s], it + 1)
                                a(ts[s][:].rearrange("p w t -> p (w t)"), pb[s][:, 0:NWA * WP], ACT.Copy).then_inc(ts_ready[s], 1)
                            for s in range(SLOTS):
                                act.wait_ge(sub_ready[s], it + 1)
                                a(pr[s][:, :, 0:WT], pr[s][:, :, 0:WT], ACT.Exp).then_inc(exp_ready[s], 1)
                            for s in range(SLOTS):
                                act.wait_ge(tr_ready[s], it + 1)
                                a(pt[s][:].rearrange("p w t -> p (w t)"), pb[s][:, 0:NWA * WP], ACT.Copy).then_inc(pt_ready[s], 1)
                            for s in range(SLOTS):
                                act.wait_ge(xc2_ready[s], it + 1)
                                a(sq[s][:], pa[s][:, 0:TA], ACT.Square).then_inc(sq2_ready[s], 1)
                            for s in range(SLOTS):
                                act.wait_ge(var2_ready[s], it + 1)
                                a(sq[s][:], pb[s][:, 0:TA], ACT.Ln, bias=eps_bn[:]).then_inc(ln2_ready[s], 1)
                            for s in range(SLOTS):
                                act.wait_ge(ln2_ready[s], it + 1)
                                a(sq[s][:], sq[s][:], ACT.Exp, scale=-0.5).then_inc(rstd2_ready[s], 1)
                            for s in range(SLOTS):
                                act.wait_ge(small[s], SMALL * it + 3)
                                a(ex[s][:], lg[s][:], ACT.Exp).then_inc(expl_ready[s], 1)
                            for s in range(SLOTS):
                                act.wait_ge(gtr_ready[s], it + 1)
                                a(gt[s][:].rearrange("g (r w) -> g r w", r=WIN),
                                  pb[s][0:48, 0:WIN * P].rearrange("g (r w) -> g r w", r=WIN)[:, :, 0:W], ACT.Copy).then_inc(gt_ready[s], 1)

                    @block.vector
                    def _(dve):
                        v = nc.vector
                        dve.wait_ge(pads_zero, 2 * SLOTS)
                        with dve.Fori(1, NP * HALF + 1) as it:
                            for s in range(SLOTS):
                                dve.wait_ge(rstd_ready[s], it + 1)
                                for side in range(2):
                                    ws = slice(side * (NWA // 2), (side + 1) * (NWA // 2))
                                    v.tensor_tensor(by_win(xw[s][:, side::2, :]), win(pa[s][:, 0:TA])[:, :, ws], win(sq[s])[:, :, ws],
                                                    ALU.mult).then_inc(xw_ready[s], 1)
                            for s in range(SLOTS):
                                score = pa[s][:].rearrange("p (w t) -> p w t", t=WP)[:, :, 0:WT]
                                dve.wait_ge(score_ready[s], it + 1)
                                v.tensor_reduce(mx[s][:], score, AX.X, ALU.max).then_inc(max_ready[s], 1)
                            for s in range(SLOTS):
                                score = pa[s][:].rearrange("p (w t) -> p w t", t=WP)[:, :, 0:WT]
                                dve.wait_ge(max_ready[s], it + 1)
                                v.tensor_tensor(pr[s][:, :, 0:WT], score, mx[s][:].unsqueeze(2).broadcast_to([P, NWA, WT]),
                                                ALU.subtract).then_inc(sub_ready[s], 1)
                            for s in range(SLOTS):
                                dve.wait_ge(v_ready[s], it + 1)
                                v.tensor_tensor(vw[s][:], pa[s][:, 0:NWA * WP].rearrange("p (w t) -> p w t", t=P),
                                                shift[:].unsqueeze(1).broadcast_to([P, NWA // 2, P]), ALU.add).then_inc(vw_ready[s], 1)
                            for s in range(SLOTS):
                                dve.wait_ge(exp_ready[s], it + 1)
                                v.tensor_reduce(sm[s][:], pr[s][:, :, 0:WT], AX.X, ALU.add).then_inc(sum_ready[s], 1)
                            for s in range(SLOTS):
                                dve.wait_ge(sum_ready[s], it + 1)
                                v.reciprocal(mx[s][:], sm[s][:]).then_inc(rec_ready[s], 1)
                            for s in range(SLOTS):
                                dve.wait_ge(rec_ready[s], it + 1)
                                v.tensor_tensor(pr[s][:, :, 0:WT], pr[s][:, :, 0:WT],
                                                mx[s][:].unsqueeze(2).broadcast_to([P, NWA, WT]), ALU.mult).then_inc(prob_ready[s], 1)
                            for s in range(SLOTS):
                                o = pb[s][:].rearrange("p (w t) -> p w t", t=WP)
                                dve.wait_ge(o_ready[s], it + 1)
                                v.tensor_tensor(win(x1[s]), by_win(o), win(xt[s]), ALU.add).then_inc(x1_ready[s], 1)
                            for s in range(SLOTS):
                                dve.wait_ge(rstd2_ready[s], it + 1)
                                v.tensor_tensor(xn[s][:], pa[s][:, 0:TA], sq[s][:], ALU.mult).then_inc(xn_ready[s], 1)

                            shape = [W, 2 * WIN, NE]
                            rank = rank8[0:W, :].unsqueeze(1).broadcast_to(shape)
                            bias = b_router[0:W, :].unsqueeze(1).broadcast_to(shape)

                            def wide(s):
                                return g1[s][:].unsqueeze(2).broadcast_to(shape)

                            def part(s, n):
                                return g3[s][:, :, 16 * n:16 * n + 16]

                            def rows(t):
                                return t[:].rearrange("p (r i) e -> p r (i e)", i=2)

                            def chain(s, n):
                                dve.wait_ge(small[s], SMALL * it + n)

                            for s in range(SLOTS):
                                dve.wait_ge(rout_ready[s], it + 1)
                                v.tensor_tensor(lg[s][:], pa[s][0:W, 0:2 * WIN * NE].rearrange("p (r e) -> p r e", e=NE), bias,
                                                ALU.add).then_inc(small[s], 1)
                            for s in range(SLOTS):
                                chain(s, 1)
                                v.tensor_reduce(g1[s][:], lg[s][:], AX.X, ALU.max).then_inc(small[s], 1)
                            for s in range(SLOTS):
                                chain(s, 2)
                                v.tensor_tensor(lg[s][:], lg[s][:], wide(s), ALU.subtract).then_inc(small[s], 1)
                            for s in range(SLOTS):
                                chain(s, 3)
                                v.scalar_tensor_tensor(cd[s][:], lg[s][:], 0.0, rank, ALU.is_ge, ALU.mult).then_inc(small[s], 1)
                            for s in range(SLOTS):
                                chain(s, 4)
                                v.tensor_reduce(g1[s][:], cd[s][:], AX.X, ALU.max).then_inc(small[s], 1)
                            for s in range(SLOTS):
                                chain(s, 5)
                                v.tensor_tensor(o1[s][:], cd[s][:], wide(s), ALU.is_equal).then_inc(small[s], 1)
                            for s in range(SLOTS):
                                dve.wait_ge(expl_ready[s], it + 1)
                                chain(s, 6)
                                v.scalar_tensor_tensor(lg[s][:], o1[s][:], -BIG, lg[s][:], ALU.mult, ALU.add).then_inc(small[s], 1)
                            for s in range(SLOTS):
                                chain(s, 7)
                                v.tensor_reduce(g1[s][:], lg[s][:], AX.X, ALU.max).then_inc(small[s], 1)
                            for s in range(SLOTS):
                                chain(s, 8)
                                v.tensor_tensor(cd[s][:], lg[s][:], wide(s), ALU.is_ge).then_inc(small[s], 1)
                            for s in range(SLOTS):
                                chain(s, 9)
                                v.tensor_tensor(cd[s][:], cd[s][:], rank, ALU.mult).then_inc(small[s], 1)
                            for s in range(SLOTS):
                                chain(s, 10)
                                v.tensor_reduce(g1[s][:], cd[s][:], AX.X, ALU.max).then_inc(small[s], 1)
                            for s in range(SLOTS):
                                chain(s, 11)
                                v.tensor_tensor(o2[s][:], cd[s][:], wide(s), ALU.is_equal).then_inc(small[s], 1)
                            for s in range(SLOTS):
                                chain(s, 12)
                                v.tensor_tensor(o1[s][:], o1[s][:], o2[s][:], ALU.add).then_inc(small[s], 1)
                            for s in range(SLOTS):
                                chain(s, 13)
                                v.tensor_tensor(o1[s][:], o1[s][:], ex[s][:], ALU.mult).then_inc(small[s], 1)
                            for s in range(SLOTS):
                                chain(s, 14)
                                v.tensor_reduce(g1[s][:], o1[s][:], AX.X, ALU.add).then_inc(small[s], 1)
                            for s in range(SLOTS):
                                chain(s, 15)
                                v.reciprocal(g1[s][:], g1[s][:]).then_inc(small[s], 1)
                            for s in range(SLOTS):
                                chain(s, 16)
                                v.tensor_tensor(o1[s][:], o1[s][:], wide(s), ALU.mult).then_inc(small[s], 1)
                            for s in range(SLOTS):
                                chain(s, 17)
                                v.tensor_copy(part(s, 0), rows(o1[s])).then_inc(small[s], 1)
                            for s in range(SLOTS):
                                chain(s, 18)
                                v.tensor_tensor(rows(cd[s]), rows(o1[s]), part(s, 0), ALU.subtract).then_inc(small[s], 1)
                            for s in range(SLOTS):
                                chain(s, 19)
                                v.tensor_copy(part(s, 1), rows(cd[s])).then_inc(small[s], 1)
                            for s in range(SLOTS):
                                chain(s, 20)
                                v.tensor_tensor(part(s, 2), rows(cd[s]), part(s, 1), ALU.subtract).then_inc(small[s], 1)
                            for x in range(NE):
                                for s in range(SLOTS):
                                    dve.wait_ge(gate_ready[s], NE * it + x + 1)
                                    if x >= 2:
                                        dve.wait_ge(moe_ready[s], NE * it + x - 1)
                                    v.tensor_tensor(xg[2 * s + x % 2][:], xn[s][:], pb[s][:, 0:TA], ALU.mult).then_inc(xg_ready[s], 1)
                            for s in range(SLOTS):
                                dve.wait_ge(acc_ready[s], it + 1)
                                dve.wait_ge(stored[s], 16 * it)
                                v.tensor_tensor(res[s][:], pa[s][:, 0:TA], x1[s][:], ALU.add).then_inc(res_ready[s], 1)

                    @block.tensor
                    def _(pe):
                        mm = nc.tensor.matmul
                        pe.wait_ge(pads_zero, 2 * SLOTS)

                        def strip(dst, weight, src):
                            for a, b in banks(TA):
                                last = mm(dst[:, a:b], weight, src[:, a:b], start=True, stop=True)
                            return last

                        with pe.Fori(1, NP * HALF + 1) as it:
                            for s in range(SLOTS):
                                pe.wait_ge(x_loaded[s], 16 * it + 16)
                                pe.wait_ge(res_ready[s], it)
                                strip(pa[s], center[:], xt[s]).then_inc(xc_ready[s], 1)
                            for s in range(SLOTS):
                                pe.wait_ge(sq_ready[s], it + 1)
                                strip(pb[s], average[:], sq[s]).then_inc(var_ready[s], 1)
                            for s in range(SLOTS):
                                pe.wait_ge(xw_ready[s], 2 * it + 2)
                                for a, b in banks(NWA * WP):
                                    last = mm(pb[s][:, a:b], w_qk[:], xw[s][:].rearrange("p w t -> p (w t)")[:, a:b],
                                              start=True, stop=True)
                                last.then_inc(t_ready[s], 1)
                            for s in range(SLOTS):
                                pe.wait_ge(pads_zero, 2 * SLOTS)
                                pe.wait_ge(ts_ready[s], it + 1)
                                for w in range(NWA):
                                    for i in range(2):
                                        r = slice(C * i, C * i + C)
                                        last = mm(pa[s][r, w * WP:w * WP + WT], ts[s][r, w, :], xw[s][r, w, 0:WT],
                                                  start=True, stop=True)
                                last.then_inc(score_ready[s], 1)
                            for s in range(SLOTS):
                                pe.wait_ge(sub_ready[s], it + 1)
                                for w in range(NWA // 2):
                                    last = mm(pa[s][:, w * P:(w + 1) * P], xw[s][:, 2 * w:2 * w + 2, :].rearrange("p w t -> p (w t)"),
                                              w_vo[:], start=True, stop=True)
                                last.then_inc(v_ready[s], 1)
                            for s in range(SLOTS):
                                pe.wait_ge(prob_ready[s], it + 1)
                                for w in range(NWA // 2):
                                    last = nc.tensor.transpose(pb[s][:, w * P:(w + 1) * P],
                                                               pr[s][:, 2 * w:2 * w + 2, :].rearrange("p w t -> p (w t)"), ident[:])
                                last.then_inc(tr_ready[s], 1)
                            for s in range(SLOTS):
                                pe.wait_ge(pads_zero, 2 * SLOTS)
                                pe.wait_ge(pt_ready[s], it + 1)
                                pe.wait_ge(vw_ready[s], it + 1)
                                for w in range(NWA):
                                    side, q = w // (NWA // 2), w % (NWA // 2)
                                    h = slice(WP * side, WP * side + WP)
                                    for i in range(2):
                                        last = mm(pb[s][C * i:C * i + C, w * WP:w * WP + WT], vw[s][h, q, C * i:C * i + C],
                                                  pt[s][h, q, WP * i:WP * i + WT], start=True, stop=True)
                                last.then_inc(o_ready[s], 1)
                            for s in range(SLOTS):
                                pe.wait_ge(x1_ready[s], it + 1)
                                strip(pa[s], center[:], x1[s]).then_inc(xc2_ready[s], 1)
                            for s in range(SLOTS):
                                pe.wait_ge(sq2_ready[s], it + 1)
                                strip(pb[s], average[:], sq[s]).then_inc(var2_ready[s], 1)
                            for s in range(SLOTS):
                                pe.wait_ge(xn_ready[s], it + 1)
                                for r in range(WIN):
                                    last = mm(pa[s][0:W, r * 2 * NE:(r + 1) * 2 * NE], xn[s][:, r * W:(r + 1) * W], w_router[:],
                                              start=True, stop=True)
                                last.then_inc(rout_ready[s], 1)
                            for s in range(SLOTS):
                                pe.wait_ge(small[s], SMALL * it + SMALL)
                                for r in range(WIN):
                                    last = mm(pb[s][0:48, r * P:r * P + W], g3[s][:, r, :], ident_bf[0:W, 0:W],
                                              start=True, stop=True)
                                last.then_inc(gtr_ready[s], 1)

                            def spread_gate(s, x):
                                for a, b in banks(TA):
                                    last = mm(pb[s][:, a:b], pick[:, x, :], gt[s][:, a:b], start=True, stop=True)
                                last.then_inc(gate_ready[s], 1)

                            for s in range(SLOTS):
                                pe.wait_ge(gt_ready[s], it + 1)
                                spread_gate(s, 0)
                            for x in range(NE):
                                for s in range(SLOTS):
                                    pe.wait_ge(xg_ready[s], NE * it + x + 1)
                                    if x < NE - 1:
                                        spread_gate(s, x + 1)
                                    for a, b in banks(TA):
                                        last = mm(pa[s][:, a:b], w_exp[:, x, :], xg[2 * s + x % 2][:, a:b],
                                                  start=(x == 0), stop=False)
                                    last.then_inc(moe_ready[s], 1)
                            for s in range(SLOTS):
                                for n in range(3):
                                    for a, b in banks(TA):
                                        last = mm(pa[s][:, a:b], b_exp3[:, n, :], gt[s][:, a:b], start=False, stop=(n == 2))
                                last.then_inc(acc_ready[s], 1)

        def phase_b():
            N = NP * SB

            final = ("out", "xc2", "var2", "lgp", "tok0", "tok1")
            ahead = ("xc", "var", "conv0", "conv1", "z0", "z1", "pre0", "pre1", "xp0", "xp1",
                     "ndt0", "ndu0", "nB", "ndt1", "ndu1", "ndt2", "ndu2", "nC")
            core0 = ("dt3", "du3", "B1", "C1", "B2", "C2", "out", "xc", "xc2", "var", "var2", "B3", "C3",
                     "lgp", "tok0", "tok1", "ndt0", "ndu0", "nB", "ndt1", "ndu1", "ndt2", "ndu2", "nC")
            core1 = ("dt3", "du3", "B1", "C1", "conv0", "conv1", "z0", "z1", "B2", "C2", "pre0", "pre1", "B3", "C3",
                     "xp0", "xp1", "ndt0", "ndu0", "nB", "ndt1", "ndu1", "ndt2", "ndu2", "nC")
            whole = [(0, n) for n in core0] + [(1, n) for n in core1]
            first_turn = [(0, n) for n in core0 if n not in final]
            last_turn = ([(0, n) for n in core0 if n not in ("xc", "var")] +
                         [(1, n) for n in core1 if n not in ahead] + [(2, n) for n in final])
            TURN = len(whole)
            NW = 3
            SL = NWB * (CONV - 1 + ST)
            assert TURN % NW == 0 and N >= 3
            MIDDLE, FIRST, LAST = "middle", "first", "last"

            def place(core, name, it, kind):
                if core == -1:
                    c = ahead.index(name)
                elif core == 0 and kind == FIRST:
                    c = len(ahead) + first_turn.index((0, name))
                elif kind == LAST:
                    c = len(ahead) - len(final) + TURN * (N - 1) + last_turn.index((core, name))
                else:
                    c = len(ahead) - len(final) - TURN + whole.index((core, name))
                    return c % NW, it * (TURN // NW) + c // NW
                return c % NW, c // NW

            with ExitStack() as st:
                def sb(name, shape, dt=F32):
                    return sbuf("b_" + name, shape, dt, st)

                def ring(name, n):
                    return [sb(f"{name}{i}", [P, TB]) for i in range(n)]

                def sem(name, turn=1):
                    return new_sem("b_" + name, turn)

                def sems(name, n=2, turn=1):
                    return [sem(f"{name}{i}", turn) for i in range(n)]

                xt = sb("x", [P, TB])
                xr = sb("xr", [P, TB])
                sq = sb("sq", [P, TB])
                xc = sb("xc", [P, TB])
                seq = [sb(f"seq{i}", [P, NWB, CONV - 1 + ST]) for i in range(2)]
                resets = sb("resets", [P, NWB])
                x3s = sb("x3s", [P, TB])
                sq2 = sb("sq2", [P, TB])
                xl = sb("xl", [P, TB])
                lg = sb("lg", [2 * EC, TB])
                tok = sb("tok", [P, TB])
                gate = ring("gate", 2)
                gate_next = sb("gate_next", [P, TB])
                yz = ring("yz", 2)
                u = ring("u", 2)
                dt = ring("dt", 2)
                dtu = ring("dtu", 2)
                rest = sq
                parts = [sb(f"parts{i}", [P, TB], BF16) for i in range(2)]
                dts = ring("dts", 4)
                dus = ring("dus", 4)
                bt = ring("bt", 2)
                ct = ring("ct", 2)
                aa = ring("a", RA)
                bb = ring("b", RB)
                hh = ring("h", RA)
                hc = ring("hc", RC)
                ww = [psum(f"b_w{i}", [P, 2 * BANK], F32, st) for i in range(NW)]
                yy = psum("b_y", [P, 2 * BANK], F32, st)

                pads_zero = sem("pads", 0)
                x_loaded, xr_loaded, x3_stored, lg_stored = (sem(n, 16) for n in ("loaded", "xrl", "x3st", "lgst"))
                tok_stored = sem("tokst", 32)
                shifted = sem("shifted", 32)
                made = sems("made", NW)
                moved = sems("moved", NW)
                sq_ready, rstd_ready, xn_ready = (sem(n) for n in ("sq", "rstd", "xn"))
                seq_ready = sems("seq")
                abs_ready, e_ready, l_ready, dt_ready, dtu_ready, reset_ready = (
                    sems(n) for n in ("abs", "e", "l", "dt", "dtu", "reset"))
                high_ready, mid_ready, parts_ready, skip_ready, yz_ready = (
                    sems(n) for n in ("high", "mid", "parts", "skip", "yz"))
                a_ready, h_ready = (sems(n, RA, TILES // RA) for n in ("a", "h"))
                b_ready = sems("b", RB, TILES // RB)
                hc_ready = sems("hc", RC, TILES // RC)
                gate1_ready = sem("gate1")
                folded = sem("fold", 8)
                sq2_ready, rstd2_ready, xl_ready = (sem(n) for n in ("sq2", "rstd2", "xl"))
                nc.all_engine_barrier()

                def win(t):
                    return t[:, 0:TB].rearrange("p (r w c) -> p r w c", r=WS, c=WS)

                def seqs(t):
                    return t[:, 0:TB].rearrange("p (w r c) -> p r w c", r=WS, c=WS)

                tokens_v = tokens.rearrange("(i r p) c -> i p r c", i=2, p=P)

                def used(it, s, n):
                    return it * (TILES // n) + s // n

                def wait_made(eng, core, name, it, kind):
                    w, c = place(core, name, it, kind)
                    eng.wait_ge(made[w], c + 2)
                    return ww[w]

                def wait_moved(eng, core, name, it, kind):
                    w, c = place(core, name, it, kind)
                    eng.wait_ge(moved[w], c + 2)

                def read(core, name, it, kind):
                    return moved[place(core, name, it, kind)[0]]

                def before(i, it, kind):
                    if i:
                        return 0, it, kind
                    return (-1, it, kind) if kind == FIRST else (1, it - 1, MIDDLE)

                def wait_spread(eng, name, t, i, it, kind):
                    if t < 3:
                        wait_moved(eng, before(i, it, kind)[0], f"n{name}{t}", *before(i, it, kind)[1:])
                    elif t == 3:
                        wait_moved(eng, i, f"{name}3", it, kind)

                def wait_block(eng, name, t, i, it, kind):
                    if t == 0:
                        wait_moved(eng, before(i, it, kind)[0], f"n{name}", *before(i, it, kind)[1:])
                    elif t % 4 == 0:
                        wait_moved(eng, i, f"{name}{t // 4}", it, kind)

                with nc.Block() as block:
                    @block.sync
                    def _(sp):
                        def turn(it, kind):
                            p = it - 1
                            if kind != LAST:
                                sp.wait_ge(sq_ready, it + 1)
                                sp.dma_start(xt[:], x2[:, bass.ds((p + 1) * TB, TB)]).then_inc(x_loaded, 16)
                            if kind != FIRST:
                                store(0, it, kind)
                            if kind != LAST:
                                shift_seq(it + 1)
                            if kind != FIRST:
                                store_rest(0, it, kind)
                            sp.dma_start(xr[:], x2[:, bass.ds(p * TB, TB)]).then_inc(xr_loaded, 16)

                        def shift_seq(o):
                            sp.wait_ge(seq_ready[0], o + 1)
                            sp.wait_ge(seq_ready[1], o + 1)
                            for i in range(2):
                                flat = seq[i][:].rearrange("p w t -> p (w t)")
                                sp.dma_start(flat[C * (1 - i):C * (1 - i) + C, 0:SL - 2],
                                             flat[C * i:C * i + C, 2:SL]).then_inc(shifted, 16)

                        def store(core, it, kind):
                            p = it - 2
                            wait_moved(sp, core, "out", it - (core == 2), kind)
                            sp.dma_start(x3[:, bass.ds(p * TB, TB)], x3s[:]).then_inc(x3_stored, 16)

                        def store_rest(core, it, kind):
                            p = it - 2
                            wait_moved(sp, core, "lgp", it - (core == 2), kind)
                            sp.dma_start(logits[:, bass.ds(p * TB, TB)], lg[:]).then_inc(lg_stored, 16)
                            wait_moved(sp, core, "tok1", it - (core == 2), kind)
                            for i in range(2):
                                sp.dma_start(tokens_v[i, :, bass.ds(p * NCH, NCH), :],
                                             tok[:].rearrange("p (n i c) -> p n i c", i=2, c=C)[:, :, i, :]).then_inc(tok_stored, 16)

                        sp.dma_start(xt[:], x2[:, 0:TB]).then_inc(x_loaded, 16)
                        shift_seq(1)
                        turn(1, FIRST)
                        with sp.Fori(2, N) as it:
                            turn(it, MIDDLE)
                        turn(N, LAST)
                        store(2, N + 1, LAST)
                        store_rest(2, N + 1, LAST)
                        sp.wait_ge(x3_stored, 16 * (N + 1))
                        sp.wait_ge(lg_stored, 16 * (N + 1))
                        sp.wait_ge(tok_stored, 32 * (N + 1))

                    @block.gpsimd
                    def _(pool):
                        def tile(t, i, it, kind):
                            s = UNIT * i + t
                            wait_block(pool, "C", t, i, it, kind)
                            pool.wait_ge(h_ready[s % RA], used(it, s, RA) + 1)
                            if t % 4 == 0:
                                pool.wait_ge(folded, 8 * it + s // 4 - RC // 4 + 1)
                            nc.gpsimd.tensor_tensor(hc[s % RC][:], hh[s % RA][:], ct[t // 4 % 2][:], ALU.mult).then_inc(hc_ready[s % RC], 1)

                        def products(i, o):
                            pool.wait_ge(dt_ready[i], o + 1)
                            nc.gpsimd.tensor_tensor(dtu[i][:], dt[i][:], u[i][:], ALU.mult).then_inc(dtu_ready[i], 1)
                            pool.wait_ge(dtu_ready[i], o + 1)
                            first = dt[i][:].rearrange("p (w t) -> p w t", t=ST)[:, :, 0]
                            nc.gpsimd.tensor_tensor(first, first, resets[:], ALU.add).then_inc(reset_ready[i], 1)

                        def turn(it, kind):
                            for i in range(2):
                                for t in range(UNIT):
                                    tile(t, i, it, kind)
                                    if i and kind != LAST and t in (10, 12):
                                        products((t - 10) // 2, it + 1)

                        for i in range(2):
                            nc.gpsimd.memset(seq[i][:], 0.0).then_inc(pads_zero, 1)
                        nc.gpsimd.memset(resets[:], RESET).then_inc(pads_zero, 1)
                        pool.wait_ge(pads_zero, 3)
                        for i in range(2):
                            products(i, 1)
                        turn(1, FIRST)
                        with pool.Fori(2, N) as it:
                            turn(it, MIDDLE)
                        turn(N, LAST)

                    @block.scalar
                    def _(act):
                        a = nc.scalar.activation

                        def move(core, name, it, kind, dst, func=ACT.Copy, rows=P, cols=slice(0, TB), **more):
                            w = wait_made(act, core, name, it, kind)
                            a(dst, w[0:rows, cols], func, **more).then_inc(read(core, name, it, kind), 1)

                        def move_spread(core, b, name, it, kind, i, cur):
                            if cur is not None:
                                s = UNIT * i + 12 + b
                                act.wait_ge(a_ready[s % RA], used(cur, s, RA) + 1)
                            move(core, f"{name}dt{b}", it, kind, dts[b][:])
                            if cur is not None:
                                act.wait_ge(b_ready[s % RB], used(cur, s, RB) + 1)
                            move(core, f"{name}du{b}", it, kind, dus[b][:])

                        def move_block(core, name, m, it, kind, i, cur):
                            if cur is not None:
                                s = UNIT * i + 4 * (m - 2) + 3
                                if name[-2:] in ("nB", "B1", "B2", "B3"):
                                    act.wait_ge(b_ready[s % RB], used(cur, s, RB) + 1)
                                else:
                                    act.wait_ge(hc_ready[s % RC], used(cur, s, RC) + 1)
                            move(core, name, it, kind, (bt if "B" in name else ct)[m % 2][:])

                        def norm_start(core, it, kind, o):
                            act.wait_ge(seq_ready[1], o)
                            act.wait_ge(parts_ready[1], o)
                            w = wait_made(act, core, "xc", it, kind)
                            a(sq[:], w[:, 0:TB], ACT.Square).then_inc(sq_ready, 1)
                            a(xc[:], w[:, 0:TB], ACT.Copy).then_inc(read(core, "xc", it, kind), 1)

                        def norm_ends(core, it, kind, names):
                            steps = {"var": (sq, eps_6, rstd_ready), "var2": (sq2, eps_bn, rstd2_ready)}
                            for name in names:
                                move(core, name, it, kind, steps[name][0][:], ACT.Ln, bias=steps[name][1][:])
                            for name in names:
                                wait_moved(act, core, name, it, kind)
                                a(steps[name][0][:], steps[name][0][:], ACT.Exp, scale=-0.5).then_inc(steps[name][2], 1)

                        def silus(core, it, kind, o):
                            for i in range(2):
                                act.wait_ge(skip_ready[i], o)
                                act.wait_ge(dtu_ready[i], o)
                                move(core, f"conv{i}", it, kind, u[i][:], ACT.Silu, bias=conv_bias[:])
                            act.wait_ge(yz_ready[0], o)
                            move(core, "z0", it, kind, gate[0][:], ACT.Silu)
                            act.wait_ge(gate1_ready, o)
                            move(core, "z1", it, kind, gate_next[:], ACT.Silu)

                        def softplus_start(core, it, kind, o):
                            for i in range(2):
                                w = wait_made(act, core, f"pre{i}", it, kind)
                                a(dtu[i][:], w[:, 0:TB], ACT.Abs, bias=dt_bias[:]).then_inc(abs_ready[i], 1)
                                a(dt[i][:], w[:, 0:TB], ACT.Relu, bias=dt_bias[:]).then_inc(read(core, f"pre{i}", it, kind), 1)
                            for i in range(2):
                                act.wait_ge(abs_ready[i], o + 1)
                                a(dtu[i][:], dtu[i][:], ACT.Exp, scale=-1.0).then_inc(e_ready[i], 1)

                        def softplus_end(o):
                            for i in range(2):
                                act.wait_ge(e_ready[i], o + 1)
                                a(dtu[i][:], dtu[i][:], ACT.Ln, bias=one_col[:]).then_inc(l_ready[i], 1)

                        def high_parts(core, it, kind):
                            for i in range(2):
                                w = wait_made(act, core, f"xp{i}", it, kind)
                                a(parts[i][:], w[:, 0:TB], ACT.Copy).then_inc(high_ready[i], 1)

                        def final_norm_start(core, it, kind):
                            w = wait_made(act, core, "xc2", it, kind)
                            a(sq2[:], w[:, 0:TB], ACT.Square).then_inc(sq2_ready, 1)
                            a(xl[:], w[:, 0:TB], ACT.Copy).then_inc(read(core, "xc2", it, kind), 1)

                        def final_moves(core, it, kind, o):
                            act.wait_ge(lg_stored, 16 * o)
                            move(core, "lgp", it, kind, lg[:], ACT.Identity, rows=2 * EC, bias=b_gate[:])
                            act.wait_ge(tok_stored, 32 * o)
                            move(core, "tok0", it, kind, tok[:, 0:BANK], cols=slice(0, BANK))
                            move(core, "tok1", it, kind, tok[:, BANK:TB], cols=slice(0, TB - BANK))

                        def core(i, it, kind):
                            prepares = i == 1 and kind != LAST
                            norms = i == 0 and kind != LAST
                            finals = i == 0 and kind != FIRST
                            here = (i, it, kind)
                            for t in range(UNIT):
                                s = UNIT * i + t
                                wait_spread(act, "dt", t, *here)
                                act.wait_ge(h_ready[s % RA], used(it, s, RA))
                                a(aa[s % RA][:], dts[t % 4][:], ACT.Exp,
                                  scale=decay[:, t % 4, t // 4:t // 4 + 1]).then_inc(a_ready[s % RA], 1)
                                if t == 0:
                                    move_spread(i, 3, "", it, kind, i - 1, it)
                                if t == 1:
                                    move_block(i, "B1", 1, it, kind, i, it)
                                if t == 2:
                                    move_block(i, "C1", 1, it, kind, i, it)
                                if t == 7 and prepares:
                                    silus(*here, it + 1)
                                if t == 5 + 2 * i:
                                    move_block(i, "B2", 2, it, kind, i, it)
                                    move_block(i, "C2", 2, it, kind, i, it)
                                if t == 7 and norms:
                                    norm_start(*here, it + 1)
                                if t == 8 and finals:
                                    final_norm_start(*here)
                                if t == 9 and i == 0:
                                    norm_ends(*here, ["var"] * norms + ["var2"] * finals)
                                if t == 8 and prepares:
                                    softplus_start(*here, it + 1)
                                if t == 9:
                                    if prepares:
                                        softplus_end(it + 1)
                                    move_block(i, "B3", 3, it, kind, i, it)
                                if t == 10:
                                    move_block(i, "C3", 3, it, kind, i, it)
                                    if prepares:
                                        high_parts(*here)
                                if t == 12 and finals:
                                    final_moves(*here, it - 1)
                                if kind == LAST and i:
                                    continue
                                if t == 14:
                                    move_spread(i, 0, "n", it, kind, i, it)
                                    move_block(i, "nB", 4, it, kind, i, it)
                                if t == 15:
                                    move_spread(i, 1, "n", it, kind, i, it)
                                    move_spread(i, 2, "n", it, kind, i, it)
                                    move_block(i, "nC", 4, it, kind, i, it)

                        here = (-1, 0, FIRST)
                        norm_start(*here, 1)
                        norm_ends(*here, ["var"])
                        silus(*here, 1)
                        softplus_start(*here, 1)
                        softplus_end(1)
                        high_parts(*here)
                        move_spread(-1, 0, "n", 0, FIRST, 0, None)
                        move_block(-1, "nB", 0, 0, FIRST, 0, None)
                        move_spread(-1, 1, "n", 0, FIRST, 0, None)
                        move_spread(-1, 2, "n", 0, FIRST, 0, None)
                        move_block(-1, "nC", 0, 0, FIRST, 0, None)
                        for i in range(2):
                            core(i, 1, FIRST)
                        with act.Fori(2, N) as it:
                            for i in range(2):
                                core(i, it, MIDDLE)
                        for i in range(2):
                            core(i, N, LAST)
                        final_norm_start(2, N, LAST)
                        norm_ends(2, N, LAST, ["var2"])
                        final_moves(2, N, LAST, N)

                    @block.vector
                    def _(dve):
                        v = nc.vector

                        def inputs(t, i, it, kind):
                            s = UNIT * i + t
                            wait_spread(dve, "du", t, i, it, kind)
                            wait_block(dve, "B", t, i, it, kind)
                            dve.wait_ge(h_ready[(s - RB) % RA], used(it, s - RB, RA) + 1)
                            v.tensor_tensor(bb[s % RB][:], dus[t % 4][:], bt[t // 4 % 2][:], ALU.mult).then_inc(b_ready[s % RB], 1)

                        def scan(s, it):
                            dve.wait_ge(a_ready[s % RA], used(it, s, RA) + 1)
                            dve.wait_ge(b_ready[s % RB], used(it, s, RB) + 1)
                            dve.wait_ge(hc_ready[(s - RA) % RC], used(it, s - RA, RC) + 1)
                            v.tensor_tensor_scan(hh[s % RA][:], aa[s % RA][:], bb[s % RB][:], 0.0,
                                                 ALU.mult, ALU.add).then_inc(h_ready[s % RA], 1)

                        def norm(core, it, kind, o, seq_free):
                            dve.wait_ge(rstd_ready, o + 1)
                            wait_moved(dve, core, "xc", it, kind)
                            v.tensor_tensor(xc[:], xc[:], sq[:], ALU.mult).then_inc(xn_ready, 1)
                            dve.wait_ge(xn_ready, o + 1)
                            if seq_free:
                                wait_moved(dve, before(0, it, kind)[0], "z1", *before(0, it, kind)[1:])
                            for i in range(2):
                                q = slice(C * i, C * i + C)
                                v.tensor_tensor(seq[i][q, :, CONV - 1:].rearrange("p w (r c) -> p r w c", c=WS), win(xc)[q],
                                                pos_t[q].rearrange("p (r c) -> p r c", c=WS).unsqueeze(2).broadcast_to([C, WS, NWB, WS]),
                                                ALU.add).then_inc(seq_ready[i], 1)

                        def steps(i, o, cur):
                            dve.wait_ge(l_ready[i], o + 1)
                            wait_moved(dve, cur[0], f"pre{i}", *cur[1:])
                            v.tensor_tensor(dt[i][:], dt[i][:], dtu[i][:], ALU.add).then_inc(dt_ready[i], 1)

                        def low_parts(i, o, cur):
                            h = slice(C, P)
                            w = wait_made(dve, cur[0], f"xp{i}", *cur[1:])
                            dve.wait_ge(high_ready[i], o + 1)
                            dve.wait_ge(parts_ready[1 - i], o + i)
                            v.tensor_tensor(rest[h, :], w[h, 0:TB], parts[i][h, :], ALU.subtract).then_inc(read(cur[0], f"xp{i}", *cur[1:]), 1)
                            wait_moved(dve, cur[0], f"xp{i}", *cur[1:])
                            v.tensor_copy(parts[i][h, :], rest[h, :]).then_inc(mid_ready[i], 1)
                            dve.wait_ge(mid_ready[i], o + 1)
                            q = slice(96, P)
                            v.tensor_tensor(parts[i][q, :], rest[q, :], parts[i][q, :], ALU.subtract).then_inc(parts_ready[i], 1)

                        def gated(i, o, rows):
                            dve.wait_ge(folded, rows)
                            if i:
                                dve.wait_ge(gate1_ready, o + 1)
                            v.tensor_tensor(yz[i][:], yy[:, 0:TB], gate[i][:], ALU.mult).then_inc(yz_ready[i], 1)

                        def gate_over(it, kind):
                            wait_moved(dve, before(0, it, kind)[0], "z1", *before(0, it, kind)[1:])
                            dve.wait_ge(yz_ready[1], it)
                            v.tensor_copy(gate[1][:], gate_next[:]).then_inc(gate1_ready, 1)

                        def residual(core, it, kind, o):
                            w = wait_made(dve, core, "out", it, kind)
                            dve.wait_ge(x3_stored, 16 * o)
                            dve.wait_ge(xr_loaded, 16 * o + 16)
                            v.tensor_tensor(win(x3s), seqs(w), win(xr), ALU.add).then_inc(read(core, "out", it, kind), 1)

                        def final_norm(core, it, kind, o):
                            dve.wait_ge(rstd2_ready, o + 1)
                            wait_moved(dve, core, "xc2", it, kind)
                            v.tensor_tensor(xl[:], xl[:], sq2[:], ALU.mult).then_inc(xl_ready, 1)

                        def core(i, it, kind):
                            finals = kind != FIRST and i == 0
                            here = (i, it, kind)
                            for t in range(UNIT):
                                s = UNIT * i + t
                                inputs(t, *here)
                                if not (kind == FIRST and s == 0):
                                    scan(s - 1, it)
                                if t == 3 and not (kind == FIRST and i == 0):
                                    gated(1 - i, it - 1 + i, 8 * it + 4 * i)
                                if t == 5 and i == 0:
                                    gate_over(it, kind)
                                if t == 5 and finals:
                                    residual(*here, it - 1)
                                if t == 10 and i == 0 and kind != LAST:
                                    norm(*here, it + 1, True)
                                if t == 11 and finals:
                                    final_norm(*here, it - 1)
                                if t in (10, 11) and i and kind != LAST:
                                    steps(t - 10, it + 1, here)
                                if t in (11, 12) and i and kind != LAST:
                                    low_parts(t - 11, it + 1, here)

                        dve.wait_ge(pads_zero, 3)
                        norm(-1, 0, FIRST, 1, False)
                        for i in range(2):
                            steps(i, 1, (-1, 0, FIRST))
                            low_parts(i, 1, (-1, 0, FIRST))
                        for i in range(2):
                            core(i, 1, FIRST)
                        with dve.Fori(2, N) as it:
                            for i in range(2):
                                core(i, it, MIDDLE)
                        for i in range(2):
                            core(i, N, LAST)
                        scan(TILES - 1, N)
                        gated(1, N, 8 * N + 8)
                        residual(2, N, LAST, N)
                        final_norm(2, N, LAST, N)

                    @block.tensor
                    def _(pe):
                        mm = nc.tensor.matmul

                        def product(core, name, it, kind):
                            w, c = place(core, name, it, kind)
                            pe.wait_ge(moved[w], c + 1)
                            return ww[w]

                        def strip(core, name, it, kind, weight, src, rows=slice(0, P)):
                            w = product(core, name, it, kind)
                            for lo, hi in banks(TB):
                                last = mm(w[rows, lo:hi], weight, src[:, lo:hi], start=True, stop=True)
                            last.then_inc(made[place(core, name, it, kind)[0]], 1)

                        def windows(core, name, it, kind, src, weights, shifts):
                            w = product(core, name, it, kind)
                            for lo, hi in banks(TB):
                                for n, (weight, shift) in enumerate(zip(weights, shifts)):
                                    last = mm(w[:, lo:hi], weight, src[:, lo // ST:hi // ST, shift:shift + ST],
                                              start=(n == 0), stop=(n == len(weights) - 1))
                            last.then_inc(made[place(core, name, it, kind)[0]], 1)

                        def norm_start(core, it, kind, o):
                            pe.wait_ge(x_loaded, 16 * o + 16)
                            strip(core, "xc", it, kind, center[:], xt)

                        def norm_end(core, it, kind, o):
                            pe.wait_ge(sq_ready, o + 1)
                            strip(core, "var", it, kind, average[:], sq)

                        def conv(core, it, kind, i, o):
                            pe.wait_ge(shifted, 32 * o + 32)
                            windows(core, f"conv{i}", it, kind, seq[i], [w_conv[:, i, k, :] for k in range(CONV // 2)], range(CONV // 2))

                        def gates(core, it, kind):
                            for i in range(2):
                                windows(core, f"z{i}", it, kind, seq[i], [w_z[:, i, :]], [CONV - 1])

                        def pres(core, it, kind):
                            for i in range(2):
                                wait_moved(pe, core, f"conv{i}", it, kind)
                                strip(core, f"pre{i}", it, kind, w_dt_full[:], u[i])

                        def xps(core, it, kind):
                            for i in range(2):
                                strip(core, f"xp{i}", it, kind, w_bc[:].rearrange("p a n -> p (a n)"), u[i])

                        def spread_block(core, b, name, it, kind, i, o):
                            if o is not None:
                                pe.wait_ge(reset_ready[i], o + 1)
                            strip(core, f"{name}dt{b}", it, kind, spread[:, b, :], dt[i])
                            strip(core, f"{name}du{b}", it, kind, spread[:, b, :], dtu[i])

                        def state_block(core, name, m, it, kind, i, o=None):
                            if o is not None:
                                pe.wait_ge(parts_ready[i], o + 1)
                            strip(core, name, it, kind, rows_bc[:, m, :], parts[i])

                        def skip_start(i, it):
                            pe.wait_ge(yz_ready[1 - i], it + i)
                            for lo, hi in banks(TB):
                                last = mm(yy[:, lo:hi], skip[:], u[i][:, lo:hi], start=True, stop=False)
                            last.then_inc(skip_ready[i], 1)

                        def fold_row(i, it, row):
                            for b in range(4):
                                s = UNIT * i + 4 * row + b
                                pe.wait_ge(hc_ready[s % RC], used(it, s, RC) + 1)
                            for lo, hi in banks(TB):
                                for b in range(4):
                                    s = UNIT * i + 4 * row + b
                                    last = mm(yy[32 * b:32 * b + 32, lo:hi], fold[:], hc[s % RC][:, lo:hi],
                                              start=False, stop=(row == 3))
                            last.then_inc(folded, 1)

                        def out(core, it, kind, o):
                            for i in range(2):
                                pe.wait_ge(yz_ready[i], o + 1)
                            w = product(core, "out", it, kind)
                            for lo, hi in banks(TB):
                                for i in range(2):
                                    last = mm(w[C * i:C * i + C, lo:hi], w_out_t[:], yz[i][:, lo:hi], start=True, stop=True)
                            last.then_inc(made[place(core, "out", it, kind)[0]], 1)

                        def final_norm_start(core, it, kind, o):
                            wait_moved(pe, core, "out", it, kind)
                            strip(core, "xc2", it, kind, center[:], x3s)

                        def final_norm_end(core, it, kind, o):
                            pe.wait_ge(sq2_ready, o + 1)
                            strip(core, "var2", it, kind, average[:], sq2)

                        def final_products(core, it, kind, o):
                            pe.wait_ge(xl_ready, o + 1)
                            strip(core, "lgp", it, kind, w_gate[:], xl, rows=slice(0, 2 * EC))
                            for name, n0, n1 in (("tok0", 0, 4), ("tok1", 4, NCH)):
                                w = product(core, name, it, kind)
                                for n in range(n0, n1):
                                    last = nc.tensor.transpose(w[:, (n - n0) * P:(n - n0 + 1) * P], xl[:, n * P:(n + 1) * P], ident[:])
                                last.then_inc(made[place(core, name, it, kind)[0]], 1)

                        def core(i, it, kind):
                            prepares = i == 1 and kind != LAST
                            norms = i == 0 and kind != LAST
                            finals = i == 0 and kind != FIRST
                            n, o, here = 1 - i, it + i, (i, it, kind)
                            for t in range(UNIT):
                                if t == 0:
                                    spread_block(i, 3, "", it, kind, i, None)
                                if t == 1:
                                    state_block(i, "B1", 1, it, kind, i)
                                if t == 2:
                                    state_block(i, "C1", 5, it, kind, i)
                                    if prepares:
                                        conv(*here, 0, o)
                                if t == 3:
                                    if not (kind == FIRST and i == 0):
                                        fold_row(1 - i, it - (1 - i), 3)
                                    if prepares:
                                        conv(*here, 1, o)
                                        gates(*here)
                                if t == 4 and i:
                                    skip_start(i, it)
                                if t == 5:
                                    state_block(i, "B2", 2, it, kind, i)
                                    state_block(i, "C2", 6, it, kind, i)
                                    if finals:
                                        out(*here, it - 1)
                                if t == 6:
                                    if i == 0:
                                        skip_start(i, it)
                                    if norms:
                                        norm_start(*here, it + 1)
                                if t == 7:
                                    fold_row(i, it, 0)
                                    if finals:
                                        final_norm_start(*here, it - 1)
                                if t == 8:
                                    if norms:
                                        norm_end(*here, it + 1)
                                    if finals:
                                        final_norm_end(*here, it - 1)
                                    if prepares:
                                        pres(*here)
                                if t == 9:
                                    state_block(i, "B3", 3, it, kind, i)
                                if t == 10:
                                    state_block(i, "C3", 7, it, kind, i)
                                    if prepares:
                                        xps(*here)
                                if t == 11:
                                    fold_row(i, it, 1)
                                    if finals:
                                        final_products(*here, it - 1)
                                if t == 13 and not (kind == LAST and i):
                                    spread_block(i, 0, "n", it, kind, n, o)
                                    state_block(i, "nB", 0, it, kind, n, o)
                                if t == 15:
                                    if not (kind == LAST and i):
                                        spread_block(i, 1, "n", it, kind, n, None)
                                        spread_block(i, 2, "n", it, kind, n, None)
                                        state_block(i, "nC", 4, it, kind, n)
                                    fold_row(i, it, 2)

                        here = (-1, 0, FIRST)
                        norm_start(*here, 1)
                        norm_end(*here, 1)
                        conv(*here, 0, 1)
                        conv(*here, 1, 1)
                        gates(*here)
                        pres(*here)
                        xps(*here)
                        spread_block(-1, 0, "n", 0, FIRST, 0, 1)
                        state_block(-1, "nB", 0, 0, FIRST, 0, 1)
                        spread_block(-1, 1, "n", 0, FIRST, 0, None)
                        spread_block(-1, 2, "n", 0, FIRST, 0, None)
                        state_block(-1, "nC", 4, 0, FIRST, 0)
                        for i in range(2):
                            core(i, 1, FIRST)
                        with pe.Fori(2, N) as it:
                            for i in range(2):
                                core(i, it, MIDDLE)
                        for i in range(2):
                            core(i, N, LAST)
                        fold_row(1, N, 3)
                        out(2, N, LAST, N)
                        final_norm_start(2, N, LAST, N)
                        final_norm_end(2, N, LAST, N)
                        final_products(2, N, LAST, N)

        def phase_c():
            IMG = min(4, B)
            R = IMG * EC
            CK = TB if HW // TB % 2 == 0 else TB // 2
            NK = HW // CK
            with ExitStack() as st:
                def sb(name, shape, dt=F32):
                    return sbuf("c_" + name, shape, dt, st)

                def sem(name, turn=0):
                    return new_sem("c_" + name, turn)

                lt = sb("l", [R, HW])
                gt = sb("g", [R, HW])
                w1 = sb("w1", [C + 1, EC, HID])
                w2 = sb("w2", [P, EC, 2, C])
                w2b = sb("w2b", [1, EC, C])
                ones = sb("ones", [1, IMG])
                top = sb("top", [R, TOPK])
                idx = sb("idx", [R, TOPK], U32)
                idf = sb("idf", [R, TOPK])
                base = sb("base", [R, 1])
                neg = sb("neg", [R, 1])
                tot = sb("tot", [R, 1])
                rec = sb("rec", [R, 1])
                p8 = sb("p8", [R, TOPK])
                rows = sb("rows", [R, TOPK, C])
                pool_t = sb("pooled", [R, C])
                pool_x = sb("pooled_t", [C + 1, R])
                hid = sb("hid", [P, 2 * EC, IMG])
                ot = sb("ot", [C, IMG, EC])
                mix = sb("mix", [R, IMG // 2, P])
                xs = [sb(f"x{i}", [P, CK]) for i in range(2)]
                ys = [sb(f"y{i}", [P, CK]) for i in range(2)]
                pt = psum("c_pt", [P, BANK], F32, st)
                ph = psum("c_ph", [P, BANK], F32, st)
                po = psum("c_po", [P, BANK], F32, st)
                pr = psum("c_pr", [P, BANK], F32, st)
                py = [psum(f"c_py{i}", [P, 2 * BANK], F32, st) for i in range(2)]

                w_loaded, l_loaded, zeroed, top_ready, neg_ready, exp_ready, e8_ready, taken = (
                    sem(n) for n in ("wl", "ll", "zero", "top", "neg", "exp", "e8", "taken"))
                chain, idx_ready, gathered, pooled, tr_ready, px_ready, h_ready, gelu_ready = (
                    sem(n) for n in ("chain", "idx", "gath", "pooled", "tr", "px", "h", "gelu"))
                o_ready, ot_ready, or_ready, mix_ready, g_ready = (sem(n) for n in ("o", "ot", "or", "mix", "gr"))
                x_loaded, stored = ([sem(f"{n}{i}", 16) for i in range(2)] for n in ("xl", "st"))
                y_prod, y_ready = ([sem(f"{n}{i}", 1) for i in range(2)] for n in ("yp", "yr"))
                nc.all_engine_barrier()
                DV = 6 + TOPK

                for tile in range(B // IMG):
                    b0 = tile * IMG
                    half = NK // 2
                    turns = []
                    for kk in range(IMG // 2):
                        turns.append((kk, half))
                    per = (IMG // 2) * half

                    with nc.Block() as block:
                        @block.sync
                        def _(sp):
                            for kk in range(IMG // 2):
                                at = (b0 // 2 + kk) * HW
                                sp.dma_start(lt[2 * EC * kk:2 * EC * (kk + 1), :], logits[:, at:at + HW]).then_inc(l_loaded, 16)
                            if tile == 0:
                                sp.dma_start(w1[:], weight1.rearrange("e d h -> d e h")).then_inc(w_loaded, 16)
                                for n in range(4):
                                    h, q = n // 2, C * (n % 2)
                                    sp.dma_start(w2[q:q + C, :, h, :],
                                                 weight2[:, h * P + q:h * P + q + C, :].rearrange("e h o -> h e o")).then_inc(w_loaded, 16)
                                sp.dma_start(w2b[:], weight2[:, HID:HID + 1, :].rearrange("e a o -> a e o")).then_inc(w_loaded, 16)
                            for kk, n in turns:
                                k = b0 // 2 + kk
                                with sp.Fori(0, n) as j:
                                    for s in range(2):
                                        at = (j * 2 + s) * CK
                                        done = j + (tile * per + kk * half + 1)
                                        sp.wait_ge(y_ready[s], done)
                                        sp.dma_start(xs[s][:], x3[:, bass.ds(at + k * HW, CK)]).then_inc(x_loaded[s], 16)
                                    for s in range(2):
                                        at = (j * 2 + s) * CK
                                        done = j + (tile * per + kk * half + 1)
                                        sp.wait_ge(y_ready[s], done + 1)
                                        sp.dma_start(out_v[k, :, bass.ds(at, CK)], ys[s][:]).then_inc(stored[s], 16)
                            for s in range(2):
                                sp.wait_ge(stored[s], 16 * (per * (tile + 1) + 1))

                        @block.gpsimd
                        def _(pool):
                            pool.wait_ge(idx_ready, tile + 1)
                            for n in range(TOPK):
                                nc.gpsimd.indirect_dma_start(out=rows[:, n, :], out_offset=None, in_=tokens,
                                                             in_offset=bass.IndirectOffsetOnAxis(ap=idx[:, n:n + 1], axis=0)).then_inc(gathered, 16)

                        @block.scalar
                        def _(act):
                            a = nc.scalar.activation
                            act.wait_ge(neg_ready, tile + 1)
                            a(gt[:], lt[:], ACT.Exp, bias=neg[:], accum_out=tot[:]).then_inc(exp_ready, 1)
                            a(p8[:], top[:], ACT.Exp, bias=neg[:]).then_inc(e8_ready, 1)
                            act.wait_ge(h_ready, tile + 1)
                            a(hid[:].rearrange("p e b -> p (e b)"), ph[:, 0:2 * EC * IMG], ACT.Gelu).then_inc(gelu_ready, 1)

                        @block.vector
                        def _(dve):
                            v = nc.vector
                            if tile == 0:
                                for n in range(IMG):
                                    v.memset(base[EC * n:EC * n + EC, :], float((n % 2 * NP + n // 2) * HW)).then_inc(zeroed, 1)
                                v.memset(pool_x[C:C + 1, :], 1.0).then_inc(zeroed, 1)
                                v.memset(ones[:], 1.0).then_inc(zeroed, 1)
                                v.memset(mix[:], 0.0).then_inc(zeroed, 1)
                                dve.wait_ge(zeroed, IMG + 3)
                            dve.wait_ge(l_loaded, 16 * (IMG // 2) * (tile + 1))
                            v.max(top[:], lt[:]).then_inc(top_ready, 1)
                            dve.wait_ge(top_ready, tile + 1)
                            v.tensor_scalar(neg[:], top[:, 0:1], -1.0, None, ALU.mult).then_inc(neg_ready, 1)
                            n = [tile * DV]

                            def link(ins):
                                n[0] += 1
                                ins.then_inc(chain, 1)
                                dve.wait_ge(chain, n[0])

                            link(v.max_index(idx[:], top[:], lt[:]))
                            link(v.tensor_copy(idf[:], idx[:]))
                            link(v.tensor_scalar(idf[:], idf[:], base[:, 0:1], float(b0 // 2 * HW), ALU.add, ALU.add))
                            v.tensor_copy(idx[:], idf[:]).then_inc(idx_ready, 1)
                            dve.wait_ge(exp_ready, tile + 1)
                            link(v.match_replace(lt[:], top[:], lt[:], TAKEN))
                            v.scalar_tensor_tensor(gt[:], lt[:], 0.99 * TAKEN, gt[:], ALU.is_le, ALU.mult).then_inc(g_ready, 1)
                            link(v.reciprocal(rec[:], tot[:]))
                            dve.wait_ge(e8_ready, tile + 1)
                            link(v.tensor_scalar(p8[:], p8[:], rec[:, 0:1], None, ALU.mult))
                            dve.wait_ge(gathered, 16 * TOPK * (tile + 1))
                            link(v.tensor_scalar(pool_t[:], rows[:, 0, :], p8[:, 0:1], None, ALU.mult))
                            for m in range(1, TOPK):
                                link(v.scalar_tensor_tensor(pool_t[:], rows[:, m, :], p8[:, m:m + 1], pool_t[:], ALU.mult, ALU.add))
                            dve.wait_ge(tr_ready, tile + 1)
                            v.tensor_copy(pool_x[0:C, :], pt[0:C, 0:R]).then_inc(px_ready, 1)
                            dve.wait_ge(o_ready, tile + 1)
                            v.tensor_copy(ot[:], po[0:C, 0:R].rearrange("o (e b) -> o b e", b=IMG)).then_inc(ot_ready, 1)
                            dve.wait_ge(or_ready, tile + 1)
                            for b in range(IMG):
                                q = slice(EC * b, EC * b + EC)
                                v.tensor_scalar(mix[q, b // 2, C * (b % 2):C * (b % 2) + C], pr[q, 0:C], rec[q, 0:1], None,
                                                ALU.mult).then_inc(mix_ready, 1)
                            for kk, turn in turns:
                                with dve.Fori(0, turn) as j:
                                    done = j + (tile * per + kk * half + 1)
                                    for s in range(2):
                                        dve.wait_ge(y_prod[s], done + 1)
                                        dve.wait_ge(x_loaded[s], 16 * done + 16)
                                        dve.wait_ge(stored[s], 16 * done)
                                        v.tensor_tensor(ys[s][:], py[s][:, 0:CK], xs[s][:], ALU.add).then_inc(y_ready[s], 1)

                        @block.tensor
                        def _(pe):
                            mm = nc.tensor.matmul
                            pe.wait_ge(chain, DV * (tile + 1))
                            nc.tensor.transpose(pt[0:C, 0:R], pool_t[:], ident[0:R, 0:R]).then_inc(tr_ready, 1)
                            pe.wait_ge(px_ready, tile + 1)
                            pe.wait_ge(w_loaded, 96)
                            by_expert = pool_x[:].rearrange("d (b e) -> d e b", e=EC)
                            for x in range(EC):
                                for h in range(2):
                                    at = (2 * x + h) * IMG
                                    last = mm(ph[:, at:at + IMG], w1[:, x, h * P:(h + 1) * P], by_expert[:, x, :], start=True, stop=True)
                            last.then_inc(h_ready, 1)
                            pe.wait_ge(gelu_ready, tile + 1)
                            for x in range(EC):
                                dst = po[0:C, x * IMG:(x + 1) * IMG]
                                for h in range(2):
                                    mm(dst, w2[:, x, h, :], hid[:, 2 * x + h, :], start=(h == 0), stop=False)
                                last = mm(dst, w2b[:, x, :], ones[:], start=False, stop=True)
                            last.then_inc(o_ready, 1)
                            pe.wait_ge(ot_ready, tile + 1)
                            nc.tensor.transpose(pr[0:R, 0:C], ot[:].rearrange("o b e -> o (b e)"), ident[0:C, 0:C]).then_inc(or_ready, 1)
                            pe.wait_ge(mix_ready, IMG * (tile + 1))
                            pe.wait_ge(g_ready, tile + 1)
                            for kk, turn in turns:
                                with pe.Fori(0, turn) as j:
                                    done = j + (tile * per + kk * half + 1)
                                    for s in range(2):
                                        pe.wait_ge(y_ready[s], done)
                                        for a, b in banks(CK):
                                            last = mm(py[s][:, a:b], mix[:, kk, :], gt[:, bass.ds((j * 2 + s) * CK + a, b - a)],
                                                      start=True, stop=True)
                                        last.then_inc(y_prod[s], 1)

        end_phase()
        phase_a()
        end_phase()
        phase_b()
        end_phase()
        phase_c()


_INS = ['x', 'L0_conv_wq', 'L0_conv_wk', 'L0_conv_wv', 'L0_conv_wo', 'L0_conv_bn_gamma', 'L0_conv_bn_beta',
        'L0_conv_bn_mean', 'L0_conv_bn_var', 'L0_ffn_router_w', 'L0_ffn_router_b', 'L0_ffn_expert_w',
        'L0_ffn_expert_b', 'L1_conv_pos', 'L1_conv_W_in', 'L1_conv_conv_w', 'L1_conv_conv_b', 'L1_conv_W_xproj',
        'L1_conv_W_dt', 'L1_conv_b_dt', 'L1_conv_A_log', 'L1_conv_Dp', 'L1_conv_W_out', 'L1_ffn_gate_w',
        'L1_ffn_gate_b', 'L1_ffn_weight1', 'L1_ffn_weight2']


def kernel(**inputs):
    import numpy as _np
    import concourse.bacc as _bacc
    from concourse.bass_utils import run_bass_kernel_spmd as _run

    arrays = {f"in_{name}": _np.ascontiguousarray(inputs[name]) for name in _INS}
    nc = _bacc.Bacc("TRN2", target_bir_lowering=False, num_devices=1)
    args = [nc.dram_tensor(f"in_{name}", arrays[f"in_{name}"].shape, F32, kind="ExternalInput").ap() for name in _INS]
    b, c, h, w = arrays["in_x"].shape
    out = nc.dram_tensor("out", [b, c, h, w], F32, kind="ExternalOutput").ap()
    x2 = nc.dram_tensor("x2", [2 * c, b // 2 * h * w], F32, kind="Internal").ap()
    x3 = nc.dram_tensor("x3", [2 * c, b // 2 * h * w], F32, kind="Internal").ap()
    logits = nc.dram_tensor("logits", [2 * EC, b // 2 * h * w], F32, kind="Internal").ap()
    tokens = nc.dram_tensor("tokens", [b * h * w, C], F32, kind="Internal").ap()
    program(nc, *args, out, x2, x3, logits, tokens)
    r = _run(nc, [arrays], core_ids=[0])
    return r.results[0]["out"]
```

```python
from contextlib import ExitStack

import concourse.bass as bass
from concourse import mybir

F32 = mybir.dt.float32
BF16 = mybir.dt.bfloat16
U32 = mybir.dt.uint32
ALU = mybir.AluOpType
ACT = mybir.ActivationFunctionType
AX = mybir.AxisListType

P = 128
C = 64
WIN = 7
WT = WIN * WIN
WP = 64
NE = 8
WS = 8
ST = WS * WS
CONV = 4
NS = 16
RK = 4
DI = 128
EC = 32
HID = 256
TOPK = 8
BANK = 512
SLOTS = 2
RESET = 1.0e15
BIG = 1.0e30
UNIT = 16
TILES = 2 * UNIT
RA = 4
RH = 8
RC = 8
SMALL = 21
TAKEN = -3.0e38


def banks(n):
    return [(a, min(a + BANK, n)) for a in range(0, n, BANK)]


def program(nc, x, wq, wk, wv, wo, gamma, beta, mean, var, router_w, router_b, expert_w, expert_b,
            pos, w_in, conv_w, conv_b, w_xproj, w_dt, b_dt, a_log, d_skip, w_out,
            gate_w, gate_b, weight1, weight2, out, x2, x3, logits, tokens):
    B, _, H, W = x.shape
    HW = H * W
    NP = B // 2
    TA = WIN * W
    NWA = W // WIN
    SA = H // WIN
    TB = WS * W
    NWB = W // WS
    SB = H // WS
    NCH = TB // P

    def pairs(t):
        return t.rearrange("(k i) c h w -> k (i c) (h w)", i=2)

    x_v, out_v = pairs(x), pairs(out)

    with ExitStack() as top:
        def sbuf(name, shape, dt=F32, on=top):
            return on.enter_context(nc.sbuf_tensor(name, shape, dt))

        def psum(name, shape, dt=F32, on=top):
            return on.enter_context(nc.psum_tensor(name, shape, dt))

        phase_sems = []

        def new_sem(name, turn=0):
            handle = nc.alloc_semaphore(name=name)
            phase_sems.append(handle)
            if turn:
                nc.sync.sem_inc(handle, turn)
            return handle

        def end_phase():
            nc.clear_and_free_semaphores(phase_sems)
            phase_sems.clear()
            nc.all_engine_barrier()

        def new_sems(name, n=SLOTS, turn=0):
            return [new_sem(f"{name}{i}", turn) for i in range(n)]

        ident = sbuf("ident", [P, P])
        ident_bf = sbuf("ident_bf", [P, P], BF16)
        center = sbuf("center", [P, P])
        average = sbuf("average", [P, P])
        pos_t = sbuf("pos_t", [P, ST])
        w_z = sbuf("w_z", [P, 2, DI])
        w_conv = sbuf("w_conv", [P, 2, CONV // 2, DI])
        conv_bias = sbuf("conv_bias", [P, 1])
        wx = sbuf("wx", [P, RK + 2 * NS])
        wx4 = sbuf("wx4", [RK, P])
        wdt = sbuf("wdt", [RK, DI])
        w_dt_full = sbuf("w_dt_full", [P, DI])
        dt_bias = sbuf("dt_bias", [P, 1])
        decay = sbuf("decay", [P, 4, 4])
        spread = sbuf("spread", [P, 4, P])
        w_bc = sbuf("w_bc", [P, 4, 2 * NS])
        rows_bc = sbuf("rows_bc", [P, 8, P], BF16)
        fold = sbuf("fold", [P, 32])
        skip = sbuf("skip", [P, P])
        skip_col = sbuf("skip_col", [P, 1])
        w_out_t = sbuf("w_out_t", [P, C])
        w_gate = sbuf("w_gate", [P, 2 * EC])
        b_gate = sbuf("b_gate", [2 * EC, 1])
        eps_bn = sbuf("eps_bn", [P, 1])
        eps_6 = sbuf("eps_6", [P, 1])
        one_col = sbuf("one_col", [P, 1])
        own = ExitStack()
        w_qk = sbuf("w_qk", [P, P], on=own)
        w_vo = sbuf("w_vo", [P, P], on=own)
        shift = sbuf("shift", [P, P], on=own)
        w_router = sbuf("w_router", [P, 2 * NE], on=own)
        b_router = sbuf("b_router", [P, NE], on=own)
        rank8 = sbuf("rank8", [P, NE], on=own)
        w_exp = sbuf("w_exp", [P, NE, P], on=own)
        b_exp = sbuf("b_exp", [48, P], on=own)
        b_exp3 = sbuf("b_exp3", [48, 3, P], BF16, own)
        pick = sbuf("pick", [48, NE, P], BF16, own)

        with ExitStack() as st:
            wq2 = sbuf("wq2", [C // 2, 2, C], on=st)
            wv2 = sbuf("wv2", [C // 2, 2, C], on=st)
            wk_t = sbuf("wk_t", [C // 2, C], on=st)
            wo_t = sbuf("wo_t", [C // 2, C], on=st)
            bn_row = sbuf("bn_row", [P, 4, C], on=st)
            inv_row = sbuf("inv_row", [P, C], on=st)
            tmp_row = sbuf("tmp_row", [P, C], on=st)
            rest = sbuf("rest", [48, P], on=st)
            rest2 = sbuf("rest2", [48, P], on=st)
            fold4 = sbuf("fold4", [P, 4, 32], on=st)
            w_in_t = sbuf("w_in_t", [P, 2 * DI], on=st)
            taps = sbuf("taps", [P, DI, CONV], on=st)
            pq = psum("pq", [P, BANK], on=st)
            pv = psum("pv", [P, BANK], on=st)
            pd = psum("pd", [P, BANK], on=st)
            zeroed = new_sem("setup_zeroed")
            loaded = new_sem("setup_loaded")
            masks = new_sem("setup_masks")
            acts = new_sem("setup_acts")
            prods = new_sem("setup_prods")
            dves = new_sem("setup_dves")

            loads = []
            for i in range(2):
                c0 = C * i
                loads += [
                    (wq2[:, i, :], wq), (wv2[:, i, :], wv),
                    (w_router[c0:c0 + C, NE * i:NE * i + NE], router_w),
                    (w_exp[c0:c0 + C, :, c0:c0 + C], expert_w.rearrange("e d c -> d e c")),
                    (pos_t[c0:c0 + C, :], pos.rearrange("a c h w -> (a c) (h w)")),
                    (w_in_t[c0:c0 + C, :], w_in),
                    (w_gate[c0:c0 + C, EC * i:EC * i + EC], gate_w.rearrange("e c -> c e")),
                    (b_gate[EC * i:EC * i + EC, :], gate_b.rearrange("(e a) -> e a", a=1)),
                ]
                for part in range(3):
                    r0 = 16 * part + NE * i
                    loads.append((b_exp[r0:r0 + NE, c0:c0 + C], expert_b))
            for n, v in enumerate((gamma, beta, mean, var)):
                loads.append((bn_row[:, n, :], v.partition_broadcast(P)))
            for n in range(4):
                for b in range(4):
                    loads.append((decay[32 * n:32 * n + 32, b, :],
                                  a_log.rearrange("(b j) (m n) -> b n j m", j=32, n=4)[b, n]))
            loads += [
                (wk_t[:, :], wk), (wo_t[:, :], wo.rearrange("o m -> m o")),
                (b_router[:, :], router_b.partition_broadcast(P)),
                (taps[:, :, :].rearrange("p d k -> p (d k)"), conv_w.rearrange("d k -> (d k)").partition_broadcast(P)),
                (conv_bias[:, :], conv_b.rearrange("(c a) -> c a", a=1)),
                (wx[:, :], w_xproj), (wx4[:, :], w_xproj[:, 0:RK].rearrange("d r -> r d")),
                (wdt[:, :], w_dt), (dt_bias[:, :], b_dt.rearrange("(c a) -> c a", a=1)),
                (skip_col[:, :], d_skip.rearrange("(c a) -> c a", a=1)),
                (w_out_t[:, :], w_out),
            ]

            with nc.Block() as block:
                @block.sync
                def _(sp):
                    sp.wait_ge(zeroed, 8)
                    for dst, src in loads:
                        with nc.allow_non_contiguous_dma(reason="small weights, once"):
                            sp.dma_start(dst, src).then_inc(loaded, 16)
                    sp.wait_ge(loaded, 16 * len(loads))

                @block.gpsimd
                def _(pool):
                    g = nc.gpsimd
                    n = [0]

                    def link(ins):
                        n[0] += 1
                        ins.then_inc(masks, 1)
                        pool.wait_ge(masks, n[0])

                    def mark(t, pattern, base=0):
                        link(g.affine_select(out=t, in_=t, compare_op=ALU.not_equal, fill=1.0, base=base,
                                             pattern=pattern, channel_multiplier=1))

                    for t in (ident, ident_bf, pick, spread, fold4, average, rows_bc):
                        link(g.memset(t[:], 0.0))
                    link(g.memset(average[0:C, 0:C], 1.0 / C))
                    link(g.memset(average[C:P, C:P], 1.0 / C))
                    mark(ident[:], [[-1, P]])
                    mark(ident_bf[:], [[-1, P]])
                    mark(spread[:].rearrange("p b (n j) -> p b n j", j=32), [[-32, 4], [0, 4], [-1, 32]])
                    mark(fold4[:], [[-32, 4], [-1, 32]])
                    for part in range(3):
                        mark(pick[:].rearrange("r e (i c) -> r e i c", i=2), [[-1, NE], [-NE, 2], [0, C]], -16 * part)
                    for part in (0, 2, 3):
                        mark(rows_bc[:].rearrange("r m (n j) -> r m n j", j=32), [[-4, 8], [-1, 4], [0, 32]], -32 * part)
                    link(g.iota(rank8[:], pattern=[[-1, NE]], base=NE, channel_multiplier=0,
                                allow_small_or_imprecise_dtypes=True))

                @block.scalar
                def _(act):
                    act.wait_ge(zeroed, 11)
                    act.wait_ge(loaded, 16 * len(loads))
                    nc.scalar.activation(inv_row[:], bn_row[:, 3, :], ACT.Ln, bias=eps_bn[:]).then_inc(acts, 1)
                    act.wait_ge(acts, 1)
                    nc.scalar.activation(inv_row[:], inv_row[:], ACT.Exp, scale=-0.5).then_inc(acts, 1)
                    nc.scalar.activation(decay[:], decay[:], ACT.Exp).then_inc(acts, 1)

                @block.tensor
                def _(pe):
                    pe.wait_ge(loaded, 16 * len(loads))
                    nc.tensor.matmul(pq[:, 0:C], wq2[:].rearrange("m i c -> m (i c)"), wk_t[:],
                                     start=True, stop=True).then_inc(prods, 1)
                    nc.tensor.matmul(pv[:, 0:C], wv2[:].rearrange("m i c -> m (i c)"), wo_t[:],
                                     start=True, stop=True).then_inc(prods, 1)
                    nc.tensor.matmul(pd[:, 0:DI], wx4[:], wdt[:], start=True, stop=True).then_inc(prods, 1)

                @block.vector
                def _(dve):
                    v = nc.vector
                    for t in (w_router, w_exp, b_exp, w_gate, w_qk, w_vo, w_z, w_conv):
                        v.memset(t[:], 0.0).then_inc(zeroed, 1)
                    v.memset(eps_bn[:], 1e-5).then_inc(zeroed, 1)
                    v.memset(eps_6[:], 1e-6).then_inc(zeroed, 1)
                    v.memset(one_col[:], 1.0).then_inc(zeroed, 1)
                    dve.wait_ge(zeroed, 11)
                    dve.wait_ge(masks, 20)
                    dve.wait_ge(acts, 3)
                    dve.wait_ge(prods, 3)
                    n = [0]

                    def link(ins):
                        n[0] += 1
                        ins.then_inc(dves, 1)
                        dve.wait_ge(dves, n[0])

                    link(v.tensor_tensor(center[:], ident[:], average[:], ALU.subtract))
                    link(v.tensor_tensor(inv_row[:], inv_row[:], bn_row[:, 0, :], ALU.mult))
                    link(v.tensor_tensor(tmp_row[:], inv_row[:], bn_row[:, 2, :], ALU.mult))
                    for c0 in (0, C):
                        link(v.tensor_tensor(shift[:, c0:c0 + C], bn_row[:, 1, :], tmp_row[:], ALU.subtract))
                    for c0 in (0, C):
                        s = slice(c0, c0 + C)
                        link(v.tensor_scalar(w_qk[s, s], pq[s, 0:C], float(C // 2) ** -0.5, None, ALU.mult))
                        link(v.tensor_tensor(w_vo[s, s], pv[s, 0:C], inv_row[s, :], ALU.mult))
                    link(v.tensor_copy(b_exp3[:, 0, :], b_exp[:]))
                    link(v.tensor_tensor(rest[:], b_exp[:], b_exp3[:, 0, :], ALU.subtract))
                    link(v.tensor_copy(b_exp3[:, 1, :], rest[:]))
                    link(v.tensor_tensor(rest2[:], rest[:], b_exp3[:, 1, :], ALU.subtract))
                    link(v.tensor_copy(b_exp3[:, 2, :], rest2[:]))
                    for i in range(2):
                        q = slice(C * i, C * i + C)
                        link(v.tensor_copy(w_z[q, i, :], w_in_t[q, DI:2 * DI]))
                        for k in range(CONV):
                            q = slice(C * ((i + k // 2) % 2), C * ((i + k // 2) % 2) + C)
                            link(v.tensor_tensor(w_conv[q, i, k % 2, :], w_in_t[q, 0:DI], taps[q, :, k], ALU.mult))
                    link(v.tensor_copy(w_dt_full[:], pd[:, 0:DI]))
                    link(v.tensor_scalar(decay[:], decay[:], -1.0, -1e-12, ALU.mult, ALU.min))
                    for part in range(4):
                        link(v.tensor_copy(w_bc[:, part, :], wx[:, RK:RK + 2 * NS]))
                    link(v.tensor_reduce(fold[:], fold4[:].rearrange("p n j -> p j n"), AX.X, ALU.add))
                    link(v.tensor_scalar(skip[:], ident[:], skip_col[:, 0:1], None, ALU.mult))


        def phase_a():
            HALF = SA // SLOTS
            with ExitStack() as st:
                def sb(name, shape, dt=F32):
                    return [sbuf(f"{name}{i}", shape, dt, st) for i in range(SLOTS)]

                xt = sb("a_x", [P, TA])
                sq = sb("a_sq", [P, TA])
                xw = sb("a_xw", [P, NWA, WP])
                ts = sb("a_t", [P, NWA, WP])
                pr = sb("a_p", [P, NWA, WP])
                pt = sb("a_pt", [P, NWA // 2, P])
                vw = sb("a_vw", [P, NWA // 2, P])
                mx = sb("a_mx", [P, NWA])
                sm = sb("a_sm", [P, NWA])
                x1 = sb("a_x1", [P, TA])
                xn = sb("a_xn", [P, TA])
                xg = [sbuf(f"a_xg{i}", [P, TA], F32, st) for i in range(2 * SLOTS)]
                res = sb("a_res", [P, TA])
                lg = sb("a_lg", [W, 2 * WIN, NE])
                ex = sb("a_ex", [W, 2 * WIN, NE])
                cd = sb("a_cd", [W, 2 * WIN, NE])
                o1 = sb("a_o1", [W, 2 * WIN, NE])
                o2 = sb("a_o2", [W, 2 * WIN, NE])
                g1 = sb("a_g1", [W, 2 * WIN])
                g3 = sb("a_g3", [W, WIN, 48], BF16)
                gt = sb("a_gt", [48, TA], BF16)
                pa = [psum(f"a_pa{i}", [P, 2 * BANK], F32, st) for i in range(SLOTS)]
                pb = [psum(f"a_pb{i}", [P, 2 * BANK], F32, st) for i in range(SLOTS)]

                def sems(name, turn=1):
                    return new_sems("a_" + name, SLOTS, turn)

                pads_zero = new_sem("a_pads")
                x_loaded, stored = sems("loaded", 16), sems("stored", 16)
                xc_ready, sq_ready, var_ready, ln_ready, rstd_ready = (sems(n) for n in ("xc", "sq", "var", "ln", "rstd"))
                xw_ready = sems("xw", 2)
                t_ready, ts_ready, score_ready, max_ready, sub_ready, exp_ready, sum_ready, rec_ready, prob_ready = (
                    sems(n) for n in ("t", "ts", "score", "max", "sub", "exp", "sum", "rec", "prob"))
                tr_ready, pt_ready, v_ready, vw_ready, o_ready, x1_ready = (
                    sems(n) for n in ("tr", "pt", "v", "vw", "o", "x1"))
                xc2_ready, sq2_ready, var2_ready, ln2_ready, rstd2_ready, xn_ready = (
                    sems(n) for n in ("xc2_", "sq2_", "var2_", "ln2_", "rstd2_", "xn"))
                rout_ready, expl_ready, gtr_ready, gt_ready = (sems(n) for n in ("rout", "expl", "gtr", "gt"))
                small = sems("small", SMALL)
                gate_ready, xg_ready, moe_ready = (sems(n, NE) for n in ("gate", "xg", "moe"))
                acc_ready, res_ready = sems("acc"), sems("res")
                nc.all_engine_barrier()

                def win(t):
                    return t[:].rearrange("p (r w c) -> p r w c", r=WIN, c=WIN)

                def by_win(t):
                    return t[:, :, 0:WT].rearrange("p w (r c) -> p r w c", r=WIN)

                T = NP * HALF

                def halves(eng, half):
                    half(0, 1, None, None)
                    with eng.Fori(1, T) as it:
                        half(1, it, 0, it)
                        half(0, it + 1, 1, it)
                    half(1, T, 0, T)
                    half(None, None, 1, T)

                with nc.Block() as block:
                    @block.sync
                    def _(sp):
                        def load(s, k, j, it):
                            sp.wait_ge(x1_ready[s], it)
                            sp.dma_start(xt[s][:], x_v[k, :, bass.ds((j * SLOTS + s) * TA, TA)]).then_inc(x_loaded[s], 16)

                        def store(s, it):
                            sp.wait_ge(res_ready[s], it + 1)
                            sp.dma_start(x2[:, bass.ds(((it - 1) * SLOTS + s) * TA, TA)], res[s][:]).then_inc(stored[s], 16)

                        load(0, 0, 0, 1)
                        load(1, 0, 0, 1)
                        load(0, 0, 1, 2)
                        load(1, 0, 1, 2)
                        store(0, 1)
                        for k in range(NP):
                            with sp.Fori(0 if k else 2, HALF) as j:
                                it = j + (k * HALF + 1)
                                load(0, k, j, it)
                                store(1, it - 2)
                                load(1, k, j, it)
                                store(0, it - 1)
                        store(1, T - 1)
                        store(0, T)
                        store(1, T)
                        for s in range(SLOTS):
                            sp.wait_ge(stored[s], 16 * (T + 1))

                    @block.gpsimd
                    def _(pool):
                        for s in range(SLOTS):
                            nc.gpsimd.memset(xw[s][:], 0.0).then_inc(pads_zero, 1)
                            nc.gpsimd.memset(pr[s][:], 0.0).then_inc(pads_zero, 1)

                    @block.scalar
                    def _(act):
                        a = nc.scalar.activation

                        def half(s, it, m, im):
                            if m is not None:
                                act.wait_ge(small[m], SMALL * im + 3)
                                a(ex[m][:], lg[m][:], ACT.Exp).then_inc(expl_ready[m], 1)
                            if s is not None:
                                act.wait_ge(xc_ready[s], it + 1)
                                a(sq[s][:], pa[s][:, 0:TA], ACT.Square).then_inc(sq_ready[s], 1)
                                act.wait_ge(var_ready[s], it + 1)
                                a(sq[s][:], pb[s][:, 0:TA], ACT.Ln, bias=eps_6[:]).then_inc(ln_ready[s], 1)
                                act.wait_ge(ln_ready[s], it + 1)
                                a(sq[s][:], sq[s][:], ACT.Exp, scale=-0.5).then_inc(rstd_ready[s], 1)
                                act.wait_ge(t_ready[s], it + 1)
                                a(ts[s][:].rearrange("p w t -> p (w t)"), pb[s][:, 0:NWA * WP], ACT.Copy).then_inc(ts_ready[s], 1)
                            if m is not None:
                                act.wait_ge(gtr_ready[m], im + 1)
                                a(gt[m][:].rearrange("g (r w) -> g r w", r=WIN),
                                  pb[m][0:48, 0:WIN * P].rearrange("g (r w) -> g r w", r=WIN)[:, :, 0:W], ACT.Copy).then_inc(gt_ready[m], 1)
                            if s is not None:
                                act.wait_ge(sub_ready[s], it + 1)
                                a(pr[s][:, :, 0:WT], pr[s][:, :, 0:WT], ACT.Exp).then_inc(exp_ready[s], 1)
                                act.wait_ge(tr_ready[s], it + 1)
                                a(pt[s][:].rearrange("p w t -> p (w t)"), pb[s][:, 0:NWA * WP], ACT.Copy).then_inc(pt_ready[s], 1)
                                act.wait_ge(xc2_ready[s], it + 1)
                                a(sq[s][:], pa[s][:, 0:TA], ACT.Square).then_inc(sq2_ready[s], 1)
                                act.wait_ge(var2_ready[s], it + 1)
                                a(sq[s][:], pb[s][:, 0:TA], ACT.Ln, bias=eps_bn[:]).then_inc(ln2_ready[s], 1)
                                act.wait_ge(ln2_ready[s], it + 1)
                                a(sq[s][:], sq[s][:], ACT.Exp, scale=-0.5).then_inc(rstd2_ready[s], 1)

                        nc.scalar.preload_act_table_set("natural_log_exp_and_others")
                        act.wait_ge(pads_zero, 2 * SLOTS)
                        halves(act, half)

                    @block.vector
                    def _(dve):
                        v = nc.vector
                        shape = [W, 2 * WIN, NE]
                        rank = rank8[0:W, :].unsqueeze(1).broadcast_to(shape)
                        bias = b_router[0:W, :].unsqueeze(1).broadcast_to(shape)

                        def half(s, it, m, im):
                            if s is not None:
                                score = pa[s][:].rearrange("p (w t) -> p w t", t=WP)[:, :, 0:WT]
                                row_max = mx[s][:].unsqueeze(2).broadcast_to([P, NWA, WT])
                            if m is not None:
                                wide = g1[m][:].unsqueeze(2).broadcast_to(shape)

                            def part(n):
                                return g3[m][:, :, 16 * n:16 * n + 16]

                            def rows(t):
                                return t[:].rearrange("p (r i) e -> p r (i e)", i=2)

                            def chain(n):
                                dve.wait_ge(small[m], SMALL * im + n)

                            def experts(lo, hi):
                                for x in range(lo, hi):
                                    dve.wait_ge(gate_ready[m], NE * im + x + 1)
                                    if x >= 2:
                                        dve.wait_ge(moe_ready[m], NE * im + x - 1)
                                    v.tensor_tensor(xg[2 * m + x % 2][:], xn[m][:], pb[m][:, 0:TA], ALU.mult).then_inc(xg_ready[m], 1)

                            if m is not None:
                                dve.wait_ge(rout_ready[m], im + 1)
                                v.tensor_tensor(lg[m][:], pa[m][0:W, 0:2 * WIN * NE].rearrange("p (r e) -> p r e", e=NE), bias,
                                                ALU.add).then_inc(small[m], 1)
                                chain(1)
                                v.tensor_reduce(g1[m][:], lg[m][:], AX.X, ALU.max).then_inc(small[m], 1)
                                chain(2)
                                v.tensor_tensor(lg[m][:], lg[m][:], wide, ALU.subtract).then_inc(small[m], 1)
                                chain(3)
                                v.scalar_tensor_tensor(cd[m][:], lg[m][:], 0.0, rank, ALU.is_ge, ALU.mult).then_inc(small[m], 1)
                                chain(4)
                                v.tensor_reduce(g1[m][:], cd[m][:], AX.X, ALU.max).then_inc(small[m], 1)
                                chain(5)
                                v.tensor_tensor(o1[m][:], cd[m][:], wide, ALU.is_equal).then_inc(small[m], 1)
                                dve.wait_ge(expl_ready[m], im + 1)
                                chain(6)
                                v.scalar_tensor_tensor(lg[m][:], o1[m][:], -BIG, lg[m][:], ALU.mult, ALU.add).then_inc(small[m], 1)
                                chain(7)
                                v.tensor_reduce(g1[m][:], lg[m][:], AX.X, ALU.max).then_inc(small[m], 1)
                                chain(8)
                                v.tensor_tensor(cd[m][:], lg[m][:], wide, ALU.is_ge).then_inc(small[m], 1)
                                chain(9)
                                v.tensor_tensor(cd[m][:], cd[m][:], rank, ALU.mult).then_inc(small[m], 1)
                                chain(10)
                                v.tensor_reduce(g1[m][:], cd[m][:], AX.X, ALU.max).then_inc(small[m], 1)
                                chain(11)
                                v.tensor_tensor(o2[m][:], cd[m][:], wide, ALU.is_equal).then_inc(small[m], 1)
                                chain(12)
                                v.tensor_tensor(o1[m][:], o1[m][:], o2[m][:], ALU.add).then_inc(small[m], 1)
                                chain(13)
                                v.tensor_tensor(o1[m][:], o1[m][:], ex[m][:], ALU.mult).then_inc(small[m], 1)
                                chain(14)
                                v.tensor_reduce(g1[m][:], o1[m][:], AX.X, ALU.add).then_inc(small[m], 1)
                                chain(15)
                                v.reciprocal(g1[m][:], g1[m][:]).then_inc(small[m], 1)
                            if s is not None:
                                dve.wait_ge(rstd_ready[s], it + 1)
                                for side in range(2):
                                    ws = slice(side * (NWA // 2), (side + 1) * (NWA // 2))
                                    v.tensor_tensor(by_win(xw[s][:, side::2, :]), win(pa[s][:, 0:TA])[:, :, ws], win(sq[s])[:, :, ws],
                                                    ALU.mult).then_inc(xw_ready[s], 1)
                            if m is not None:
                                chain(16)
                                v.tensor_tensor(o1[m][:], o1[m][:], wide, ALU.mult).then_inc(small[m], 1)
                                chain(17)
                                v.tensor_copy(part(0), rows(o1[m])).then_inc(small[m], 1)
                                chain(18)
                                v.tensor_tensor(rows(cd[m]), rows(o1[m]), part(0), ALU.subtract).then_inc(small[m], 1)
                                chain(19)
                                v.tensor_copy(part(1), rows(cd[m])).then_inc(small[m], 1)
                                chain(20)
                                v.tensor_tensor(part(2), rows(cd[m]), part(1), ALU.subtract).then_inc(small[m], 1)
                                experts(0, 1)
                            if s is not None:
                                dve.wait_ge(score_ready[s], it + 1)
                                v.tensor_reduce(mx[s][:], score, AX.X, ALU.max).then_inc(max_ready[s], 1)
                            if m is not None:
                                experts(1, 2)
                            if s is not None:
                                dve.wait_ge(max_ready[s], it + 1)
                                v.tensor_tensor(pr[s][:, :, 0:WT], score, row_max, ALU.subtract).then_inc(sub_ready[s], 1)
                            if m is not None:
                                experts(2, 3)
                            if s is not None:
                                dve.wait_ge(exp_ready[s], it + 1)
                                v.tensor_reduce(sm[s][:], pr[s][:, :, 0:WT], AX.X, ALU.add).then_inc(sum_ready[s], 1)
                                dve.wait_ge(sum_ready[s], it + 1)
                                v.reciprocal(mx[s][:], sm[s][:]).then_inc(rec_ready[s], 1)
                                dve.wait_ge(rec_ready[s], it + 1)
                                v.tensor_tensor(pr[s][:, :, 0:WT], pr[s][:, :, 0:WT], row_max, ALU.mult).then_inc(prob_ready[s], 1)
                            if m is not None:
                                experts(3, 4)
                            if s is not None:
                                dve.wait_ge(v_ready[s], it + 1)
                                v.tensor_tensor(vw[s][:], pa[s][:, 0:NWA * WP].rearrange("p (w t) -> p w t", t=P),
                                                shift[:].unsqueeze(1).broadcast_to([P, NWA // 2, P]), ALU.add).then_inc(vw_ready[s], 1)
                            if m is not None:
                                experts(4, 6)
                            if s is not None:
                                dve.wait_ge(o_ready[s], it + 1)
                                v.tensor_tensor(win(x1[s]), by_win(pb[s][:].rearrange("p (w t) -> p w t", t=WP)), win(xt[s]),
                                                ALU.add).then_inc(x1_ready[s], 1)
                            if m is not None:
                                experts(6, 8)
                            if s is not None:
                                dve.wait_ge(rstd2_ready[s], it + 1)
                                v.tensor_tensor(xn[s][:], pa[s][:, 0:TA], sq[s][:], ALU.mult).then_inc(xn_ready[s], 1)
                            if m is not None:
                                dve.wait_ge(acc_ready[m], im + 1)
                                dve.wait_ge(stored[m], 16 * im)
                                v.tensor_tensor(res[m][:], pa[m][:, 0:TA], x1[m][:], ALU.add).then_inc(res_ready[m], 1)

                        dve.wait_ge(pads_zero, 2 * SLOTS)
                        halves(dve, half)

                    @block.tensor
                    def _(pe):
                        mm = nc.tensor.matmul

                        def strip(dst, weight, src):
                            for a, b in banks(TA):
                                last = mm(dst[:, a:b], weight, src[:, a:b], start=True, stop=True)
                            return last

                        def half(s, it, m, im):
                            def spread_gate(x):
                                for a, b in banks(TA):
                                    last = mm(pb[m][:, a:b], pick[:, x, :], gt[m][:, a:b], start=True, stop=True)
                                last.then_inc(gate_ready[m], 1)

                            def experts(lo, hi):
                                for x in range(lo, hi):
                                    pe.wait_ge(xg_ready[m], NE * im + x + 1)
                                    if x < NE - 1:
                                        spread_gate(x + 1)
                                    for a, b in banks(TA):
                                        last = mm(pa[m][:, a:b], w_exp[:, x, :], xg[2 * m + x % 2][:, a:b],
                                                  start=(x == 0), stop=False)
                                    last.then_inc(moe_ready[m], 1)

                            if s is not None:
                                pe.wait_ge(x_loaded[s], 16 * it + 16)
                                pe.wait_ge(res_ready[s], it)
                                strip(pa[s], center[:], xt[s]).then_inc(xc_ready[s], 1)
                                pe.wait_ge(sq_ready[s], it + 1)
                                strip(pb[s], average[:], sq[s]).then_inc(var_ready[s], 1)
                                pe.wait_ge(xw_ready[s], 2 * it + 2)
                                for a, b in banks(NWA * WP):
                                    last = mm(pb[s][:, a:b], w_qk[:], xw[s][:].rearrange("p w t -> p (w t)")[:, a:b],
                                              start=True, stop=True)
                                last.then_inc(t_ready[s], 1)
                            if m is not None:
                                pe.wait_ge(small[m], SMALL * im + SMALL)
                                for r in range(WIN):
                                    last = mm(pb[m][0:48, r * P:r * P + W], g3[m][:, r, :], ident_bf[0:W, 0:W],
                                              start=True, stop=True)
                                last.then_inc(gtr_ready[m], 1)
                                pe.wait_ge(gt_ready[m], im + 1)
                                spread_gate(0)
                            if s is not None:
                                pe.wait_ge(pads_zero, 2 * SLOTS)
                                pe.wait_ge(ts_ready[s], it + 1)
                                for w in range(NWA):
                                    for i in range(2):
                                        r = slice(C * i, C * i + C)
                                        last = mm(pa[s][r, w * WP:w * WP + WT], ts[s][r, w, :], xw[s][r, w, 0:WT],
                                                  start=True, stop=True)
                                last.then_inc(score_ready[s], 1)
                            if m is not None:
                                experts(0, 2)
                            if s is not None:
                                pe.wait_ge(sub_ready[s], it + 1)
                                for w in range(NWA // 2):
                                    last = mm(pa[s][:, w * P:(w + 1) * P], xw[s][:, 2 * w:2 * w + 2, :].rearrange("p w t -> p (w t)"),
                                              w_vo[:], start=True, stop=True)
                                last.then_inc(v_ready[s], 1)
                            if m is not None:
                                experts(2, 3)
                            if s is not None:
                                pe.wait_ge(prob_ready[s], it + 1)
                                for w in range(NWA // 2):
                                    last = nc.tensor.transpose(pb[s][:, w * P:(w + 1) * P],
                                                               pr[s][:, 2 * w:2 * w + 2, :].rearrange("p w t -> p (w t)"), ident[:])
                                last.then_inc(tr_ready[s], 1)
                            if m is not None:
                                experts(3, 5)
                            if s is not None:
                                pe.wait_ge(pads_zero, 2 * SLOTS)
                                pe.wait_ge(pt_ready[s], it + 1)
                                pe.wait_ge(vw_ready[s], it + 1)
                                for w in range(NWA):
                                    side, q = w // (NWA // 2), w % (NWA // 2)
                                    h = slice(WP * side, WP * side + WP)
                                    for i in range(2):
                                        last = mm(pb[s][C * i:C * i + C, w * WP:w * WP + WT], vw[s][h, q, C * i:C * i + C],
                                                  pt[s][h, q, WP * i:WP * i + WT], start=True, stop=True)
                                last.then_inc(o_ready[s], 1)
                            if m is not None:
                                experts(5, 6)
                            if s is not None:
                                pe.wait_ge(x1_ready[s], it + 1)
                                strip(pa[s], center[:], x1[s]).then_inc(xc2_ready[s], 1)
                            if m is not None:
                                experts(6, 7)
                            if s is not None:
                                pe.wait_ge(sq2_ready[s], it + 1)
                                strip(pb[s], average[:], sq[s]).then_inc(var2_ready[s], 1)
                            if m is not None:
                                experts(7, 8)
                                for n in range(3):
                                    for a, b in banks(TA):
                                        last = mm(pa[m][:, a:b], b_exp3[:, n, :], gt[m][:, a:b], start=False, stop=(n == 2))
                                last.then_inc(acc_ready[m], 1)
                            if s is not None:
                                pe.wait_ge(xn_ready[s], it + 1)
                                for r in range(WIN):
                                    last = mm(pa[s][0:W, r * 2 * NE:(r + 1) * 2 * NE], xn[s][:, r * W:(r + 1) * W], w_router[:],
                                              start=True, stop=True)
                                last.then_inc(rout_ready[s], 1)

                        pe.wait_ge(pads_zero, 2 * SLOTS)
                        halves(pe, half)

        def phase_b():
            N = NP * SB

            final = ("out", "xc2", "var2", "lgp", "tok0", "tok1")
            ahead = ("xc", "var", "conv0", "conv1", "z0", "z1", "pre0", "xp0",
                     "ndt0", "ndt1", "ndt2", "ndu0", "nB")
            core0 = ("du1", "C0", "du2", "dt3", "du3", "B1", "C1", "pre1", "xp1", "B2", "out", "C2", "xc", "xc2",
                     "var", "var2", "B3", "C3", "ndt0", "ndt1", "ndt2", "ndu0", "nB", "lgp", "tok0", "tok1")
            core1 = ("du1", "C0", "du2", "dt3", "du3", "B1", "C1", "conv0", "conv1", "z0", "B2", "z1", "pre0",
                     "C2", "B3", "C3", "xp0", "ndt0", "ndt1", "ndt2", "ndu0", "nB")
            whole = [(0, n) for n in core0] + [(1, n) for n in core1]
            first_turn = [(0, n) for n in core0 if n not in final]
            last_turn = ([(0, n) for n in core0 if n not in ("xc", "var")] +
                         [(1, n) for n in core1 if n not in ahead] + [(2, n) for n in final])
            TURN = len(whole)
            NW = 3
            SL = NWB * (CONV - 1 + ST)
            assert TURN % NW == 0 and N >= 3
            MIDDLE, FIRST, LAST = "middle", "first", "last"

            def place(core, name, it, kind):
                if core == -1:
                    c = ahead.index(name)
                elif core == 0 and kind == FIRST:
                    c = len(ahead) + first_turn.index((0, name))
                elif kind == LAST:
                    c = len(ahead) - len(final) + TURN * (N - 1) + last_turn.index((core, name))
                else:
                    c = len(ahead) - len(final) - TURN + whole.index((core, name))
                    return c % NW, it * (TURN // NW) + c // NW
                return c % NW, c // NW

            with ExitStack() as st:
                def sb(name, shape, dt=F32):
                    return sbuf("b_" + name, shape, dt, st)

                def ring(name, n):
                    return [sb(f"{name}{i}", [P, TB]) for i in range(n)]

                def sem(name, turn=1):
                    return new_sem("b_" + name, turn)

                def sems(name, n=2, turn=1):
                    return [sem(f"{name}{i}", turn) for i in range(n)]

                xt = sb("x", [P, TB])
                xr = sb("xr", [P, TB])
                sq = sb("sq", [P, TB])
                xc = sb("xc", [P, TB])
                seq = [sb(f"seq{i}", [P, NWB, CONV - 1 + ST]) for i in range(2)]
                resets = sb("resets", [P, NWB])
                x3s = sb("x3s", [P, TB])
                sq2 = sb("sq2", [P, TB])
                xl = sb("xl", [P, TB])
                lg = sb("lg", [2 * EC, TB])
                tok = sb("tok", [P, TB])
                gate = ring("gate", 2)
                gate_next = sb("gate_next", [P, TB])
                yz = ring("yz", 2)
                u = ring("u", 2)
                dt = ring("dt", 2)
                dtu = ring("dtu", 2)
                rest = sq
                parts = [sb(f"parts{i}", [P, TB], BF16) for i in range(2)]
                dts = ring("dts", 4)
                dus = ring("dus", 4)
                bt = ring("bt", 2)
                ct = ring("ct", 2)
                aa = ring("a", RA)
                hh = ring("h", RH)
                hc = ring("hc", RC)
                ww = [psum(f"b_w{i}", [P, 2 * BANK], F32, st) for i in range(NW)]
                yy = psum("b_y", [P, 2 * BANK], F32, st)

                pads_zero = sem("pads", 0)
                x_loaded, xr_loaded, x3_stored, lg_stored = (sem(n, 16) for n in ("loaded", "xrl", "x3st", "lgst"))
                tok_stored = sem("tokst", 32)
                shifted = sem("shifted", 32)
                made = sems("made", NW)
                moved = sems("moved", NW)
                sq_ready, rstd_ready, xn_ready = (sem(n) for n in ("sq", "rstd", "xn"))
                seq_ready = sems("seq")
                abs_ready, e_ready, l_ready, dt_ready, dtu_ready, reset_ready = (
                    sems(n) for n in ("abs", "e", "l", "dt", "dtu", "reset"))
                high_ready, mid_ready, parts_ready, skip_ready, yz_ready = (
                    sems(n) for n in ("high", "mid", "parts", "skip", "yz"))
                a_ready = sems("a", RA, TILES // RA)
                b_ready, h_ready = (sems(n, RH, TILES // RH) for n in ("b", "h"))
                hc_ready = sems("hc", RC, TILES // RC)
                gate1_ready = sem("gate1")
                folded = sem("fold", 8)
                sq2_ready, rstd2_ready, xl_ready = (sem(n) for n in ("sq2", "rstd2", "xl"))
                nc.all_engine_barrier()

                def win(t):
                    return t[:, 0:TB].rearrange("p (r w c) -> p r w c", r=WS, c=WS)

                def seqs(t):
                    return t[:, 0:TB].rearrange("p (w r c) -> p r w c", r=WS, c=WS)

                tokens_v = tokens.rearrange("(i r p) c -> i p r c", i=2, p=P)

                def used(it, s, n):
                    return it * (TILES // n) + s // n

                def wait_made(eng, core, name, it, kind):
                    w, c = place(core, name, it, kind)
                    eng.wait_ge(made[w], c + 2)
                    return ww[w]

                def wait_moved(eng, core, name, it, kind):
                    w, c = place(core, name, it, kind)
                    eng.wait_ge(moved[w], c + 2)

                def read(core, name, it, kind):
                    return moved[place(core, name, it, kind)[0]]

                def before(i, it, kind):
                    if i:
                        return 0, it, kind
                    return (-1, it, kind) if kind == FIRST else (1, it - 1, MIDDLE)

                def wait_spread(eng, name, t, i, it, kind):
                    if t < (3 if name == "dt" else 1):
                        wait_moved(eng, before(i, it, kind)[0], f"n{name}{t}", *before(i, it, kind)[1:])
                    elif t < 4:
                        wait_moved(eng, i, f"{name}{t}", it, kind)

                def wait_block(eng, name, t, i, it, kind):
                    if t == 0 and name == "B":
                        wait_moved(eng, before(i, it, kind)[0], "nB", *before(i, it, kind)[1:])
                    elif t % 4 == 0:
                        wait_moved(eng, i, f"{name}{t // 4}", it, kind)

                with nc.Block() as block:
                    @block.sync
                    def _(sp):
                        def turn(it, kind):
                            p = it - 1
                            if kind != LAST:
                                sp.wait_ge(sq_ready, it + 1)
                                sp.dma_start(xt[:], x2[:, bass.ds((p + 1) * TB, TB)]).then_inc(x_loaded, 16)
                            if kind != FIRST:
                                store(0, it, kind)
                            if kind != LAST:
                                shift_seq(it + 1)
                            if kind != FIRST:
                                store_rest(0, it, kind)
                            sp.dma_start(xr[:], x2[:, bass.ds(p * TB, TB)]).then_inc(xr_loaded, 16)

                        def shift_seq(o):
                            sp.wait_ge(seq_ready[0], o + 1)
                            sp.wait_ge(seq_ready[1], o + 1)
                            for i in range(2):
                                flat = seq[i][:].rearrange("p w t -> p (w t)")
                                sp.dma_start(flat[C * (1 - i):C * (1 - i) + C, 0:SL - 2],
                                             flat[C * i:C * i + C, 2:SL]).then_inc(shifted, 16)

                        def store(core, it, kind):
                            p = it - 2
                            wait_moved(sp, core, "out", it - (core == 2), kind)
                            sp.dma_start(x3[:, bass.ds(p * TB, TB)], x3s[:]).then_inc(x3_stored, 16)

                        def store_rest(core, it, kind):
                            p = it - 2
                            wait_moved(sp, core, "lgp", it - (core == 2), kind)
                            sp.dma_start(logits[:, bass.ds(p * TB, TB)], lg[:]).then_inc(lg_stored, 16)
                            wait_moved(sp, core, "tok1", it - (core == 2), kind)
                            for i in range(2):
                                sp.dma_start(tokens_v[i, :, bass.ds(p * NCH, NCH), :],
                                             tok[:].rearrange("p (n i c) -> p n i c", i=2, c=C)[:, :, i, :]).then_inc(tok_stored, 16)

                        sp.dma_start(xt[:], x2[:, 0:TB]).then_inc(x_loaded, 16)
                        shift_seq(1)
                        turn(1, FIRST)
                        with sp.Fori(2, N) as it:
                            turn(it, MIDDLE)
                        turn(N, LAST)
                        store(2, N + 1, LAST)
                        store_rest(2, N + 1, LAST)
                        sp.wait_ge(x3_stored, 16 * (N + 1))
                        sp.wait_ge(lg_stored, 16 * (N + 1))
                        sp.wait_ge(tok_stored, 32 * (N + 1))

                    @block.gpsimd
                    def _(pool):
                        def tile(t, i, it, kind):
                            s = UNIT * i + t
                            wait_block(pool, "C", t, i, it, kind)
                            pool.wait_ge(h_ready[s % RH], used(it, s, RH) + 1)
                            if t % 4 == 0:
                                pool.wait_ge(folded, 8 * it + s // 4 - RC // 4 + 1)
                            nc.gpsimd.tensor_tensor(hc[s % RC][:], hh[s % RH][:], ct[t // 4 % 2][:], ALU.mult).then_inc(hc_ready[s % RC], 1)

                        def products(i, o):
                            pool.wait_ge(dt_ready[i], o + 1)
                            nc.gpsimd.tensor_tensor(dtu[i][:], dt[i][:], u[i][:], ALU.mult).then_inc(dtu_ready[i], 1)
                            pool.wait_ge(dtu_ready[i], o + 1)
                            first = dt[i][:].rearrange("p (w t) -> p w t", t=ST)[:, :, 0]
                            nc.gpsimd.tensor_tensor(first, first, resets[:], ALU.add).then_inc(reset_ready[i], 1)

                        def turn(it, kind):
                            for i in range(2):
                                for t in range(UNIT):
                                    tile(t, i, it, kind)
                                    if i == 0 and t == 7:
                                        products(1, it)
                                    if i and kind != LAST and t == 9:
                                        products(0, it + 1)

                        for i in range(2):
                            nc.gpsimd.memset(seq[i][:], 0.0).then_inc(pads_zero, 1)
                        nc.gpsimd.memset(resets[:], RESET).then_inc(pads_zero, 1)
                        pool.wait_ge(pads_zero, 3)
                        products(0, 1)
                        turn(1, FIRST)
                        with pool.Fori(2, N) as it:
                            turn(it, MIDDLE)
                        turn(N, LAST)

                    @block.scalar
                    def _(act):
                        a = nc.scalar.activation

                        def move(core, name, it, kind, dst, func=ACT.Copy, rows=P, cols=slice(0, TB), **more):
                            w = wait_made(act, core, name, it, kind)
                            a(dst, w[0:rows, cols], func, **more).then_inc(read(core, name, it, kind), 1)

                        def move_dt(core, b, name, it, kind, s):
                            act.wait_ge(a_ready[s % RA], used(it, s, RA) + 1)
                            move(core, f"{name}{b}", it, kind, dts[b][:])

                        def move_du(core, b, name, it, kind, s):
                            act.wait_ge(b_ready[s % RH], used(it, s, RH) + 1)
                            move(core, f"{name}{b}", it, kind, dus[b][:])

                        def move_block(core, name, m, it, kind, i, cur):
                            if cur is not None:
                                s = UNIT * i + 4 * (m - 2) + 3
                                if "B" in name:
                                    act.wait_ge(b_ready[s % RH], used(cur, s, RH) + 1)
                                else:
                                    act.wait_ge(hc_ready[s % RC], used(cur, s, RC) + 1)
                            move(core, name, it, kind, (bt if "B" in name else ct)[m % 2][:])

                        def norm_start(core, it, kind, o):
                            act.wait_ge(seq_ready[1], o)
                            act.wait_ge(parts_ready[1], o)
                            w = wait_made(act, core, "xc", it, kind)
                            a(sq[:], w[:, 0:TB], ACT.Square).then_inc(sq_ready, 1)
                            a(xc[:], w[:, 0:TB], ACT.Copy).then_inc(read(core, "xc", it, kind), 1)

                        def norm_ends(core, it, kind, names):
                            steps = {"var": (sq, eps_6, rstd_ready), "var2": (sq2, eps_bn, rstd2_ready)}
                            for name in names:
                                move(core, name, it, kind, steps[name][0][:], ACT.Ln, bias=steps[name][1][:])
                            for name in names:
                                wait_moved(act, core, name, it, kind)
                                a(steps[name][0][:], steps[name][0][:], ACT.Exp, scale=-0.5).then_inc(steps[name][2], 1)

                        def silus(core, it, kind, o):
                            for i in range(2):
                                act.wait_ge(skip_ready[i], o)
                                act.wait_ge(dtu_ready[i], o)
                                move(core, f"conv{i}", it, kind, u[i][:], ACT.Silu, bias=conv_bias[:])

                        def gate_silus(core, it, kind, o):
                            act.wait_ge(yz_ready[0], o)
                            move(core, "z0", it, kind, gate[0][:], ACT.Silu)
                            act.wait_ge(gate1_ready, o)
                            move(core, "z1", it, kind, gate_next[:], ACT.Silu)
                            nc.scalar.preload_act_table_set("natural_log_exp_and_others")

                        def softplus_start(core, it, kind, i):
                            w = wait_made(act, core, f"pre{i}", it, kind)
                            a(dtu[i][:], w[:, 0:TB], ACT.Abs, bias=dt_bias[:]).then_inc(abs_ready[i], 1)
                            if i:
                                a(dt[i][:], w[:, 0:TB], ACT.Relu, bias=dt_bias[:]).then_inc(read(core, f"pre{i}", it, kind), 1)

                        def softplus_exp(i, o):
                            act.wait_ge(abs_ready[i], o + 1)
                            a(dtu[i][:], dtu[i][:], ACT.Exp, scale=-1.0).then_inc(e_ready[i], 1)

                        def softplus_ln(i, o):
                            act.wait_ge(e_ready[i], o + 1)
                            a(dtu[i][:], dtu[i][:], ACT.Ln, bias=one_col[:]).then_inc(l_ready[i], 1)

                        def high_part(core, it, kind, i):
                            w = wait_made(act, core, f"xp{i}", it, kind)
                            a(parts[i][:], w[:, 0:TB], ACT.Copy).then_inc(high_ready[i], 1)

                        def final_norm_start(core, it, kind):
                            w = wait_made(act, core, "xc2", it, kind)
                            a(sq2[:], w[:, 0:TB], ACT.Square).then_inc(sq2_ready, 1)
                            a(xl[:], w[:, 0:TB], ACT.Copy).then_inc(read(core, "xc2", it, kind), 1)

                        def final_moves(core, it, kind, o):
                            act.wait_ge(lg_stored, 16 * o)
                            move(core, "lgp", it, kind, lg[:], ACT.Identity, rows=2 * EC, bias=b_gate[:])
                            act.wait_ge(tok_stored, 32 * o)
                            move(core, "tok0", it, kind, tok[:, 0:BANK], cols=slice(0, BANK))
                            move(core, "tok1", it, kind, tok[:, BANK:TB], cols=slice(0, TB - BANK))

                        def core(i, it, kind):
                            prepares = i == 1 and kind != LAST
                            norms = i == 0 and kind != LAST
                            finals = i == 0 and kind != FIRST
                            here = (i, it, kind)
                            for t in range(UNIT):
                                s = UNIT * i + t
                                wait_spread(act, "dt", t, *here)
                                act.wait_ge(h_ready[(s - RA) % RH], used(it, s - RA, RH) + 1)
                                a(aa[s % RA][:], dts[t % 4][:], ACT.Exp,
                                  scale=decay[:, t % 4, t // 4:t // 4 + 1]).then_inc(a_ready[s % RA], 1)
                                if t in (0, 1, 2):
                                    move_du(i, t + 1, "du", it, kind, s - 3)
                                if t == 0:
                                    move_block(i, "C0", 0, it, kind, i, it)
                                if t == 1:
                                    move_dt(i, 3, "dt", it, kind, s - 2)
                                if t == 2:
                                    move_block(i, "B1", 1, it, kind, i, it)
                                if t == 4:
                                    move_block(i, "C1", 1, it, kind, i, it)
                                if i == 0 and t == 3:
                                    softplus_start(*here, 1)
                                    high_part(*here, 1)
                                if i == 0 and t == 4:
                                    softplus_exp(1, it)
                                if i == 0 and t == 5:
                                    softplus_ln(1, it)
                                if t == 7 and prepares:
                                    silus(*here, it + 1)
                                if t == 6 + i:
                                    move_block(i, "B2", 2, it, kind, i, it)
                                if t == 7 and prepares:
                                    gate_silus(*here, it + 1)
                                if t == 8 and prepares:
                                    softplus_start(*here, 0)
                                if t == 7 + i:
                                    move_block(i, "C2", 2, it, kind, i, it)
                                if t == 7 and norms:
                                    norm_start(*here, it + 1)
                                if t == 8 and finals:
                                    final_norm_start(*here)
                                if t == 9 and i == 0:
                                    norm_ends(*here, ["var"] * norms + ["var2"] * finals)
                                if t == 8 and prepares:
                                    softplus_exp(0, it + 1)
                                if t == 9 and prepares:
                                    softplus_ln(0, it + 1)
                                if t == 10:
                                    move_block(i, "B3", 3, it, kind, i, it)
                                if t == 11:
                                    move_block(i, "C3", 3, it, kind, i, it)
                                    if prepares:
                                        high_part(*here, 0)
                                if t >= 13 and i == 0:
                                    move_dt(i, t - 13, "ndt", it, kind, s - 1)
                                if t == 15 and not (kind == LAST and i):
                                    for b in range(3 * i):
                                        move_dt(i, b, "ndt", it, kind, UNIT * i + 12 + b)
                                    move_du(i, 0, "ndu", it, kind, UNIT * i + 12)
                                    move_block(i, "nB", 4, it, kind, i, it)
                                if t == 15 and finals:
                                    final_moves(*here, it - 1)

                        nc.scalar.preload_act_table_set("natural_log_exp_and_others")
                        here = (-1, 0, FIRST)
                        norm_start(*here, 1)
                        norm_ends(*here, ["var"])
                        silus(*here, 1)
                        gate_silus(*here, 1)
                        softplus_start(*here, 0)
                        softplus_exp(0, 1)
                        softplus_ln(0, 1)
                        high_part(*here, 0)
                        for b in range(3):
                            move(-1, f"ndt{b}", 0, FIRST, dts[b][:])
                        move(-1, "ndu0", 0, FIRST, dus[0][:])
                        move(-1, "nB", 0, FIRST, bt[0][:])
                        for i in range(2):
                            core(i, 1, FIRST)
                        with act.Fori(2, N) as it:
                            for i in range(2):
                                core(i, it, MIDDLE)
                        for i in range(2):
                            core(i, N, LAST)
                        final_norm_start(2, N, LAST)
                        norm_ends(2, N, LAST, ["var2"])
                        final_moves(2, N, LAST, N)

                    @block.vector
                    def _(dve):
                        v = nc.vector

                        def inputs(t, i, it, kind):
                            s = UNIT * i + t
                            wait_spread(dve, "du", t, i, it, kind)
                            wait_block(dve, "B", t, i, it, kind)
                            dve.wait_ge(hc_ready[(s - RH) % RC], used(it, s - RH, RC) + 1)
                            v.tensor_tensor(hh[s % RH][:], dus[t % 4][:], bt[t // 4 % 2][:], ALU.mult).then_inc(b_ready[s % RH], 1)

                        def scan(s, it):
                            dve.wait_ge(a_ready[s % RA], used(it, s, RA) + 1)
                            dve.wait_ge(b_ready[s % RH], used(it, s, RH) + 1)
                            v.tensor_tensor_scan(hh[s % RH][:], aa[s % RA][:], hh[s % RH][:], 0.0,
                                                 ALU.mult, ALU.add).then_inc(h_ready[s % RH], 1)

                        def norm(core, it, kind, o, seq_free):
                            dve.wait_ge(rstd_ready, o + 1)
                            wait_moved(dve, core, "xc", it, kind)
                            v.tensor_tensor(xc[:], xc[:], sq[:], ALU.mult).then_inc(xn_ready, 1)
                            dve.wait_ge(xn_ready, o + 1)
                            if seq_free:
                                wait_moved(dve, before(0, it, kind)[0], "z1", *before(0, it, kind)[1:])
                            for i in range(2):
                                q = slice(C * i, C * i + C)
                                v.tensor_tensor(seq[i][q, :, CONV - 1:].rearrange("p w (r c) -> p r w c", c=WS), win(xc)[q],
                                                pos_t[q].rearrange("p (r c) -> p r c", c=WS).unsqueeze(2).broadcast_to([C, WS, NWB, WS]),
                                                ALU.add).then_inc(seq_ready[i], 1)

                        def relu(i, o, cur):
                            dve.wait_ge(abs_ready[i], o + 1)
                            w = wait_made(dve, cur[0], f"pre{i}", *cur[1:])
                            v.tensor_scalar(dt[i][:], w[:, 0:TB], dt_bias[:, 0:1], 0.0, ALU.add, ALU.max).then_inc(
                                read(cur[0], f"pre{i}", *cur[1:]), 1)

                        def steps(i, o, cur):
                            dve.wait_ge(l_ready[i], o + 1)
                            wait_moved(dve, cur[0], f"pre{i}", *cur[1:])
                            v.tensor_tensor(dt[i][:], dt[i][:], dtu[i][:], ALU.add).then_inc(dt_ready[i], 1)

                        def low_parts(i, o, cur):
                            h = slice(C, P)
                            w = wait_made(dve, cur[0], f"xp{i}", *cur[1:])
                            dve.wait_ge(high_ready[i], o + 1)
                            dve.wait_ge(parts_ready[1 - i], o + i)
                            v.tensor_tensor(rest[h, :], w[h, 0:TB], parts[i][h, :], ALU.subtract).then_inc(read(cur[0], f"xp{i}", *cur[1:]), 1)
                            wait_moved(dve, cur[0], f"xp{i}", *cur[1:])
                            v.tensor_copy(parts[i][h, :], rest[h, :]).then_inc(mid_ready[i], 1)
                            dve.wait_ge(mid_ready[i], o + 1)
                            q = slice(96, P)
                            v.tensor_tensor(parts[i][q, :], rest[q, :], parts[i][q, :], ALU.subtract).then_inc(parts_ready[i], 1)

                        def gated(i, o, rows):
                            dve.wait_ge(folded, rows)
                            if i:
                                dve.wait_ge(gate1_ready, o + 1)
                            v.tensor_tensor(yz[i][:], yy[:, 0:TB], gate[i][:], ALU.mult).then_inc(yz_ready[i], 1)

                        def gate_over(it, kind):
                            wait_moved(dve, before(0, it, kind)[0], "z1", *before(0, it, kind)[1:])
                            dve.wait_ge(yz_ready[1], it)
                            v.tensor_copy(gate[1][:], gate_next[:]).then_inc(gate1_ready, 1)

                        def residual(core, it, kind, o):
                            w = wait_made(dve, core, "out", it, kind)
                            dve.wait_ge(x3_stored, 16 * o)
                            dve.wait_ge(xr_loaded, 16 * o + 16)
                            v.tensor_tensor(win(x3s), seqs(w), win(xr), ALU.add).then_inc(read(core, "out", it, kind), 1)

                        def final_norm(core, it, kind, o):
                            dve.wait_ge(rstd2_ready, o + 1)
                            wait_moved(dve, core, "xc2", it, kind)
                            v.tensor_tensor(xl[:], xl[:], sq2[:], ALU.mult).then_inc(xl_ready, 1)

                        def core(i, it, kind):
                            finals = kind != FIRST and i == 0
                            here = (i, it, kind)
                            for t in range(UNIT):
                                s = UNIT * i + t
                                inputs(t, *here)
                                if not (kind == FIRST and s == 0):
                                    scan(s - 1, it)
                                if t == 3 and not (kind == FIRST and i == 0):
                                    gated(1 - i, it - 1 + i, 8 * it + 4 * i)
                                if t == 5 and i == 0:
                                    gate_over(it, kind)
                                if t == 6 and finals:
                                    residual(*here, it - 1)
                                if t == 12 and i == 0 and kind != LAST:
                                    norm(*here, it + 1, True)
                                if t == 11 and finals:
                                    final_norm(*here, it - 1)
                                if t == 5 and i == 0:
                                    low_parts(1, it, here)
                                if t == 7 and i == 0:
                                    steps(1, it, here)
                                if t == 9 and i and kind != LAST:
                                    relu(0, it + 1, here)
                                if t == 10 and i and kind != LAST:
                                    steps(0, it + 1, here)
                                if t == 12 and i and kind != LAST:
                                    low_parts(0, it + 1, here)

                        dve.wait_ge(pads_zero, 3)
                        norm(-1, 0, FIRST, 1, False)
                        relu(0, 1, (-1, 0, FIRST))
                        steps(0, 1, (-1, 0, FIRST))
                        low_parts(0, 1, (-1, 0, FIRST))
                        for i in range(2):
                            core(i, 1, FIRST)
                        with dve.Fori(2, N) as it:
                            for i in range(2):
                                core(i, it, MIDDLE)
                        for i in range(2):
                            core(i, N, LAST)
                        scan(TILES - 1, N)
                        gated(1, N, 8 * N + 8)
                        residual(2, N, LAST, N)
                        final_norm(2, N, LAST, N)

                    @block.tensor
                    def _(pe):
                        mm = nc.tensor.matmul

                        def product(core, name, it, kind):
                            w, c = place(core, name, it, kind)
                            pe.wait_ge(moved[w], c + 1)
                            return ww[w]

                        def strip(core, name, it, kind, weight, src, rows=slice(0, P)):
                            w = product(core, name, it, kind)
                            for lo, hi in banks(TB):
                                last = mm(w[rows, lo:hi], weight, src[:, lo:hi], start=True, stop=True)
                            last.then_inc(made[place(core, name, it, kind)[0]], 1)

                        def windows(core, name, it, kind, src, weights, shifts):
                            w = product(core, name, it, kind)
                            for lo, hi in banks(TB):
                                for n, (weight, shift) in enumerate(zip(weights, shifts)):
                                    last = mm(w[:, lo:hi], weight, src[:, lo // ST:hi // ST, shift:shift + ST],
                                              start=(n == 0), stop=(n == len(weights) - 1))
                            last.then_inc(made[place(core, name, it, kind)[0]], 1)

                        def norm_start(core, it, kind, o):
                            pe.wait_ge(x_loaded, 16 * o + 16)
                            strip(core, "xc", it, kind, center[:], xt)

                        def norm_end(core, it, kind, o):
                            pe.wait_ge(sq_ready, o + 1)
                            strip(core, "var", it, kind, average[:], sq)

                        def conv(core, it, kind, i, o):
                            pe.wait_ge(shifted, 32 * o + 32)
                            windows(core, f"conv{i}", it, kind, seq[i], [w_conv[:, i, k, :] for k in range(CONV // 2)], range(CONV // 2))

                        def gate(core, it, kind, i):
                            windows(core, f"z{i}", it, kind, seq[i], [w_z[:, i, :]], [CONV - 1])

                        def pre(core, it, kind, i):
                            wait_moved(pe, *((core, f"conv{i}", it, kind) if i == 0 else
                                             (before(0, it, kind)[0], "conv1", *before(0, it, kind)[1:])))
                            strip(core, f"pre{i}", it, kind, w_dt_full[:], u[i])

                        def xp(core, it, kind, i):
                            strip(core, f"xp{i}", it, kind, w_bc[:].rearrange("p a n -> p (a n)"), u[i])

                        def spread_dt(core, b, name, it, kind, i):
                            strip(core, f"{name}{b}", it, kind, spread[:, b, :], dt[i])

                        def spread_du(core, b, name, it, kind, i):
                            strip(core, f"{name}{b}", it, kind, spread[:, b, :], dtu[i])

                        def state_block(core, name, m, it, kind, i, o=None):
                            if o is not None:
                                pe.wait_ge(parts_ready[i], o + 1)
                            strip(core, name, it, kind, rows_bc[:, m, :], parts[i])

                        def skip_start(i, it):
                            pe.wait_ge(yz_ready[1 - i], it + i)
                            for lo, hi in banks(TB):
                                last = mm(yy[:, lo:hi], skip[:], u[i][:, lo:hi], start=True, stop=False)
                            last.then_inc(skip_ready[i], 1)

                        def fold_row(i, it, row):
                            for b in range(4):
                                s = UNIT * i + 4 * row + b
                                pe.wait_ge(hc_ready[s % RC], used(it, s, RC) + 1)
                            for lo, hi in banks(TB):
                                for b in range(4):
                                    s = UNIT * i + 4 * row + b
                                    last = mm(yy[32 * b:32 * b + 32, lo:hi], fold[:], hc[s % RC][:, lo:hi],
                                              start=False, stop=(row == 3))
                            last.then_inc(folded, 1)

                        def out(core, it, kind, o):
                            for i in range(2):
                                pe.wait_ge(yz_ready[i], o + 1)
                            w = product(core, "out", it, kind)
                            for lo, hi in banks(TB):
                                for i in range(2):
                                    last = mm(w[C * i:C * i + C, lo:hi], w_out_t[:], yz[i][:, lo:hi], start=True, stop=True)
                            last.then_inc(made[place(core, "out", it, kind)[0]], 1)

                        def final_norm_start(core, it, kind, o):
                            wait_moved(pe, core, "out", it, kind)
                            strip(core, "xc2", it, kind, center[:], x3s)

                        def final_norm_end(core, it, kind, o):
                            pe.wait_ge(sq2_ready, o + 1)
                            strip(core, "var2", it, kind, average[:], sq2)

                        def final_products(core, it, kind, o):
                            pe.wait_ge(xl_ready, o + 1)
                            strip(core, "lgp", it, kind, w_gate[:], xl, rows=slice(0, 2 * EC))
                            for name, n0, n1 in (("tok0", 0, 4), ("tok1", 4, NCH)):
                                w = product(core, name, it, kind)
                                for n in range(n0, n1):
                                    last = nc.tensor.transpose(w[:, (n - n0) * P:(n - n0 + 1) * P], xl[:, n * P:(n + 1) * P], ident[:])
                                last.then_inc(made[place(core, name, it, kind)[0]], 1)

                        def core(i, it, kind):
                            prepares = i == 1 and kind != LAST
                            norms = i == 0 and kind != LAST
                            finals = i == 0 and kind != FIRST
                            n, o, here = 1 - i, it + i, (i, it, kind)
                            for t in range(UNIT):
                                if t == 0:
                                    spread_du(i, 1, "du", it, kind, i)
                                    state_block(i, "C0", 4, it, kind, i)
                                    spread_du(i, 2, "du", it, kind, i)
                                if t == 1:
                                    spread_dt(i, 3, "dt", it, kind, i)
                                    spread_du(i, 3, "du", it, kind, i)
                                    state_block(i, "B1", 1, it, kind, i)
                                if t == 2:
                                    state_block(i, "C1", 5, it, kind, i)
                                    if not (kind == FIRST and i == 0):
                                        fold_row(1 - i, it - (1 - i), 3)
                                    if prepares:
                                        conv(*here, 0, o)
                                        conv(*here, 1, o)
                                        skip_start(i, it)
                                if t == 4:
                                    if kind == LAST and i:
                                        skip_start(i, it)
                                    if i == 0:
                                        pre(*here, 1)
                                        xp(*here, 1)
                                    if prepares:
                                        gate(*here, 0)
                                    state_block(i, "B2", 2, it, kind, i)
                                    if prepares:
                                        gate(*here, 1)
                                if t == 5 and finals:
                                    out(*here, it - 1)
                                if t == 6:
                                    if i == 0:
                                        skip_start(i, it)
                                    if prepares:
                                        pre(*here, 0)
                                    state_block(i, "C2", 6, it, kind, i)
                                    if norms:
                                        norm_start(*here, it + 1)
                                if t == 7:
                                    fold_row(i, it, 0)
                                    if finals:
                                        final_norm_start(*here, it - 1)
                                if t == 8:
                                    if norms:
                                        norm_end(*here, it + 1)
                                    if finals:
                                        final_norm_end(*here, it - 1)
                                if t == 10:
                                    state_block(i, "B3", 3, it, kind, i)
                                    state_block(i, "C3", 7, it, kind, i)
                                    if prepares:
                                        xp(*here, 0)
                                if t == 11:
                                    fold_row(i, it, 1)
                                if t == 12 and not (kind == LAST and i):
                                    pe.wait_ge(reset_ready[n], o + 1)
                                    for b in range(3):
                                        spread_dt(i, b, "ndt", it, kind, n)
                                    spread_du(i, 0, "ndu", it, kind, n)
                                    state_block(i, "nB", 0, it, kind, n, o)
                                if t == 14 and finals:
                                    final_products(*here, it - 1)
                                if t == 15:
                                    fold_row(i, it, 2)

                        here = (-1, 0, FIRST)
                        norm_start(*here, 1)
                        norm_end(*here, 1)
                        conv(*here, 0, 1)
                        conv(*here, 1, 1)
                        gate(*here, 0)
                        gate(*here, 1)
                        pre(*here, 0)
                        xp(*here, 0)
                        pe.wait_ge(reset_ready[0], 2)
                        for b in range(3):
                            spread_dt(-1, b, "ndt", 0, FIRST, 0)
                        spread_du(-1, 0, "ndu", 0, FIRST, 0)
                        state_block(-1, "nB", 0, 0, FIRST, 0, 1)
                        for i in range(2):
                            core(i, 1, FIRST)
                        with pe.Fori(2, N) as it:
                            for i in range(2):
                                core(i, it, MIDDLE)
                        for i in range(2):
                            core(i, N, LAST)
                        fold_row(1, N, 3)
                        out(2, N, LAST, N)
                        final_norm_start(2, N, LAST, N)
                        final_norm_end(2, N, LAST, N)
                        final_products(2, N, LAST, N)

        def phase_c():
            IMG = min(4, B)
            R = IMG * EC
            CK = TB if HW // TB % 2 == 0 else TB // 2
            NK = HW // CK
            with ExitStack() as st:
                def sb(name, shape, dt=F32):
                    return sbuf("c_" + name, shape, dt, st)

                def sem(name, turn=0):
                    return new_sem("c_" + name, turn)

                lt = sb("l", [R, HW])
                gt = sb("g", [R, HW])
                w1 = sb("w1", [C + 1, EC, HID])
                w2 = sb("w2", [P, EC, 2, C])
                w2b = sb("w2b", [1, EC, C])
                ones = sb("ones", [1, IMG])
                top = sb("top", [R, TOPK])
                idx = sb("idx", [R, TOPK], U32)
                idf = sb("idf", [R, TOPK])
                base = sb("base", [R, 1])
                neg = sb("neg", [R, 1])
                tot = sb("tot", [R, 1])
                rec = sb("rec", [R, 1])
                p8 = sb("p8", [R, TOPK])
                rows = sb("rows", [R, TOPK, C])
                pool_t = sb("pooled", [R, C])
                pool_x = sb("pooled_t", [C + 1, R])
                hid = sb("hid", [P, 2 * EC, IMG])
                ot = sb("ot", [C, IMG, EC])
                mix = sb("mix", [R, IMG // 2, P])
                xs = [sb(f"x{i}", [P, CK]) for i in range(2)]
                ys = [sb(f"y{i}", [P, CK]) for i in range(2)]
                pt = psum("c_pt", [P, BANK], F32, st)
                ph = psum("c_ph", [P, BANK], F32, st)
                po = psum("c_po", [P, BANK], F32, st)
                pr = psum("c_pr", [P, BANK], F32, st)
                py = [psum(f"c_py{i}", [P, 2 * BANK], F32, st) for i in range(2)]

                w_loaded, l_loaded, zeroed, top_ready, neg_ready, exp_ready, e8_ready = (
                    sem(n) for n in ("wl", "ll", "zero", "top", "neg", "exp", "e8"))
                chain, idx_ready, gathered, tr_ready, px_ready, h_ready, gelu_ready = (
                    sem(n) for n in ("chain", "idx", "gath", "tr", "px", "h", "gelu"))
                o_ready, ot_ready, or_ready, mix_ready, g_ready = (sem(n) for n in ("o", "ot", "or", "mix", "gr"))
                x_loaded, stored = ([sem(f"{n}{i}", 16) for i in range(2)] for n in ("xl", "st"))
                y_prod, y_ready = ([sem(f"{n}{i}", 1) for i in range(2)] for n in ("yp", "yr"))
                nc.all_engine_barrier()
                DV = 6 + TOPK

                for tile in range(B // IMG):
                    b0 = tile * IMG
                    half = NK // 2
                    turns = []
                    for kk in range(IMG // 2):
                        turns.append((kk, half))
                    per = (IMG // 2) * half

                    with nc.Block() as block:
                        @block.sync
                        def _(sp):
                            for kk in range(IMG // 2):
                                at = (b0 // 2 + kk) * HW
                                sp.dma_start(lt[2 * EC * kk:2 * EC * (kk + 1), :], logits[:, at:at + HW]).then_inc(l_loaded, 16)
                            if tile == 0:
                                sp.dma_start(w1[:], weight1.rearrange("e d h -> d e h")).then_inc(w_loaded, 16)
                                for n in range(4):
                                    h, q = n // 2, C * (n % 2)
                                    sp.dma_start(w2[q:q + C, :, h, :],
                                                 weight2[:, h * P + q:h * P + q + C, :].rearrange("e h o -> h e o")).then_inc(w_loaded, 16)
                                sp.dma_start(w2b[:], weight2[:, HID:HID + 1, :].rearrange("e a o -> a e o")).then_inc(w_loaded, 16)
                            for kk, n in turns:
                                k = b0 // 2 + kk
                                with sp.Fori(0, n) as j:
                                    for s in range(2):
                                        at = (j * 2 + s) * CK
                                        done = j + (tile * per + kk * half + 1)
                                        sp.wait_ge(y_ready[s], done)
                                        sp.dma_start(xs[s][:], x3[:, bass.ds(at + k * HW, CK)]).then_inc(x_loaded[s], 16)
                                    for s in range(2):
                                        at = (j * 2 + s) * CK
                                        done = j + (tile * per + kk * half + 1)
                                        sp.wait_ge(y_ready[s], done + 1)
                                        sp.dma_start(out_v[k, :, bass.ds(at, CK)], ys[s][:]).then_inc(stored[s], 16)
                            for s in range(2):
                                sp.wait_ge(stored[s], 16 * (per * (tile + 1) + 1))

                        @block.gpsimd
                        def _(pool):
                            pool.wait_ge(idx_ready, tile + 1)
                            for n in range(TOPK):
                                nc.gpsimd.indirect_dma_start(out=rows[:, n, :], out_offset=None, in_=tokens,
                                                             in_offset=bass.IndirectOffsetOnAxis(ap=idx[:, n:n + 1], axis=0)).then_inc(gathered, 16)

                        @block.scalar
                        def _(act):
                            a = nc.scalar.activation
                            act.wait_ge(neg_ready, tile + 1)
                            a(gt[:], lt[:], ACT.Exp, bias=neg[:], accum_out=tot[:]).then_inc(exp_ready, 1)
                            a(p8[:], top[:], ACT.Exp, bias=neg[:]).then_inc(e8_ready, 1)
                            act.wait_ge(h_ready, tile + 1)
                            a(hid[:].rearrange("p e b -> p (e b)"), ph[:, 0:2 * EC * IMG], ACT.Gelu).then_inc(gelu_ready, 1)

                        @block.vector
                        def _(dve):
                            v = nc.vector
                            if tile == 0:
                                for n in range(IMG):
                                    v.memset(base[EC * n:EC * n + EC, :], float((n % 2 * NP + n // 2) * HW)).then_inc(zeroed, 1)
                                v.memset(pool_x[C:C + 1, :], 1.0).then_inc(zeroed, 1)
                                v.memset(ones[:], 1.0).then_inc(zeroed, 1)
                                v.memset(mix[:], 0.0).then_inc(zeroed, 1)
                                dve.wait_ge(zeroed, IMG + 3)
                            dve.wait_ge(l_loaded, 16 * (IMG // 2) * (tile + 1))
                            v.max(top[:], lt[:]).then_inc(top_ready, 1)
                            dve.wait_ge(top_ready, tile + 1)
                            v.tensor_scalar(neg[:], top[:, 0:1], -1.0, None, ALU.mult).then_inc(neg_ready, 1)
                            n = [tile * DV]

                            def link(ins):
                                n[0] += 1
                                ins.then_inc(chain, 1)
                                dve.wait_ge(chain, n[0])

                            link(v.max_index(idx[:], top[:], lt[:]))
                            link(v.tensor_copy(idf[:], idx[:]))
                            link(v.tensor_scalar(idf[:], idf[:], base[:, 0:1], float(b0 // 2 * HW), ALU.add, ALU.add))
                            v.tensor_copy(idx[:], idf[:]).then_inc(idx_ready, 1)
                            dve.wait_ge(exp_ready, tile + 1)
                            link(v.match_replace(lt[:], top[:], lt[:], TAKEN))
                            link(v.reciprocal(rec[:], tot[:]))
                            dve.wait_ge(e8_ready, tile + 1)
                            link(v.tensor_scalar(p8[:], p8[:], rec[:, 0:1], None, ALU.mult))
                            dve.wait_ge(gathered, 16 * TOPK * (tile + 1))
                            link(v.tensor_scalar(pool_t[:], rows[:, 0, :], p8[:, 0:1], None, ALU.mult))
                            for m in range(1, TOPK):
                                link(v.scalar_tensor_tensor(pool_t[:], rows[:, m, :], p8[:, m:m + 1], pool_t[:], ALU.mult, ALU.add))
                            dve.wait_ge(tr_ready, tile + 1)
                            v.tensor_copy(pool_x[0:C, :], pt[0:C, 0:R]).then_inc(px_ready, 1)
                            v.scalar_tensor_tensor(gt[:], lt[:], 0.99 * TAKEN, gt[:], ALU.is_le, ALU.mult).then_inc(g_ready, 1)
                            dve.wait_ge(o_ready, tile + 1)
                            v.tensor_copy(ot[:], po[0:C, 0:R].rearrange("o (e b) -> o b e", b=IMG)).then_inc(ot_ready, 1)
                            dve.wait_ge(or_ready, tile + 1)
                            for b in range(IMG):
                                q = slice(EC * b, EC * b + EC)
                                v.tensor_scalar(mix[q, b // 2, C * (b % 2):C * (b % 2) + C], pr[q, 0:C], rec[q, 0:1], None,
                                                ALU.mult).then_inc(mix_ready, 1)
                            for kk, turn in turns:
                                with dve.Fori(0, turn) as j:
                                    done = j + (tile * per + kk * half + 1)
                                    for s in range(2):
                                        dve.wait_ge(y_prod[s], done + 1)
                                        dve.wait_ge(x_loaded[s], 16 * done + 16)
                                        dve.wait_ge(stored[s], 16 * done)
                                        v.tensor_tensor(ys[s][:], py[s][:, 0:CK], xs[s][:], ALU.add).then_inc(y_ready[s], 1)

                        @block.tensor
                        def _(pe):
                            mm = nc.tensor.matmul
                            pe.wait_ge(chain, DV * (tile + 1))
                            nc.tensor.transpose(pt[0:C, 0:R], pool_t[:], ident[0:R, 0:R]).then_inc(tr_ready, 1)
                            pe.wait_ge(px_ready, tile + 1)
                            pe.wait_ge(w_loaded, 96)
                            by_expert = pool_x[:].rearrange("d (b e) -> d e b", e=EC)
                            for x in range(EC):
                                for h in range(2):
                                    at = (2 * x + h) * IMG
                                    last = mm(ph[:, at:at + IMG], w1[:, x, h * P:(h + 1) * P], by_expert[:, x, :], start=True, stop=True)
                            last.then_inc(h_ready, 1)
                            pe.wait_ge(gelu_ready, tile + 1)
                            for x in range(EC):
                                dst = po[0:C, x * IMG:(x + 1) * IMG]
                                for h in range(2):
                                    mm(dst, w2[:, x, h, :], hid[:, 2 * x + h, :], start=(h == 0), stop=False)
                                last = mm(dst, w2b[:, x, :], ones[:], start=False, stop=True)
                            last.then_inc(o_ready, 1)
                            pe.wait_ge(ot_ready, tile + 1)
                            nc.tensor.transpose(pr[0:R, 0:C], ot[:].rearrange("o b e -> o (b e)"), ident[0:C, 0:C]).then_inc(or_ready, 1)
                            pe.wait_ge(mix_ready, IMG * (tile + 1))
                            pe.wait_ge(g_ready, tile + 1)
                            for kk, turn in turns:
                                with pe.Fori(0, turn) as j:
                                    done = j + (tile * per + kk * half + 1)
                                    for s in range(2):
                                        pe.wait_ge(y_ready[s], done)
                                        for a, b in banks(CK):
                                            last = mm(py[s][:, a:b], mix[:, kk, :], gt[:, bass.ds((j * 2 + s) * CK + a, b - a)],
                                                      start=True, stop=True)
                                        last.then_inc(y_prod[s], 1)

        end_phase()
        phase_a()
        own.close()
        end_phase()
        phase_b()
        end_phase()
        phase_c()


_INS = ['x', 'L0_conv_wq', 'L0_conv_wk', 'L0_conv_wv', 'L0_conv_wo', 'L0_conv_bn_gamma', 'L0_conv_bn_beta',
        'L0_conv_bn_mean', 'L0_conv_bn_var', 'L0_ffn_router_w', 'L0_ffn_router_b', 'L0_ffn_expert_w',
        'L0_ffn_expert_b', 'L1_conv_pos', 'L1_conv_W_in', 'L1_conv_conv_w', 'L1_conv_conv_b', 'L1_conv_W_xproj',
        'L1_conv_W_dt', 'L1_conv_b_dt', 'L1_conv_A_log', 'L1_conv_Dp', 'L1_conv_W_out', 'L1_ffn_gate_w',
        'L1_ffn_gate_b', 'L1_ffn_weight1', 'L1_ffn_weight2']


def kernel(**inputs):
    import numpy as _np
    import concourse.bacc as _bacc
    from concourse.bass_utils import run_bass_kernel_spmd as _run

    arrays = {f"in_{name}": _np.ascontiguousarray(inputs[name]) for name in _INS}
    nc = _bacc.Bacc("TRN2", target_bir_lowering=False, num_devices=1)
    args = [nc.dram_tensor(f"in_{name}", arrays[f"in_{name}"].shape, F32, kind="ExternalInput").ap() for name in _INS]
    b, c, h, w = arrays["in_x"].shape
    out = nc.dram_tensor("out", [b, c, h, w], F32, kind="ExternalOutput").ap()
    x2 = nc.dram_tensor("x2", [2 * c, b // 2 * h * w], F32, kind="Internal").ap()
    x3 = nc.dram_tensor("x3", [2 * c, b // 2 * h * w], F32, kind="Internal").ap()
    logits = nc.dram_tensor("logits", [2 * EC, b // 2 * h * w], F32, kind="Internal").ap()
    tokens = nc.dram_tensor("tokens", [b * h * w, C], F32, kind="Internal").ap()
    program(nc, *args, out, x2, x3, logits, tokens)
    r = _run(nc, [arrays], core_ids=[0])
    return r.results[0]["out"]
```
